# Optimizing a Trainium2 kernel written in Bass

```python
import numpy as np
import jax
import jax.numpy as jnp

def _softmax(x, axis=-1):
    return jax.nn.softmax(x, axis=axis)

def _gelu(x):
    return jax.nn.gelu(x, approximate=True)

def _silu(x):
    return jax.nn.silu(x)

def _sigmoid(x):
    return jax.nn.sigmoid(x)

def _layernorm(x, axis=-1, eps=1e-05):
    m = jnp.mean(x, axis=axis, keepdims=True)
    v = jnp.var(x, axis=axis, keepdims=True)
    return (x - m) / jnp.sqrt(v + eps)

def _scatter_add(tgt, idx, src, axis=0):
    return tgt.at[idx].add(src)

def _segment_sum(src, seg, n):
    return jax.ops.segment_sum(src, seg, n)
kernel_name = 'mk_early_fusion_d2_tok_img1024_r4_3a2726'

def setup_inputs(seed: int=0):
    np.random.seed(seed)
    _w = jnp.asarray

    def _rec_inputs():
        import jax
        import jax.numpy as jnp
        _rk = jax.random.key(seed)
        x = -0.00016672 + 0.999947 * jax.random.normal(jax.random.fold_in(_rk, 1), (16, 3, 128, 128), jnp.float32)
        txt = -0.000196989 + 0.577976 * jax.random.normal(jax.random.fold_in(_rk, 2), (16, 77, 256), jnp.float32)
        return (x, txt)
    x, txt = _rec_inputs()

    def _L0_tok_setup():
        import jax, jax.numpy as jnp
        import numpy as np
        PATCH = 16
        D_MODEL = 256

        def patchify(imgs, p):
            n, c, H, W = imgs.shape
            h, w = (H // p, W // p)
            x = imgs.reshape(n, c, h, p, w, p)
            x = jnp.einsum('nchpwq->nhwpqc', x)
            return x.reshape(n, h * w, p * p * c)
        key = jax.random.key(seed)
        k1, k2, k3 = jax.random.split(key, 3)
        val = jax.random.normal(k1, (64, 3, 96, 96), dtype=jnp.float32)
        in_dim = PATCH * PATCH * 3
        bound = 1.0 / np.sqrt(in_dim)
        W = jax.random.uniform(k2, (D_MODEL, in_dim), dtype=jnp.float32, minval=-bound, maxval=bound)
        b = jax.random.uniform(k3, (D_MODEL,), dtype=jnp.float32, minval=-bound, maxval=bound)
        return {'val': val, 'W': W, 'b': b}
    _L0_tok_all = _L0_tok_setup()
    _L0_tok_in = {k: v for k, v in _L0_tok_all.items() if k in ('W', 'b')}
    del _L0_tok_all

    def _L0_attn_setup():
        import jax, jax.numpy as jnp
        import numpy as np
        import math
        D_MODEL = 256
        N_HEADS = 16
        HEAD_DIM = D_MODEL // N_HEADS

        def rotary_embedding(dim, seq_len):
            inv_freq = 1.0 / 10000.0 ** (jnp.arange(0, dim, 2, dtype=jnp.float32) / dim)
            t = jnp.arange(seq_len, dtype=jnp.float32)
            freqs = t[:, None] * inv_freq[None, :]
            return jnp.concatenate((freqs, freqs), axis=-1)

        def apply_rope(x, rope):
            x1 = x[..., ::2]
            x2 = x[..., 1::2]
            ang = rope[..., ::2]
            c, s = (jnp.cos(ang), jnp.sin(ang))
            o1 = x1 * c - x2 * s
            o2 = x1 * s + x2 * c
            return jnp.stack((o1, o2), axis=-1).reshape(x.shape)
        key = jax.random.key(seed)
        ks = jax.random.split(key, 9)
        d = D_MODEL
        sc = 1.0 / math.sqrt(d)
        return {'x': jax.random.normal(ks[0], (2, 512, d), dtype=jnp.float32), 'Wq': jax.random.normal(ks[1], (d, d), dtype=jnp.float32) * sc, 'bq': jax.random.normal(ks[2], (d,), dtype=jnp.float32) * 0.02, 'Wk': jax.random.normal(ks[3], (d, d), dtype=jnp.float32) * sc, 'bk': jax.random.normal(ks[4], (d,), dtype=jnp.float32) * 0.02, 'Wv': jax.random.normal(ks[5], (d, d), dtype=jnp.float32) * sc, 'bv': jax.random.normal(ks[6], (d,), dtype=jnp.float32) * 0.02, 'Wo': jax.random.normal(ks[7], (d, d), dtype=jnp.float32) * sc, 'bo': jax.random.normal(ks[8], (d,), dtype=jnp.float32) * 0.02}
    _L0_attn_all = _L0_attn_setup()
    _L0_attn_in = {k: v for k, v in _L0_attn_all.items() if k in ('Wq', 'bq', 'Wk', 'bk', 'Wv', 'bv', 'Wo', 'bo')}
    del _L0_attn_all

    def _L0_ffn_setup():
        import jax, jax.numpy as jnp
        import numpy as np
        HIDDEN = 256
        INTER = 128
        N_EXPERTS = 16
        N_GROUP = 4
        TOPK_GROUP = 2
        TOP_K = 4
        SCALING = 2.5

        def _gate(x_flat, gate_w, e_bias):
            logits = x_flat @ gate_w.T
            scores = jax.nn.sigmoid(logits)
            scores_for_choice = scores + e_bias[None, :]
            T = x_flat.shape[0]
            per_group = N_EXPERTS // N_GROUP
            grouped = scores_for_choice.reshape(T, N_GROUP, per_group)
            top2, _ = jax.lax.top_k(grouped, 2)
            group_scores = top2.sum(-1)
            _, group_idx = jax.lax.top_k(group_scores, TOPK_GROUP)
            group_mask = jax.nn.one_hot(group_idx, N_GROUP, dtype=jnp.float32).sum(1) > 0
            score_mask = jnp.repeat(group_mask, per_group, axis=-1)
            tmp_scores = jnp.where(score_mask, scores_for_choice, 0.0)
            _, topk_idx = jax.lax.top_k(tmp_scores, TOP_K)
            topk_weight = jnp.take_along_axis(scores, topk_idx, axis=1)
            topk_weight = topk_weight / (topk_weight.sum(-1, keepdims=True) + 1e-20)
            topk_weight = topk_weight * SCALING
            return (topk_idx, topk_weight)
        key = jax.random.key(seed)
        ks = jax.random.split(key, 8)
        B, S = (2, 512)
        hidden_states = jax.random.normal(ks[0], (B, S, HIDDEN), dtype=jnp.float32)
        gate_w = jax.random.normal(ks[1], (N_EXPERTS, HIDDEN), dtype=jnp.float32) * 0.02
        e_bias = jnp.zeros((N_EXPERTS,), dtype=jnp.float32)
        gate_proj = jax.random.normal(ks[2], (N_EXPERTS, INTER, HIDDEN), dtype=jnp.float32) * 0.02
        up_proj = jax.random.normal(ks[3], (N_EXPERTS, INTER, HIDDEN), dtype=jnp.float32) * 0.02
        down_proj = jax.random.normal(ks[4], (N_EXPERTS, HIDDEN, INTER), dtype=jnp.float32) * 0.02
        shared_gate_w = jax.random.normal(ks[5], (INTER, HIDDEN), dtype=jnp.float32) * 0.02
        shared_up_w = jax.random.normal(ks[6], (INTER, HIDDEN), dtype=jnp.float32) * 0.02
        shared_down_w = jax.random.normal(ks[7], (HIDDEN, INTER), dtype=jnp.float32) * 0.02
        return {'hidden_states': hidden_states, 'gate_w': gate_w, 'e_bias': e_bias, 'gate_proj': gate_proj, 'up_proj': up_proj, 'down_proj': down_proj, 'shared_gate_w': shared_gate_w, 'shared_up_w': shared_up_w, 'shared_down_w': shared_down_w}
    _L0_ffn_all = _L0_ffn_setup()
    _L0_ffn_in = {k: v for k, v in _L0_ffn_all.items() if k in ('gate_w', 'e_bias', 'gate_proj', 'up_proj', 'down_proj', 'shared_gate_w', 'shared_up_w', 'shared_down_w')}
    del _L0_ffn_all

    def _L1_attn_setup():
        import jax, jax.numpy as jnp
        import numpy as np
        import math
        B, S, D, H = (4, 512, 256, 16)
        DK = D // H
        key = jax.random.key(seed)
        ks = jax.random.split(key, 5)
        scale = 1.0 / math.sqrt(D)
        return {'x': jax.random.normal(ks[0], (B, S, D), dtype=jnp.float32), 'Wv': jax.random.normal(ks[1], (D, D), dtype=jnp.float32) * scale, 'bv': jax.random.normal(ks[2], (D,), dtype=jnp.float32) * scale, 'Wo': jax.random.normal(ks[3], (D, D), dtype=jnp.float32) * scale, 'bo': jax.random.normal(ks[4], (D,), dtype=jnp.float32) * scale}
    _L1_attn_all = _L1_attn_setup()
    _L1_attn_in = {k: v for k, v in _L1_attn_all.items() if k in ('Wv', 'bv', 'Wo', 'bo')}
    del _L1_attn_all

    def _L1_ffn_setup():
        import jax, jax.numpy as jnp
        import numpy as np
        HIDDEN = 256
        INNER = 1024

        def _weight_quant(w):
            scale = 1.0 / jnp.clip(jnp.mean(jnp.abs(w)), 1e-05)
            wq = jnp.clip(jnp.round(w * scale), -1.0, 1.0) / scale
            return w + jax.lax.stop_gradient(wq - w)

        def _act_quant(x):
            scale = 127.0 / jnp.clip(jnp.max(jnp.abs(x), axis=-1, keepdims=True), 1e-05)
            xq = jnp.clip(jnp.round(x * scale), -128.0, 127.0) / scale
            return x + jax.lax.stop_gradient(xq - x)

        def _bitlinear(x, w):
            return jnp.einsum('bsi,oi->bso', _act_quant(x), _weight_quant(w))
        key = jax.random.key(seed)
        k0, k1, k2, k3 = jax.random.split(key, 4)
        x = jax.random.normal(k0, (4, 512, HIDDEN), dtype=jnp.float32)
        w_gate = jax.random.normal(k1, (INNER, HIDDEN), dtype=jnp.float32) / np.sqrt(HIDDEN)
        w_up = jax.random.normal(k2, (INNER, HIDDEN), dtype=jnp.float32) / np.sqrt(HIDDEN)
        w_down = jax.random.normal(k3, (HIDDEN, INNER), dtype=jnp.float32) / np.sqrt(INNER)
        return {'x': x, 'w_gate': w_gate, 'w_up': w_up, 'w_down': w_down}
    _L1_ffn_all = _L1_ffn_setup()
    _L1_ffn_in = {k: v for k, v in _L1_ffn_all.items() if k in ('w_gate', 'w_up', 'w_down')}
    del _L1_ffn_all
    return {'x': x, 'txt': txt, 'L0_tok_W': _L0_tok_in['W'], 'L0_tok_b': _L0_tok_in['b'], 'L0_attn_Wq': _L0_attn_in['Wq'], 'L0_attn_bq': _L0_attn_in['bq'], 'L0_attn_Wk': _L0_attn_in['Wk'], 'L0_attn_bk': _L0_attn_in['bk'], 'L0_attn_Wv': _L0_attn_in['Wv'], 'L0_attn_bv': _L0_attn_in['bv'], 'L0_attn_Wo': _L0_attn_in['Wo'], 'L0_attn_bo': _L0_attn_in['bo'], 'L0_ffn_gate_w': _L0_ffn_in['gate_w'], 'L0_ffn_e_bias': _L0_ffn_in['e_bias'], 'L0_ffn_gate_proj': _L0_ffn_in['gate_proj'], 'L0_ffn_up_proj': _L0_ffn_in['up_proj'], 'L0_ffn_down_proj': _L0_ffn_in['down_proj'], 'L0_ffn_shared_gate_w': _L0_ffn_in['shared_gate_w'], 'L0_ffn_shared_up_w': _L0_ffn_in['shared_up_w'], 'L0_ffn_shared_down_w': _L0_ffn_in['shared_down_w'], 'L1_attn_Wv': _L1_attn_in['Wv'], 'L1_attn_bv': _L1_attn_in['bv'], 'L1_attn_Wo': _L1_attn_in['Wo'], 'L1_attn_bo': _L1_attn_in['bo'], 'L1_ffn_w_gate': _L1_ffn_in['w_gate'], 'L1_ffn_w_up': _L1_ffn_in['w_up'], 'L1_ffn_w_down': _L1_ffn_in['w_down']}

def reference(x, txt, L0_tok_W, L0_tok_b, L0_attn_Wq, L0_attn_bq, L0_attn_Wk, L0_attn_bk, L0_attn_Wv, L0_attn_bv, L0_attn_Wo, L0_attn_bo, L0_ffn_gate_w, L0_ffn_e_bias, L0_ffn_gate_proj, L0_ffn_up_proj, L0_ffn_down_proj, L0_ffn_shared_gate_w, L0_ffn_shared_up_w, L0_ffn_shared_down_w, L1_attn_Wv, L1_attn_bv, L1_attn_Wo, L1_attn_bo, L1_ffn_w_gate, L1_ffn_w_up, L1_ffn_w_down):
    import jax
    import jax.numpy as jnp

    def _L0_tok_ref(val, W, b):
        import jax, jax.numpy as jnp
        import numpy as np
        PATCH = 16
        D_MODEL = 256

        def patchify(imgs, p):
            n, c, H, W = imgs.shape
            h, w = (H // p, W // p)
            x = imgs.reshape(n, c, h, p, w, p)
            x = jnp.einsum('nchpwq->nhwpqc', x)
            return x.reshape(n, h * w, p * p * c)
        patches = patchify(val, PATCH)
        return jnp.einsum('nld,md->nlm', patches, W) + b

    def _L0_attn_ref(x, Wq, bq, Wk, bk, Wv, bv, Wo, bo):
        import jax, jax.numpy as jnp
        import numpy as np
        import math
        D_MODEL = 256
        N_HEADS = 16
        HEAD_DIM = D_MODEL // N_HEADS

        def rotary_embedding(dim, seq_len):
            inv_freq = 1.0 / 10000.0 ** (jnp.arange(0, dim, 2, dtype=jnp.float32) / dim)
            t = jnp.arange(seq_len, dtype=jnp.float32)
            freqs = t[:, None] * inv_freq[None, :]
            return jnp.concatenate((freqs, freqs), axis=-1)

        def apply_rope(x, rope):
            x1 = x[..., ::2]
            x2 = x[..., 1::2]
            ang = rope[..., ::2]
            c, s = (jnp.cos(ang), jnp.sin(ang))
            o1 = x1 * c - x2 * s
            o2 = x1 * s + x2 * c
            return jnp.stack((o1, o2), axis=-1).reshape(x.shape)
        B, S, d = x.shape
        H, Dh = (N_HEADS, HEAD_DIM)
        q = (x @ Wq + bq).reshape(B, S, H, Dh).transpose(0, 2, 1, 3)
        k = (x @ Wk + bk).reshape(B, S, H, Dh).transpose(0, 2, 1, 3)
        v = (x @ Wv + bv).reshape(B, S, H, Dh).transpose(0, 2, 1, 3)
        rope = rotary_embedding(Dh, S)
        q = apply_rope(q, rope)
        k = apply_rope(k, rope)
        scores = jnp.einsum('bhqd,bhkd->bhqk', q, k) / math.sqrt(Dh)
        attn = jax.nn.softmax(scores, axis=-1)
        out = jnp.einsum('bhqk,bhkd->bhqd', attn, v)
        out = out.transpose(0, 2, 1, 3).reshape(B, S, d)
        return out @ Wo + bo

    def _L0_ffn_ref(hidden_states, gate_w, e_bias, gate_proj, up_proj, down_proj, shared_gate_w, shared_up_w, shared_down_w):
        import jax, jax.numpy as jnp
        import numpy as np
        HIDDEN = 256
        INTER = 128
        N_EXPERTS = 16
        N_GROUP = 4
        TOPK_GROUP = 2
        TOP_K = 4
        SCALING = 2.5

        def _gate(x_flat, gate_w, e_bias):
            logits = x_flat @ gate_w.T
            scores = jax.nn.sigmoid(logits)
            scores_for_choice = scores + e_bias[None, :]
            T = x_flat.shape[0]
            per_group = N_EXPERTS // N_GROUP
            grouped = scores_for_choice.reshape(T, N_GROUP, per_group)
            top2, _ = jax.lax.top_k(grouped, 2)
            group_scores = top2.sum(-1)
            _, group_idx = jax.lax.top_k(group_scores, TOPK_GROUP)
            group_mask = jax.nn.one_hot(group_idx, N_GROUP, dtype=jnp.float32).sum(1) > 0
            score_mask = jnp.repeat(group_mask, per_group, axis=-1)
            tmp_scores = jnp.where(score_mask, scores_for_choice, 0.0)
            _, topk_idx = jax.lax.top_k(tmp_scores, TOP_K)
            topk_weight = jnp.take_along_axis(scores, topk_idx, axis=1)
            topk_weight = topk_weight / (topk_weight.sum(-1, keepdims=True) + 1e-20)
            topk_weight = topk_weight * SCALING
            return (topk_idx, topk_weight)
        B, S, H = hidden_states.shape
        x = hidden_states.reshape(-1, H)
        T = x.shape[0]
        topk_idx, topk_weight = _gate(x, gate_w, e_bias)
        g = jnp.einsum('th,eih->eti', x, gate_proj)
        u = jnp.einsum('th,eih->eti', x, up_proj)
        inter = jax.nn.silu(g) * u
        expert_out = jnp.einsum('eti,ehi->eth', inter, down_proj)
        sel = expert_out[topk_idx, jnp.arange(T)[:, None]]
        y = jnp.einsum('tkh,tk->th', sel, topk_weight)
        y = y.reshape(B, S, H)
        sg = hidden_states @ shared_gate_w.T
        su = hidden_states @ shared_up_w.T
        shared_out = jax.nn.silu(sg) * su @ shared_down_w.T
        return y + shared_out

    def _L1_attn_ref(x, Wv, bv, Wo, bo):
        import jax, jax.numpy as jnp
        import numpy as np
        import math
        B, S, D, H = (4, 512, 256, 16)
        DK = D // H
        b, s, d = x.shape
        h, dk = (H, DK)
        p = jnp.einsum('bsd,ed->bse', x, Wv) + bv
        p = p.reshape(b, s, h, dk).transpose(0, 2, 1, 3)
        q = k = v = p
        scores = jnp.einsum('bhqd,bhkd->bhqk', q, k) / math.sqrt(dk)
        attn = jax.nn.softmax(scores, axis=-1)
        out = jnp.einsum('bhqk,bhkd->bhqd', attn, v)
        out = out.reshape(b, s, h * dk)
        return jnp.einsum('bsd,ed->bse', out, Wo) + bo

    def _L1_ffn_ref(x, w_gate, w_up, w_down):
        import jax, jax.numpy as jnp
        import numpy as np
        HIDDEN = 256
        INNER = 1024

        def _weight_quant(w):
            scale = 1.0 / jnp.clip(jnp.mean(jnp.abs(w)), 1e-05)
            wq = jnp.clip(jnp.round(w * scale), -1.0, 1.0) / scale
            return w + jax.lax.stop_gradient(wq - w)

        def _act_quant(x):
            scale = 127.0 / jnp.clip(jnp.max(jnp.abs(x), axis=-1, keepdims=True), 1e-05)
            xq = jnp.clip(jnp.round(x * scale), -128.0, 127.0) / scale
            return x + jax.lax.stop_gradient(xq - x)

        def _bitlinear(x, w):
            return jnp.einsum('bsi,oi->bso', _act_quant(x), _weight_quant(w))
        gate = jax.nn.silu(_bitlinear(x, w_gate))
        up = _bitlinear(x, w_up)
        return _bitlinear(gate * up, w_down)
    h = _L0_tok_ref(x, L0_tok_W, L0_tok_b)
    h = jnp.concatenate([h, txt], axis=1)
    h = h + _L0_attn_ref(_layernorm(h, axis=-1), L0_attn_Wq, L0_attn_bq, L0_attn_Wk, L0_attn_bk, L0_attn_Wv, L0_attn_bv, L0_attn_Wo, L0_attn_bo)
    h = h + _L0_ffn_ref(_layernorm(h, axis=-1), L0_ffn_gate_w, L0_ffn_e_bias, L0_ffn_gate_proj, L0_ffn_up_proj, L0_ffn_down_proj, L0_ffn_shared_gate_w, L0_ffn_shared_up_w, L0_ffn_shared_down_w)
    h = h + _L1_attn_ref(_layernorm(h, axis=-1), L1_attn_Wv, L1_attn_bv, L1_attn_Wo, L1_attn_bo)
    h = h + _L1_ffn_ref(_layernorm(h, axis=-1), L1_ffn_w_gate, L1_ffn_w_up, L1_ffn_w_down)
    return h

_drawn_inputs = setup_inputs


def setup_inputs(seed=0):
    import zlib

    import numpy as np

    out = dict(_drawn_inputs(seed))
    spreads = {'L0_ffn_e_bias': (0.0, 0.356)}
    factors = {'L0_attn_bq': 8.0, 'L0_attn_bk': 8.0, 'L0_ffn_gate_w': 11.287}
    for name, (base, spread) in spreads.items():
        noise = np.random.default_rng([zlib.crc32(name.encode()), seed]).standard_normal(out[name].shape)
        drawn = base * np.exp(spread * noise) if base else spread * noise
        out[name] = jnp.asarray(drawn.astype(out[name].dtype))
    for name, factor in factors.items():
        out[name] = (out[name] * factor).astype(out[name].dtype)
    return out
```

```python
from contextlib import ExitStack

import numpy as np

import concourse.bass as bass
from concourse import mybir

ALU = mybir.AluOpType
ACT = mybir.ActivationFunctionType
AX = mybir.AxisListType
F32 = mybir.dt.float32
BF16 = mybir.dt.bfloat16
F16 = mybir.dt.float16
U32 = mybir.dt.uint32

P = 128
D = 256
KT = D // P
IMAGES = 16
PATCHES = 64
TEXT = 77
SEQ = PATCHES + TEXT
ROWS = IMAGES * SEQ
TILES = -(-ROWS // P)
PADDED = TILES * P
EMB_K = 768 // P
EMB_TILES = IMAGES * PATCHES // P
PAIR = 2
PASSES = TILES // PAIR
HEADS = 16
DH = D // HEADS
HH = HEADS // KT
REM = SEQ - P
HR = HH * REM
VC = 3 * DH + 1
SLOTS = HEADS + KT
SGROUPS = SLOTS // 3
TGROUPS = 6
EXPERTS = 16
BRANCHES = EXPERTS + 1
INTER = 128
GROUPS = 4
TOPK = 4
CHUNK = 3 * P
CHUNKS = PADDED // CHUNK
INNER = 1024
IB = INNER // P
BANK = 512
ROUND = 12582912.0
LN_EPS = 1e-5
LOWEST = -3.0e38


def for_each(eng, count, body):
    body(0)
    with eng.Fori(1, count) as i:
        body(i)


def is_first(i):
    return isinstance(i, int) and i == 0


class Chain:

    def __init__(self, eng, semaphore):
        self.eng, self.semaphore, self.base, self.n, self.per_pass = eng, semaphore, 0, 0, 0

    def at(self, i):
        if not is_first(i):
            self.per_pass = self.per_pass or self.n
            self.base = i * self.per_pass
        self.n = 0

    def link(self, instruction):
        instruction.then_inc(self.semaphore, 1)
        self.n += 1
        self.eng.wait_ge(self.semaphore, self.base + self.n)


def fusion_kernel(nc, patches_t, txt, w_emb_t, b_emb, w_qkv, b_qkv, w_o0, b_o0, w_gate_t, e_bias,
                  w_gu_t, w_down_t, w_v1_t, b_v1, w_o1_t, b_o1, ffn_up_t, ffn_down_t,
                  rope_cos, rope_sin, head_mask, rem_mask, ident_in, iota_in, out):
    ctx = ExitStack()
    with ctx:
        def sb(name, shape, dt=F32):
            return ctx.enter_context(nc.sbuf_tensor(name, shape, dt))

        def sem(name):
            return nc.alloc_semaphore(name=name)

        def dram(name, shape, dt=F32):
            return nc.dram_tensor(name, shape, dt, kind="Internal").ap()

        h0_dram = dram("h0_dram", [PADDED, D])
        v_dram = dram("v_dram", [PADDED, HEADS * VC], BF16)
        o_dram = dram("o_dram", [PADDED, D])

        h = sb("h", [P, TILES, D])
        qT = sb("qT", [P, KT, PADDED])
        kT = sb("kT", [P, KT, PADDED])
        stats = sb("stats", [P, TILES, 6])
        mean_var = sb("mean_var", [P, TILES, 2])
        rstd = sb("rstd", [P, TILES])
        shift = sb("shift", [P, TILES])
        expo = sb("expo", [P, TILES])
        ident = sb("ident", [P, P])
        ident_bf = sb("ident_bf", [P, P], BF16)
        iota = sb("iota", [P, EXPERTS])
        ones = sb("ones", [P, P])

        wqkv_sb = sb("wqkv_sb", [P, KT, 3 * D])
        wo_sb = [sb(f"wo{n}_sb", [P, KT, D]) for n in range(2)]
        wv1_sb = sb("wv1_sb", [P, KT, D])
        wgate_sb = sb("wgate_sb", [P, KT, EXPERTS])
        bqkv_sb = sb("bqkv_sb", [P, 3 * D])
        bo_sb = [sb(f"bo{n}_sb", [P, D]) for n in range(2)]
        bv1_sb = sb("bv1_sb", [P, D])
        bemb_sb = sb("bemb_sb", [P, D])
        ebias_sb = sb("ebias_sb", [P, EXPERTS])
        ffn_up_q = sb("ffn_up_q", [P, KT, 2 * INNER], BF16)
        ffn_down_q = sb("ffn_down_q", [P, IB, D], BF16)
        w_scale = sb("w_scale", [P, 3])
        cos_sb = sb("cos_sb", [P, TILES, 2 * DH])
        sin_sb = sb("sin_sb", [P, TILES, 2 * DH])
        mask_sb = sb("mask_sb", [P, HH])
        rmask_sb = sb("rmask_sb", [HR, HH])
        rmask_bf = sb("rmask_bf", [HR, HH], BF16)

        xn = sb("xn", [P, PAIR, D])
        xT = sb("xT", [P, PAIR, D])
        work = sb("work", [P, PAIR, 2 * INNER])

        moe_up = BRANCHES * 2 * INTER
        region = sb("region", [P, 18600])
        used = [0]

        def piece(n, dt=F32):
            words = n if dt == F32 else n // 2
            a = used[0]
            used[0] += words
            v = region[:, a:a + words]
            return v if dt == F32 else v.bitcast(dt)

        q_masked = piece(PAIR * KT * HH * P).rearrange("p (s t h q) -> p s t h q", s=PAIR, t=KT, h=HH)
        q_rem = piece(PAIR * KT * P).rearrange("p (s t q) -> p s t q", s=PAIR, t=KT)
        prob = piece(PAIR * SLOTS * SEQ).rearrange("p (s n k) -> p s n k", s=PAIR, n=SLOTS)
        pT = piece(2 * HEADS * P, F16).rearrange("p (a h q) -> p a h q", a=2, h=HEADS)
        pT_rem = piece(2 * 2 * KT * P, F16).rearrange("p (a n q) -> p a n q", a=2, n=2 * KT)
        pT_corner = piece(KT * P, F16).rearrange("p (t q) -> p t q", t=KT)
        v_main = piece(PAIR * HEADS * VC, BF16).rearrange("p (s c) -> p s c", s=PAIR)
        v_rem = piece(PAIR * HEADS * VC, BF16).rearrange("p (s c) -> p s c", s=PAIR)
        v_rep = piece(PAIR * HEADS * VC, BF16).rearrange("p (s c) -> p s c", s=PAIR)
        v_diag = piece(PAIR * HEADS * VC, BF16).rearrange("p (s c) -> p s c", s=PAIR)
        prob_last = piece(PAIR * HEADS * REM).rearrange("p (s c) -> p s c", s=PAIR)
        neg_max = piece(PAIR * SLOTS).rearrange("p (s n) -> p s n", s=PAIR)
        o_sum = piece(D)
        o_den = piece(HEADS)
        o_out = piece(PAIR * D).rearrange("p (s c) -> p s c", s=PAIR)
        r_raw = piece(HEADS * VC)
        r_sum = piece(D)
        r_den = piece(HEADS)
        r_out = piece(PAIR * D).rearrange("p (s c) -> p s c", s=PAIR)
        assert used[0] <= 18600 and KT * moe_up + BRANCHES * D <= 18600
        gu_sb = region[:, 0:KT * moe_up].rearrange("p (t e c) -> p t e c", t=KT, e=BRANCHES)
        down_sb = region[:, KT * moe_up:KT * moe_up + BRANCHES * D].rearrange("p (e c) -> p e c", e=BRANCHES)
        ffn_raw = region[:, 0:KT * 2 * INNER + IB * D]

        bank = [ctx.enter_context(nc.psum_tensor(f"bank{n}", [P, BANK], F32)) for n in range(8)]

        def col(t, n=1):
            return lambda x: x[:, bass.ds(t, 1), :].rearrange("p a c -> p (a c)")

        def tile_cols(x, t):
            return x[:, :, bass.ds(P * t, P)]

        def embed_phase():
            s_const = sem("e_const")
            s_late = sem("e_late")
            s_raw = sem("e_raw")
            s_patch = [sem(f"e_patch{u}") for u in range(PAIR)]
            s_mm = sem("e_mm")
            s_add = sem("e_add")
            s_st = [sem(f"e_st{u}") for u in range(PAIR)]
            s_zero = sem("e_zero")
            s_pad = sem("e_pad")
            s_ones = sem("e_ones")
            s_chain = sem("e_chain")
            s_sum = sem("e_sum")
            s_tot = sem("e_tot")
            s_h = sem("e_h")
            s_id = sem("e_id")
            w_emb = work[:, 0, 0:EMB_K * D].rearrange("p (k c) -> p k c", k=EMB_K)
            patch = [xT_patch[:, u] for u in range(PAIR)]
            abs_sum = stats[:, 0, 0:3]
            zero = v_zero
            n_const = 7
            with nc.Block() as block:
                @block.sync
                def _(sp):
                    sp.dma_start(w_emb, w_emb_t.rearrange("(k p) c -> p k c", p=P)).then_inc(s_const, 16)
                    sp.dma_start(bemb_sb[:, :], b_emb.rearrange("(a c) -> a c", a=1).broadcast_to([P, D])).then_inc(s_const, 16)
                    sp.dma_start(ident[:, :], ident_in).then_inc(s_const, 16)
                    sp.dma_start(iota[:, :], iota_in).then_inc(s_const, 16)
                    sp.dma_start(mask_sb[:, :], head_mask).then_inc(s_const, 16)
                    sp.dma_start(rmask_sb[:, :], rem_mask).then_inc(s_const, 16)
                    sp.dma_start(ebias_sb[:, :], e_bias.rearrange("(a c) -> a c", a=1).broadcast_to([P, EXPERTS])).then_inc(s_const, 16)

                    def body(i):
                        for u in range(PAIR):
                            t = PAIR * i + u
                            if not is_first(i):
                                sp.wait_ge(s_mm, t - 1)
                            sp.dma_start(patch[u], patches_t.rearrange("(k p) r -> p k r", p=P)[:, :, bass.ds(P * t, P)]).then_inc(s_patch[u], 16)
                        for u in range(PAIR):
                            t = PAIR * i + u
                            sp.wait_ge(s_add, t + 1)
                            for j in range(2):
                                dst = h0_dram[bass.ds(SEQ * (2 * t + j), PATCHES), :]
                                sp.dma_start(dst, xn[PATCHES * j:PATCHES * (j + 1), u, :]).then_inc(s_st[u], 16)
                    for_each(sp, EMB_TILES // PAIR, body)
                    for u in range(PAIR):
                        sp.wait_ge(s_st[u], 16 * 2 * EMB_TILES // PAIR)
                    sp.wait_ge(s_pad, 16 * 3)
                    sp.dma_start(h[:, :, :], h0_dram.rearrange("(t p) c -> p t c", p=P)).then_inc(s_h, 16)
                    sp.wait_ge(s_h, 16)

                @block.gpsimd
                def _(pool):
                    pool.memset(zero, 0.0).then_inc(s_zero, 1)
                    pool.memset(ones[:, :], 1.0).then_inc(s_ones, 1)
                    pool.memset(expo[:, :], -0.5).then_inc(s_ones, 1)
                    pool.memset(v_out[:, :, :], 1.0).then_inc(s_ones, 1)
                    pool.wait_ge(s_zero, 1)
                    pad = PADDED - ROWS
                    pool.dma_start(h0_dram[ROWS:PADDED, :], zero[0:pad, :]).then_inc(s_pad, 16)
                    pool.dma_start(o_dram[ROWS:PADDED, :], zero[0:pad, :]).then_inc(s_pad, 16)
                    rows = h0_dram[0:ROWS, :].rearrange("(b s) c -> b s c", s=SEQ)
                    pool.dma_start(rows[:, PATCHES:SEQ, :], txt).then_inc(s_pad, 16)
                    pool.wait_ge(s_pad, 16 * 3)
                    pool.wait_ge(s_ones, 3)

                @block.scalar
                def _(act):
                    def up(dst, src):
                        act.dma_start(dst, src).then_inc(s_late, 16)
                    raw_up = ffn_raw[:, 0:KT * 2 * INNER].rearrange("p (k c) -> p k c", k=KT)
                    raw_down = ffn_raw[:, KT * 2 * INNER:].rearrange("p (k c) -> p k c", k=IB)
                    act.dma_start(raw_up, ffn_up_t.rearrange("(k p) c -> p k c", p=P)).then_inc(s_raw, 16)
                    act.dma_start(raw_down, ffn_down_t.rearrange("(k p) c -> p k c", p=P)).then_inc(s_raw, 16)
                    up(wqkv_sb[:, :, :], w_qkv.rearrange("(k p) c -> p k c", p=P))
                    up(bqkv_sb[:, :], b_qkv.rearrange("(a c) -> a c", a=1).broadcast_to([P, 3 * D]))
                    up(cos_sb[:, :, :], rope_cos.rearrange("(t p) c -> p t c", p=P))
                    up(sin_sb[:, :, :], rope_sin.rearrange("(t p) c -> p t c", p=P))
                    for n, (w, b) in enumerate(((w_o0, b_o0), (w_o1_t, b_o1))):
                        up(wo_sb[n][:, :, :], w.rearrange("(k p) c -> p k c", p=P))
                        up(bo_sb[n][:, :], b.rearrange("(a c) -> a c", a=1).broadcast_to([P, D]))
                    up(wv1_sb[:, :, :], w_v1_t.rearrange("(k p) c -> p k c", p=P))
                    up(bv1_sb[:, :], b_v1.rearrange("(a c) -> a c", a=1).broadcast_to([P, D]))
                    up(wgate_sb[:, :, :], w_gate_t.rearrange("(k p) c -> p k c", p=P))
                    act.wait_ge(s_const, 16 * n_const)
                    act.activation(ident_bf[:, :], ident[:, :], ACT.Copy).then_inc(s_id, 1)
                    act.activation(rmask_bf[:, :], rmask_sb[:, :], ACT.Copy).then_inc(s_id, 1)
                    act.wait_ge(s_id, 2)
                    act.wait_ge(s_late, 16 * 11)

                @block.tensor
                def _(pe):
                    pe.wait_ge(s_const, 16 * n_const)

                    def body(i):
                        for u in range(PAIR):
                            t = PAIR * i + u
                            pe.wait_ge(s_patch[u], 16 * i + 16)
                            if not is_first(i):
                                pe.wait_ge(s_add, t - 1)
                            for k in range(EMB_K):
                                mm = nc.tensor.matmul(bank[u][:, 0:D], patch[u][:, k, :], w_emb[:, k, :],
                                                      start=(k == 0), stop=(k == EMB_K - 1))
                            mm.then_inc(s_mm, 1)
                    for_each(pe, EMB_TILES // PAIR, body)
                    pe.wait_ge(s_ones, 3)
                    pe.wait_ge(s_sum, 1)
                    nc.tensor.matmul(bank[2][:, 0:3], ones[:, :], abs_sum, start=True, stop=True).then_inc(s_tot, 1)

                @block.vector
                def _(dve):
                    dve.wait_ge(s_const, 16 * n_const)

                    def body(i):
                        for u in range(PAIR):
                            t = PAIR * i + u
                            dve.wait_ge(s_mm, t + 1)
                            if not is_first(i):
                                dve.wait_ge(s_st[u], 32 * i)
                            nc.vector.tensor_tensor(xn[:, u, :], bank[u][:, 0:D], bemb_sb[:, :], ALU.add).then_inc(s_add, 1)
                    for_each(dve, EMB_TILES // PAIR, body)

                    chain = Chain(dve, s_chain)
                    dve.wait_ge(s_raw, 32)
                    up = KT * 2 * INNER
                    both = ffn_raw[:, 0:up].rearrange("p (k g c) -> p g k c", k=KT, g=2)
                    for g in range(2):
                        ins = nc.vector.tensor_reduce(abs_sum[:, g:g + 1], both[:, g], AX.XY, ALU.add, apply_absolute_value=True)
                    ins = nc.vector.tensor_reduce(abs_sum[:, 2:3], ffn_raw[:, up:], AX.X, ALU.add, apply_absolute_value=True)
                    ins.then_inc(s_sum, 1)
                    dve.wait_ge(s_tot, 1)
                    chain.link(nc.vector.tensor_scalar(w_scale[:, :], bank[2][:, 0:3], 1.0 / (D * INNER), 1e-5, ALU.mult, ALU.max))
                    inverse = stats[:, 1, 0:3]
                    chain.link(nc.vector.reciprocal(inverse, w_scale[:, :]))
                    quant = ffn_up_q[:, :, :].rearrange("p k (g c) -> p g k c", g=2)
                    parts = [(both[:, 0], quant[:, 0]), (both[:, 1], quant[:, 1]),
                             (ffn_raw[:, up:], ffn_down_q[:, :, :].rearrange("p k c -> p (k c)"))]
                    for g, (raw, q) in enumerate(parts):
                        chain.link(nc.vector.tensor_scalar(raw, raw, inverse[:, g:g + 1], ROUND, ALU.mult, ALU.add))
                        chain.link(nc.vector.tensor_scalar(raw, raw, ROUND, 1.0, ALU.subtract, ALU.min))
                        chain.link(nc.vector.tensor_scalar(q, raw, -1.0, None, ALU.max))

        xT_patch = qT[:, :, 0:PAIR * EMB_K * P // KT].rearrange("p k (a r) -> p k a r", r=P)
        v_zero = kT[:, 0, 0:D]
        v_out = sb("v_out", [P, PAIR, HEADS * VC], BF16)

        def finish_stats(dve, chain, s_var, s_rstd):
            for t in range(TILES):
                last = nc.vector.bn_aggr(mean_var[:, t, :], stats[:, t, :])
            chain.link(last)
            nc.vector.tensor_scalar(rstd[:, :], mean_var[:, :, 1], LN_EPS, None, ALU.add).then_inc(s_var, 1)
            dve.wait_ge(s_rstd, 1)
            chain.link(nc.vector.scalar_tensor_tensor(shift[:, :], mean_var[:, :, 0], -1.0, rstd[:, :], ALU.mult, ALU.mult))

        def raise_power(pool, s_var, s_rstd):
            pool.wait_ge(s_var, 1)
            nc.gpsimd.tensor_tensor(rstd[:, :], rstd[:, :], expo[:, :], ALU.pow).then_inc(s_rstd, 1)

        def stats_phase():
            s_chain = sem("st_chain")
            with nc.Block() as block:
                @block.vector
                def _(dve):
                    chain = Chain(dve, s_chain)
                    for t in range(TILES):
                        last = nc.vector.bn_stats(stats[:, t, :], h[:, t, :])
                    chain.link(last)

        def project_phase(layer):
            n = f"p{layer}_"
            s_chain = sem(n + "chain")
            s_var, s_rstd, s_ln = sem(n + "var"), sem(n + "rstd"), sem(n + "ln")
            s_xn, s_tx, s_xT = sem(n + "xn"), sem(n + "tx"), sem(n + "xT")
            s_qk, s_v = sem(n + "qk"), sem(n + "v")
            s_qkb, s_vb = sem(n + "qkb"), sem(n + "vb")
            s_cos, s_rot = sem(n + "cos"), sem(n + "rot")
            s_tq, s_qT = sem(n + "tq"), sem(n + "qT")
            s_v0, s_r1, s_v1, s_v2 = sem(n + "v0"), sem(n + "r1"), sem(n + "v1"), sem(n + "v2")
            s_st = [sem(n + f"st{u}") for u in range(PAIR)]
            qk_cols = 2 * D if layer == 0 else 0
            qk = work[:, :, 0:2 * D]
            qk_cos = work[:, :, 2 * D:4 * D]
            qk_rot = work[:, :, 4 * D:6 * D]
            v = work[:, :, 6 * D:7 * D]
            v_res = work[:, :, 7 * D:8 * D]
            w = wqkv_sb if layer == 0 else wv1_sb
            bias = bqkv_sb if layer == 0 else bv1_sb
            turned = qk_rot if layer == 0 else v
            turns = 4 if layer == 0 else 2
            s_turned = s_rot if layer == 0 else s_vb
            v_parts = [v_out[:, u, :].rearrange("p (h c) -> p h c", c=VC) for u in range(PAIR)]

            def heads(x):
                return x.rearrange("p (h c) -> p h c", c=DH)

            with nc.Block() as block:
                @block.gpsimd
                def _(pool):
                    raise_power(pool, s_var, s_rstd)

                    def body(i):
                        for u in range(PAIR):
                            t = PAIR * i + u
                            if layer == 0:
                                pool.wait_ge(s_qkb, t + 1)
                                if not is_first(i):
                                    pool.wait_ge(s_rot, t - 1)
                                x = qk[:, u, :].rearrange("p (a h c) -> p a h c", a=2, c=DH)
                                o = qk_cos[:, u, :].rearrange("p (a h c) -> p a h c", a=2, c=DH)
                                c = cos_sb[:, bass.ds(t, 1), :].rearrange("p x (a c) -> p (x a) c", a=2)
                                c = c.unsqueeze(2).broadcast_to([P, 2, HEADS, DH])
                                nc.gpsimd.tensor_tensor(o, x, c, ALU.mult).then_inc(s_cos, 1)
                        for u in range(PAIR):
                            t = PAIR * i + u
                            pool.wait_ge(s_v0, t + 1)
                            if not is_first(i):
                                pool.wait_ge(s_v2, t - 1)
                            nc.gpsimd.tensor_tensor(heads(v_res[:, u, :]), heads(v[:, u, :]), v_parts[u][:, :, 0:DH], ALU.subtract).then_inc(s_r1, 1)
                        for u in range(PAIR):
                            t = PAIR * i + u
                            pool.wait_ge(s_v1, t + 1)
                            nc.gpsimd.tensor_tensor(v_parts[u][:, :, 2 * DH:3 * DH], heads(v_res[:, u, :]),
                                                    v_parts[u][:, :, DH:2 * DH], ALU.subtract).then_inc(s_v2, 1)
                    for_each(pool, PASSES, body)

                @block.scalar
                def _(act):
                    act.wait_ge(s_ln, 1)

                    def body(i):
                        for u in range(PAIR):
                            t = PAIR * i + u
                            if not is_first(i):
                                act.wait_ge(s_tx, t - 1)
                            nc.scalar.activation(xn[:, u, :], col(t)(h), ACT.Identity, bias=shift[:, bass.ds(t, 1)],
                                                 scale=rstd[:, bass.ds(t, 1)]).then_inc(s_xn, 1)
                        for u in range(PAIR):
                            t = PAIR * i + u
                            act.wait_ge(s_tx, t + 1)
                            if not is_first(i):
                                act.wait_ge(s_v, t - 1)
                            nc.scalar.activation(xT[:, u, :], bank[u][:, 0:D], ACT.Copy).then_inc(s_xT, 1)
                        for u in range(PAIR):
                            t = PAIR * i + u
                            act.wait_ge(s_vb, t + 1)
                            if not is_first(i):
                                act.wait_ge(s_st[u], 16 * i)
                            nc.scalar.activation(v_parts[u][:, :, 0:DH], heads(v[:, u, :]), ACT.Copy).then_inc(s_v0, 1)
                        for u in range(PAIR):
                            t = PAIR * i + u
                            act.wait_ge(s_r1, t + 1)
                            nc.scalar.activation(v_parts[u][:, :, DH:2 * DH], heads(v_res[:, u, :]), ACT.Copy).then_inc(s_v1, 1)
                        for u in range(PAIR):
                            t = PAIR * i + u
                            act.wait_ge(s_tq, t + 1)
                            src = bank[6 + u][:, 0:turns * P].rearrange("p (k q) -> p k q", q=P)
                            if layer == 0:
                                nc.scalar.activation(tile_cols(qT, t), src[:, 0:KT], ACT.Copy)
                                nc.scalar.activation(tile_cols(kT, t), src[:, KT:2 * KT], ACT.Copy).then_inc(s_qT, 1)
                            else:
                                nc.scalar.activation(tile_cols(qT, t), src, ACT.Copy, scale=0.5).then_inc(s_qT, 1)
                    for_each(act, PASSES, body)

                @block.tensor
                def _(pe):
                    def body(i):
                        for u in range(PAIR):
                            t = PAIR * i + u
                            pe.wait_ge(s_xn, t + 1)
                            if not is_first(i):
                                pe.wait_ge(s_xT, t - 1)
                            for k in range(KT):
                                mm = nc.tensor.transpose(bank[u][:, P * k:P * (k + 1)], xn[:, u, P * k:P * (k + 1)], ident[:, :])
                            mm.then_inc(s_tx, 1)
                        for u in range(PAIR):
                            t = PAIR * i + u
                            pe.wait_ge(s_xT, t + 1)
                            if not is_first(i):
                                if layer == 0:
                                    pe.wait_ge(s_qkb, t - 1)
                                pe.wait_ge(s_vb, t - 1)
                            if layer == 0:
                                for k in range(KT):
                                    mm = nc.tensor.matmul(bank[4 + u][:, :], xT[:, u, P * k:P * (k + 1)], w[:, k, 0:2 * D],
                                                          start=(k == 0), stop=(k == KT - 1))
                                mm.then_inc(s_qk, 1)
                            for k in range(KT):
                                mm = nc.tensor.matmul(bank[2 + u][:, 0:D], xT[:, u, P * k:P * (k + 1)], w[:, k, qk_cols:qk_cols + D],
                                                      start=(k == 0), stop=(k == KT - 1))
                            mm.then_inc(s_v, 1)
                        for u in range(PAIR):
                            t = PAIR * i + u
                            pe.wait_ge(s_turned, t + 1)
                            if not is_first(i):
                                pe.wait_ge(s_qT, t - 1)
                            for k in range(turns):
                                mm = nc.tensor.transpose(bank[6 + u][:, P * k:P * (k + 1)], turned[:, u, P * k:P * (k + 1)], ident[:, :])
                            mm.then_inc(s_tq, 1)
                    for_each(pe, PASSES, body)

                @block.vector
                def _(dve):
                    chain = Chain(dve, s_chain)
                    finish_stats(dve, chain, s_var, s_rstd)
                    nc.vector.tensor_copy(neg_max[:, 0, 0:1], shift[:, 0:1]).then_inc(s_ln, 1)

                    def body(i):
                        for u in range(PAIR):
                            t = PAIR * i + u
                            if layer == 0:
                                dve.wait_ge(s_qk, t + 1)
                                if not is_first(i):
                                    dve.wait_ge(s_cos, t - 1)
                                nc.vector.tensor_tensor(qk[:, u, :], bank[4 + u][:, :], bias[:, 0:2 * D], ALU.add).then_inc(s_qkb, 1)
                            dve.wait_ge(s_v, t + 1)
                            if not is_first(i):
                                dve.wait_ge(s_r1, t - 1)
                                if layer == 1:
                                    dve.wait_ge(s_tq, t - 1)
                            nc.vector.tensor_tensor(v[:, u, :], bank[2 + u][:, 0:D], bias[:, qk_cols:qk_cols + D], ALU.add).then_inc(s_vb, 1)
                        if layer == 1:
                            return
                        for u in range(PAIR):
                            t = PAIR * i + u
                            dve.wait_ge(s_qkb, t + 1)
                            if not is_first(i):
                                dve.wait_ge(s_tq, t - 1)
                            x = qk[:, u, :].rearrange("p (a h j w) -> p a h j w", a=2, h=HEADS, w=2)
                            o = qk_rot[:, u, :].rearrange("p (a h j w) -> p a h j w", a=2, h=HEADS, w=2)
                            s = sin_sb[:, bass.ds(t, 1), :].rearrange("p x (a j w) -> p (x a) j w", a=2, w=2)
                            for a in range(2):
                                for w2 in range(2):
                                    sw = s[:, a, :, w2].unsqueeze(1).broadcast_to([P, HEADS, DH // 2])
                                    last = nc.vector.tensor_tensor(o[:, a, :, :, w2], x[:, a, :, :, 1 - w2], sw, ALU.mult)
                            chain.link(last)
                            dve.wait_ge(s_cos, t + 1)
                            nc.vector.tensor_tensor(qk_rot[:, u, :], qk_rot[:, u, :], qk_cos[:, u, :], ALU.add).then_inc(s_rot, 1)

                    base = chain.n

                    def counted(i):
                        chain.n = 0
                        chain.base = base + (i * PAIR)
                        body(i)
                    for_each(dve, PASSES, counted)

                @block.sync
                def _(sp):
                    def body(i):
                        for u in range(PAIR):
                            t = PAIR * i + u
                            sp.wait_ge(s_v2, t + 1)
                            sp.dma_start(v_dram[bass.ds(P * t, P), :], v_out[:, u, :]).then_inc(s_st[u], 16)
                    for_each(sp, PASSES, body)
                    for u in range(PAIR):
                        sp.wait_ge(s_st[u], 16 * PASSES)

        def attention_phase(layer):
            n = f"a{layer}_"
            keys = kT if layer == 0 else qT
            s_zero = sem(n + "zero")
            s_ld = [sem(n + f"ld{u}") for u in range(PAIR)]
            s_qm = sem(n + "qm")
            s_s = sem(n + "s")
            s_max = sem(n + "max")
            s_exp = sem(n + "exp")
            s_t = sem(n + "t")
            s_hi, s_lo = sem(n + "hi"), sem(n + "lo")
            s_pl = sem(n + "pl")
            s_vd = sem(n + "vd")
            s_o, s_oe = sem(n + "o"), sem(n + "oe")
            s_r, s_rc = sem(n + "r"), sem(n + "rc")
            s_rs, s_rd, s_ro = sem(n + "rs"), sem(n + "rd"), sem(n + "ro")
            s_oo = sem(n + "oo")
            s_chain, s_pchain = sem(n + "chain"), sem(n + "pchain")
            s_st = [sem(n + f"st{u}") for u in range(PAIR)]
            passes = IMAGES // PAIR
            LOADS = 4
            hc = HH * VC
            turn_needs = [2, 3, 4, 6, 6, 6]

            def o_rows(b, lo, count):
                if layer == 0:
                    return o_dram[bass.ds(SEQ * b + lo, count), :]
                flat = o_dram[bass.ds(SEQ * b, SEQ), :].rearrange("s c -> (s c)")
                return flat.rearrange("(h s d) -> s h d", h=HEADS, d=DH)[lo:lo + count]

            with nc.Block() as block:
                @block.sync
                def _(sp):
                    def load(b, u):
                        rows, rem = v_dram[bass.ds(SEQ * b, P), :], v_dram[bass.ds(SEQ * b + P, REM), :]
                        sp.dma_start(v_main[:, u, :], rows).then_inc(s_ld[u], 16)
                        sp.dma_start(v_rem[0:REM, u, :], rem).then_inc(s_ld[u], 16)
                        sp.dma_start(v_rem[32:32 + REM, u, :], rem).then_inc(s_ld[u], 16)
                        sp.dma_start(v_rep[0:HR, u, :], rem.unsqueeze(0).broadcast_to([HH, REM, HEADS * VC])).then_inc(s_ld[u], 16)

                    def store(b, u):
                        sp.wait_ge(s_oo, b + 1)
                        src, rsrc = o_out[:, u, :], r_out[0:REM, u, :]
                        if layer == 1:
                            src, rsrc = (x.rearrange("p (h d) -> p h d", d=DH) for x in (src, rsrc))
                        sp.dma_start(o_rows(b, 0, P), src).then_inc(s_st[u], 16)
                        sp.wait_ge(s_ro, b + 1)
                        sp.dma_start(o_rows(b, P, REM), rsrc).then_inc(s_st[u], 16)

                    sp.wait_ge(s_zero, 3)
                    for u in range(PAIR):
                        load(u, u)

                    def body(i, last=False):
                        for u in range(PAIR):
                            b = PAIR * i + u
                            sp.wait_ge(s_r, b + 1)
                            if not last:
                                load(b + PAIR, u)
                            store(b, u)
                    body(0)
                    with sp.Fori(1, passes - 1) as i:
                        body(i)
                    body(passes - 1, last=True)
                    for u in range(PAIR):
                        sp.wait_ge(s_st[u], 32 * passes)

                @block.gpsimd
                def _(pool):
                    pool.memset(q_rem[:, :, :, :], 0.0).then_inc(s_zero, 1)
                    pool.memset(pT_corner, 0.0).then_inc(s_zero, 1)
                    pool.memset(v_rem, 0.0).then_inc(s_zero, 1)
                    pool.wait_ge(s_zero, 3)

                    def masks(b, u, first):
                        if not first:
                            pool.wait_ge(s_s, SGROUPS * b - SGROUPS * (PAIR - 1))
                        m = mask_sb[:, :]
                        for k in range(KT):
                            q = qT[:, k, bass.ds(SEQ * b, P)].unsqueeze(1).broadcast_to([P, HH, P])
                            nc.gpsimd.tensor_tensor(q_masked[:, u, k], q, m.unsqueeze(2).broadcast_to([P, HH, P]), ALU.mult).then_inc(s_qm, 1)
                        for k in range(KT):
                            q = qT[:, k, bass.ds(SEQ * b + P, REM)].unsqueeze(1).broadcast_to([P, HH, REM])
                            o = q_rem[:, u, k, 0:HR].rearrange("p (h q) -> p h q", h=HH)
                            nc.gpsimd.tensor_tensor(o, q, m.unsqueeze(2).broadcast_to([P, HH, REM]), ALU.mult).then_inc(s_qm, 1)

                    def last_keys(b, u, first):
                        pool.wait_ge(s_exp, SGROUPS * b + SGROUPS)
                        if not first:
                            pool.wait_ge(s_t, TGROUPS * b - TGROUPS * (PAIR - 1))
                        one = ones[:, 0:1].unsqueeze(2).broadcast_to([P, HEADS, REM])
                        nc.gpsimd.tensor_tensor(prob_last[:, u, :].rearrange("p (h k) -> p h k", k=REM), prob[:, u, 0:HEADS, P:SEQ], one,
                                                ALU.mult).then_inc(s_pl, 1)

                    def last_rows(b, u, first, base):
                        pool.wait_ge(s_rc, b + 1)
                        parts = r_raw[0:REM, :].rearrange("p (h c) -> p h c", c=VC)
                        total = r_sum[0:REM, :].rearrange("p (h c) -> p h c", c=DH)
                        nc.gpsimd.tensor_tensor(total, parts[:, :, 0:DH], parts[:, :, DH:2 * DH], ALU.add).then_inc(s_pchain, 1)
                        pool.wait_ge(s_pchain, base + 1)
                        nc.gpsimd.tensor_tensor(total, total, parts[:, :, 2 * DH:3 * DH], ALU.add).then_inc(s_pchain, 1)
                        pool.wait_ge(s_pchain, base + 2)
                        pool.wait_ge(s_rd, b + 1)
                        if not first:
                            pool.wait_ge(s_st[u], 16 * b - 16 * u)
                        o = r_out[0:REM, u, :].rearrange("p (h c) -> p h c", c=DH)
                        den = r_den[0:REM, :].unsqueeze(2).broadcast_to([REM, HEADS, DH])
                        nc.gpsimd.tensor_tensor(o, total, den, ALU.mult).then_inc(s_ro, 1)

                    for u in range(PAIR):
                        masks(u, u, True)

                    def body(i, last=False):
                        for u in range(PAIR):
                            last_keys(PAIR * i + u, u, is_first(i))
                            if not last:
                                masks(PAIR * i + PAIR + u, u, False)
                        for u in range(PAIR):
                            b = PAIR * i + u
                            last_rows(b, u, is_first(i), 2 * b)
                    body(0)
                    with pool.Fori(1, passes - 1) as i:
                        body(i)
                    body(passes - 1, last=True)

                @block.tensor
                def _(pe):
                    def scores(b, u, g, first):
                        n = SGROUPS * b + g
                        if not (first and u == 0 and g < 2):
                            pe.wait_ge(s_exp, n - 1)
                        for j in range(3):
                            s = 3 * g + j
                            k = s // HH if s < HEADS else s - HEADS
                            q = q_masked[:, u, k, s % HH, :] if s < HEADS else q_rem[:, u, k, :]
                            mm = nc.tensor.matmul(bank[g % 2][:, SEQ * j:SEQ * (j + 1)], q, keys[:, k, bass.ds(SEQ * b, SEQ)],
                                                  start=True, stop=True)
                        mm.then_inc(s_s, 1)

                    def turn(b, u, g, first):
                        n = TGROUPS * b + g
                        pe.wait_ge(s_exp, SGROUPS * b + turn_needs[g])
                        if not (first and u == 0 and g < 2):
                            pe.wait_ge(s_lo, n - 1)
                        ps = bank[2 + g % 2]
                        if g < 4:
                            for j in range(4):
                                mm = nc.tensor.transpose(ps[:, P * j:P * (j + 1)], prob[:, u, 4 * g + j, 0:P], ident[:, :])
                        elif g == 4:
                            for k in range(KT):
                                nc.tensor.transpose(ps[:, P * k:P * (k + 1)], prob[:, u, HEADS + k, 0:P], ident[:, :])
                            pe.wait_ge(s_pl, b + 1)
                            for k in range(KT):
                                mm = nc.tensor.transpose(ps[0:HR, P * (KT + k):P * (KT + k + 1)],
                                                         prob_last[:, u, HR * k:HR * (k + 1)], ident[:, :])
                        else:
                            for k in range(KT):
                                mm = nc.tensor.transpose(ps[0:REM, P * k:P * (k + 1)], prob[:, u, HEADS + k, P:SEQ], ident[:, :])
                        mm.then_inc(s_t, 1)

                    def values(b, u, g, first):
                        n = TGROUPS * b + g
                        pe.wait_ge(s_lo, n + 1)
                        for hd in range(4 * g, 4 * g + 4) if g < 4 else ():
                            k, j = hd // HH, hd % HH
                            if j == 0 and not (first and u == 0):
                                pe.wait_ge(s_oe, KT * b + k - 1)
                            for a in range(2):
                                nc.tensor.matmul(bank[4 + k][:, VC * j:VC * (j + 1)], pT[:, a, hd, :], v_main[:, u, VC * hd:VC * (hd + 1)],
                                                 start=(j == 0 and a == 0), stop=False, skip_group_check=True)
                        if g == 4:
                            pe.wait_ge(s_vd, b + 1)
                            for k in range(KT):
                                for a in range(2):
                                    mm = nc.tensor.matmul(bank[4 + k][:, 0:hc], pT_rem[0:HR, a, KT + k, :], v_diag[0:HR, u, hc * k:hc * (k + 1)],
                                                          start=False, stop=(a == 1), skip_group_check=True)
                            mm.then_inc(s_o, 1)
                            if not (first and u == 0):
                                pe.wait_ge(s_rc, b)
                            for hd in range(HEADS):
                                k, j = hd // HH, hd % HH
                                for a in range(2):
                                    nc.tensor.matmul(bank[6 + k][0:REM, VC * j:VC * (j + 1)], pT_rem[:, a, k, REM * j:REM * (j + 1)],
                                                     v_main[:, u, VC * hd:VC * (hd + 1)], start=(j == 0 and a == 0), stop=False,
                                                     skip_group_check=True)
                        if g == 5:
                            for hd in range(HEADS):
                                k, j = hd // HH, hd % HH
                                mm = nc.tensor.matmul(bank[6 + k][0:REM, VC * j:VC * (j + 1)], pT_corner[:, k, REM * j:REM * (j + 1)],
                                                      v_rem[:, u, VC * hd:VC * (hd + 1)], start=False, stop=(j == HH - 1),
                                                      skip_group_check=True)
                            mm.then_inc(s_r, 1)

                    pe.wait_ge(s_zero, 3)

                    pe.wait_ge(s_qm, 4)
                    for g in range(SGROUPS):
                        scores(0, 0, g, True)

                    def body(i, last=False):
                        first = is_first(i)
                        for u in range(PAIR):
                            b = PAIR * i + u
                            ahead = not (last and u == PAIR - 1)
                            if ahead:
                                pe.wait_ge(s_qm, 4 * b + 8)
                            for g in range(TGROUPS):
                                if ahead:
                                    scores(b + 1, 1 - u, g, False)
                                if g == 0 and not (first and u == 0):
                                    values(b - 1, 1 - u, TGROUPS - 1, first)
                                turn(b, u, g, first)
                                if g == 1:
                                    pe.wait_ge(s_ld[u], 16 * LOADS * i + 16 * LOADS)
                                if g >= 1:
                                    values(b, u, g - 1, first)
                    body(0)
                    with pe.Fori(1, passes - 1) as i:
                        body(i)
                    body(passes - 1, last=True)
                    values(IMAGES - 1, 1, TGROUPS - 1, False)

                @block.scalar
                def _(act):
                    def exps(b, u, g, first):
                        if g == 0 and not first:
                            act.wait_ge(s_t, TGROUPS * b - TGROUPS * (PAIR - 1))
                        act.wait_ge(s_max, SGROUPS * b + g + 1)
                        for j in range(3):
                            s = 3 * g + j
                            e = nc.scalar.activation(prob[:, u, s, :], bank[g % 2][:, SEQ * j:SEQ * (j + 1)], ACT.Exp,
                                                     bias=neg_max[:, u, s:s + 1])
                        e.then_inc(s_exp, 1)

                    def high(b, u, g):
                        act.wait_ge(s_t, TGROUPS * b + g + 1)
                        ps = bank[2 + g % 2]
                        if g < 4:
                            c = nc.scalar.activation(pT[:, 0, 4 * g:4 * g + 4, :], ps[:, :].rearrange("p (h q) -> p h q", q=P), ACT.Copy)
                        elif g == 4:
                            both = ps[:, :].rearrange("p (n q) -> p n q", q=P)
                            nc.scalar.activation(pT_rem[:, 0, 0:KT, :], both[:, 0:KT], ACT.Copy)
                            c = nc.scalar.activation(pT_rem[0:HR, 0, KT:2 * KT, :], both[0:HR, KT:2 * KT], ACT.Copy)
                        else:
                            if not (isinstance(b, int) and b == 0):
                                act.wait_ge(s_r, b)
                            c = nc.scalar.activation(pT_corner[0:REM, :, :], ps[0:REM, 0:KT * P].rearrange("p (n q) -> p n q", q=P), ACT.Copy)
                        c.then_inc(s_hi, 1)

                    def last_rows(b, first):
                        act.wait_ge(s_r, b + 1)
                        if not first:
                            act.wait_ge(s_ro, b)
                        for k in range(KT):
                            c = nc.scalar.activation(r_raw[0:REM, hc * k:hc * (k + 1)], bank[6 + k][0:REM, 0:hc], ACT.Copy)
                        c.then_inc(s_rc, 1)

                    for g in range(SGROUPS):
                        exps(0, 0, g, True)

                    def body(i, last=False):
                        first = is_first(i)
                        for u in range(PAIR):
                            b = PAIR * i + u
                            for g in range(TGROUPS):
                                high(b, u, g)
                                if not (last and u == PAIR - 1):
                                    exps(b + 1, 1 - u, g, first and u == 0)
                                if g == 1 and not (first and u == 0):
                                    last_rows(b - 1, first and u == 1)
                    body(0)
                    with act.Fori(1, passes - 1) as i:
                        body(i)
                    body(passes - 1, last=True)
                    last_rows(IMAGES - 1, False)

                @block.vector
                def _(dve):
                    dve.wait_ge(s_zero, 3)

                    def diagonal(b, u):
                        dve.wait_ge(s_ld[u], (16 * LOADS // PAIR) * (b - u) + 16 * LOADS)
                        m = rmask_bf[:, :].unsqueeze(2).broadcast_to([HR, HH, VC])
                        for k in range(KT):
                            o = v_diag[0:HR, u, hc * k:hc * (k + 1)].rearrange("p (h c) -> p h c", c=VC)
                            x = v_rep[0:HR, u, hc * k:hc * (k + 1)].rearrange("p (h c) -> p h c", c=VC)
                            c = nc.vector.tensor_tensor(o, x, m, ALU.mult)
                        c.then_inc(s_vd, 1)

                    def maxima(b, u, g):
                        dve.wait_ge(s_s, SGROUPS * b + g + 1)
                        nc.vector.tensor_reduce(neg_max[:, u, 3 * g:3 * g + 3], bank[g % 2][:, 0:3 * SEQ].rearrange("p (n k) -> p n k", n=3),
                                                AX.X, ALU.max, negate=True).then_inc(s_max, 1)

                    def low(b, u, g):
                        dve.wait_ge(s_hi, TGROUPS * b + g + 1)
                        ps = bank[2 + g % 2][:, :].rearrange("p (n q) -> p n q", q=P)
                        if g < 4:
                            c = nc.vector.tensor_tensor(pT[:, 1, 4 * g:4 * g + 4, :], ps, pT[:, 0, 4 * g:4 * g + 4, :], ALU.subtract)
                        elif g == 4:
                            nc.vector.tensor_tensor(pT_rem[:, 1, 0:KT, :], ps[:, 0:KT], pT_rem[:, 0, 0:KT, :], ALU.subtract)
                            c = nc.vector.tensor_tensor(pT_rem[0:HR, 1, KT:2 * KT, :], ps[0:HR, KT:2 * KT], pT_rem[0:HR, 0, KT:2 * KT, :], ALU.subtract)
                        else:
                            c = nc.vector.tensor_tensor(pT_corner[32:32 + REM, :, :], ps[0:REM, 0:KT], pT_corner[0:REM, :, :], ALU.subtract)
                        c.then_inc(s_lo, 1)

                    def rows(b, u):
                        dve.wait_ge(s_o, b + 1)
                        for k in range(KT):
                            parts = bank[4 + k][:, 0:hc].rearrange("p (h c) -> p h c", c=VC)
                            nc.vector.reciprocal(o_den[:, HH * k:HH * (k + 1)], parts[:, :, VC - 1])
                            three = parts[:, :, 0:3 * DH].rearrange("p h (a d) -> p h d a", a=3)
                            nc.vector.tensor_reduce(o_sum[:, P * k:P * (k + 1)].rearrange("p (h d) -> p h d", d=DH),
                                                    three, AX.X, ALU.add).then_inc(s_oe, 1)
                        dve.wait_ge(s_oe, KT * b + KT)
                        if not (isinstance(b, int) and b < PAIR):
                            dve.wait_ge(s_st[u], 16 * b - 16 * u)
                        den = o_den[:, :].unsqueeze(2).broadcast_to([P, HEADS, DH])
                        nc.vector.tensor_tensor(o_out[:, u, :].rearrange("p (h d) -> p h d", d=DH),
                                                o_sum[:, :].rearrange("p (h d) -> p h d", d=DH), den, ALU.mult).then_inc(s_oo, 1)

                    def last_sums(b):
                        dve.wait_ge(s_rc, b + 1)
                        nc.vector.reciprocal(r_den[0:REM, :], r_raw[0:REM, :].rearrange("p (h c) -> p h c", c=VC)[:, :, VC - 1]).then_inc(s_rd, 1)

                    for g in range(SGROUPS):
                        maxima(0, 0, g)

                    def body(i, last=False):
                        first = is_first(i)
                        for u in range(PAIR):
                            b = PAIR * i + u
                            for g in range(TGROUPS):
                                if not (last and u == PAIR - 1):
                                    maxima(b + 1, 1 - u, g)
                                if g == 0 and not (first and u == 0):
                                    rows(b - 1, 1 - u)
                                low(b, u, g)
                                if g == 1:
                                    diagonal(b, u)
                                if g == 2 and not (first and u == 0):
                                    last_sums(b - 1)
                    body(0)
                    body(1)
                    with dve.Fori(2, passes - 1) as i:
                        body(i)
                    body(passes - 1, last=True)
                    rows(IMAGES - 1, 1)
                    last_sums(IMAGES - 1)

        def output_phase(layer):
            n = f"o{layer}_"
            s_ld = [sem(n + f"ld{u}") for u in range(PAIR)]
            s_t, s_T, s_mm, s_bias, s_add = (sem(n + x) for x in ("t", "T", "mm", "bias", "add"))
            s_st = sem(n + "stats")
            s_moe = sem(n + "moe")
            with nc.Block() as block:
                @block.sync
                def _(sp):
                    if layer == 0:
                        sp.dma_start(gu_sb, w_gu_t.rearrange("(k p) e c -> p k e c", p=P)).then_inc(s_moe, 16)
                        sp.dma_start(down_sb, w_down_t).then_inc(s_moe, 16)

                    def body(i):
                        for u in range(PAIR):
                            t = PAIR * i + u
                            if not is_first(i):
                                sp.wait_ge(s_t, t - 1)
                            sp.dma_start(xn[:, u, :], o_dram[bass.ds(P * t, P), :]).then_inc(s_ld[u], 16)
                    for_each(sp, PASSES, body)
                    if layer == 0:
                        sp.wait_ge(s_moe, 32)

                @block.gpsimd
                def _(pool):
                    def body(i):
                        for u in range(PAIR):
                            t = PAIR * i + u
                            nc.gpsimd.tensor_tensor(col(t)(h), col(t)(h), bo_sb[layer][:, :], ALU.add).then_inc(s_bias, 1)
                    for_each(pool, PASSES, body)

                @block.tensor
                def _(pe):
                    def body(i):
                        for u in range(PAIR):
                            t = PAIR * i + u
                            pe.wait_ge(s_ld[u], 16 * i + 16)
                            if not is_first(i):
                                pe.wait_ge(s_T, t - 1)
                            for k in range(KT):
                                mm = nc.tensor.transpose(bank[u][:, P * k:P * (k + 1)], xn[:, u, P * k:P * (k + 1)], ident[:, :])
                            mm.then_inc(s_t, 1)
                        for u in range(PAIR):
                            t = PAIR * i + u
                            pe.wait_ge(s_T, t + 1)
                            if not is_first(i):
                                pe.wait_ge(s_add, t - 1)
                            for k in range(KT):
                                mm = nc.tensor.matmul(bank[2 + u][:, 0:D], xT[:, u, P * k:P * (k + 1)], wo_sb[layer][:, k, :],
                                                      start=(k == 0), stop=(k == KT - 1))
                            mm.then_inc(s_mm, 1)
                    for_each(pe, PASSES, body)

                @block.scalar
                def _(act):
                    def body(i):
                        for u in range(PAIR):
                            t = PAIR * i + u
                            act.wait_ge(s_t, t + 1)
                            if not is_first(i):
                                act.wait_ge(s_mm, t - 1)
                            nc.scalar.activation(xT[:, u, :], bank[u][:, 0:D], ACT.Copy).then_inc(s_T, 1)
                    for_each(act, PASSES, body)

                @block.vector
                def _(dve):
                    def body(i):
                        for u in range(PAIR):
                            t = PAIR * i + u
                            dve.wait_ge(s_mm, t + 1)
                            dve.wait_ge(s_bias, t + 1)
                            nc.vector.tensor_tensor(col(t)(h), bank[2 + u][:, 0:D], col(t)(h), ALU.add).then_inc(s_add, 1)
                        for u in range(PAIR):
                            t = PAIR * i + u
                            dve.wait_ge(s_add, t + 1)
                            nc.vector.bn_stats(col(t)(stats), col(t)(h)).then_inc(s_st, 1)
                    for_each(dve, PASSES, body)
                    dve.wait_ge(s_st, TILES)

        w_rows = sb("w_rows", [P, PADDED], BF16)
        w3 = sb("w3", [P, PAIR, P], BF16)
        group_pad = sb("group_pad", [P, PAIR, 8])

        def route_phase():
            s_chain = sem("r_chain")
            s_var, s_rstd, s_ln = sem("r_var"), sem("r_rstd"), sem("r_ln")
            s_xn, s_tx, s_xT, s_res = sem("r_xn"), sem("r_tx"), sem("r_xT"), sem("r_res")
            s_mm, s_sig, s_w, s_tw, s_wT = (sem("r_" + x) for x in ("mm", "sig", "w", "tw", "wT"))
            sc = work[:, 0, 0:2048]
            at = [0]

            def cut(n):
                a = at[0]
                at[0] += n
                return sc[:, a:a + n]
            scores = cut(PAIR * EXPERTS)
            choice = cut(PAIR * EXPERTS)
            hi2 = cut(PAIR * GROUPS * 2)
            lo2 = cut(PAIR * GROUPS * 2)
            top1, mid, low = cut(PAIR * GROUPS), cut(PAIR * GROUPS), cut(PAIR * GROUPS)
            gval = cut(PAIR * 8).rearrange("p (t k) -> p t k", t=PAIR)
            gidx = cut(PAIR * 8).bitcast(U32).rearrange("p (t k) -> p t k", t=PAIR)
            ghot = cut(PAIR * GROUPS * 2).rearrange("p (t g k) -> p t g k", t=PAIR, k=2)
            gmask = cut(PAIR * GROUPS)
            kept = cut(PAIR * EXPERTS)
            kval = cut(PAIR * 8).rearrange("p (t k) -> p t k", t=PAIR)
            kidx = cut(PAIR * 8).bitcast(U32).rearrange("p (t k) -> p t k", t=PAIR)
            khot = cut(PAIR * EXPERTS * TOPK).rearrange("p (t e k) -> p t e k", t=PAIR, k=TOPK)
            chosen = cut(PAIR * EXPERTS)
            weight = cut(PAIR * EXPERTS)
            den = cut(PAIR)
            rest = cut(PAIR * EXPERTS)
            carrier = cut(1)
            w_part = w3[:, :, 0:3 * EXPERTS].rearrange("p t (a e) -> p t a e", a=3)

            def by_tile(x):
                return x.rearrange("p (t e) -> p t e", t=PAIR)

            with nc.Block() as block:
                @block.gpsimd
                def _(pool):
                    raise_power(pool, s_var, s_rstd)

                @block.scalar
                def _(act):
                    act.wait_ge(s_ln, 1)

                    def body(i):
                        for u in range(PAIR):
                            t = PAIR * i + u
                            if not is_first(i):
                                act.wait_ge(s_tx, t - 1)
                            nc.scalar.activation(xn[:, u, :], col(t)(h), ACT.Identity, bias=shift[:, bass.ds(t, 1)],
                                                 scale=rstd[:, bass.ds(t, 1)]).then_inc(s_xn, 1)
                        for u in range(PAIR):
                            t = PAIR * i + u
                            act.wait_ge(s_tx, t + 1)
                            if not is_first(i):
                                act.wait_ge(s_mm, t - 1)
                            nc.scalar.activation(xT[:, u, :], bank[u][:, 0:D], ACT.Copy).then_inc(s_xT, 1)
                            nc.scalar.activation(tile_cols(qT, t), bank[u][:, 0:D].rearrange("p (k q) -> p k q", q=P),
                                                 ACT.Copy).then_inc(s_res, 1)
                        for u in range(PAIR):
                            t = PAIR * i + u
                            act.wait_ge(s_mm, t + 1)
                            if not is_first(i):
                                act.wait_ge(s_w, i)
                            nc.scalar.activation(scores[:, EXPERTS * u:EXPERTS * (u + 1)], bank[2 + u][:, 0:EXPERTS],
                                                 ACT.Sigmoid).then_inc(s_sig, 1)
                        for u in range(PAIR):
                            t = PAIR * i + u
                            act.wait_ge(s_tw, t + 1)
                            src = bank[4 + u][:, :].bitcast(BF16)[:, 0:P]
                            nc.scalar.activation(w_rows[:, bass.ds(P * t, P)], src, ACT.Copy).then_inc(s_wT, 1)
                    for_each(act, PASSES, body)

                @block.tensor
                def _(pe):
                    def body(i):
                        for u in range(PAIR):
                            t = PAIR * i + u
                            pe.wait_ge(s_xn, t + 1)
                            if not is_first(i):
                                pe.wait_ge(s_res, t - 1)
                            for k in range(KT):
                                mm = nc.tensor.transpose(bank[u][:, P * k:P * (k + 1)], xn[:, u, P * k:P * (k + 1)], ident[:, :])
                            mm.then_inc(s_tx, 1)
                        for u in range(PAIR):
                            t = PAIR * i + u
                            pe.wait_ge(s_xT, t + 1)
                            if not is_first(i):
                                pe.wait_ge(s_sig, t - 1)
                            for k in range(KT):
                                mm = nc.tensor.matmul(bank[2 + u][:, 0:EXPERTS], xT[:, u, P * k:P * (k + 1)], wgate_sb[:, k, :],
                                                      start=(k == 0), stop=(k == KT - 1))
                            mm.then_inc(s_mm, 1)
                        for u in range(PAIR):
                            t = PAIR * i + u
                            pe.wait_ge(s_w, i + 1)
                            if not is_first(i):
                                pe.wait_ge(s_wT, t - 1)
                            nc.tensor.transpose(bank[4 + u][:, :].bitcast(BF16)[:, 0:P],
                                                w3[:, u, :], ident_bf[:, :]).then_inc(s_tw, 1)
                    for_each(pe, PASSES, body)

                @block.vector
                def _(dve):
                    chain = Chain(dve, s_chain)
                    nc.vector.memset(w3[:, :, :], 0.0)
                    chain.link(nc.vector.memset(group_pad[:, :, :], LOWEST))
                    finish_stats(dve, chain, s_var, s_rstd)
                    nc.vector.tensor_copy(group_pad[:, 0, 0:1], shift[:, 0:1]).then_inc(s_ln, 1)
                    base = chain.n
                    links = [0]

                    def body(i):
                        chain.n = 0
                        chain.base = base + i * links[0]
                        V = nc.vector
                        tt = V.tensor_tensor
                        dve.wait_ge(s_sig, PAIR * i + PAIR)
                        eb = ebias_sb[:, :].unsqueeze(1).broadcast_to([P, PAIR, EXPERTS])
                        chain.link(tt(by_tile(choice), by_tile(scores), eb, ALU.add))
                        four = choice.rearrange("p (g x) -> p g x", x=4)
                        a2, b2 = (x.rearrange("p (g x) -> p g x", x=2) for x in (hi2, lo2))
                        tt(a2, four[:, :, 0:2], four[:, :, 2:4], ALU.max)
                        chain.link(tt(b2, four[:, :, 0:2], four[:, :, 2:4], ALU.min))
                        tt(top1, a2[:, :, 0], a2[:, :, 1], ALU.max)
                        tt(mid, a2[:, :, 0], a2[:, :, 1], ALU.min)
                        chain.link(tt(low, b2[:, :, 0], b2[:, :, 1], ALU.max))
                        chain.link(tt(mid, mid, low, ALU.max))
                        g4 = group_pad[:, :, 0:GROUPS]
                        chain.link(tt(g4, top1.rearrange("p (t g) -> p t g", t=PAIR), mid.rearrange("p (t g) -> p t g", t=PAIR), ALU.add))
                        V.tensor_copy(carrier, ones[:, 0:1])
                        for u in range(PAIR):
                            last = V.max(gval[:, u, :], group_pad[:, u, :])
                        chain.link(last)
                        V.tensor_copy(carrier, ones[:, 0:1])
                        for u in range(PAIR):
                            last = V.max_index(gidx[:, u, :], gval[:, u, :], group_pad[:, u, :])
                        chain.link(last)
                        io = iota[:, 0:GROUPS].unsqueeze(1).unsqueeze(3).broadcast_to([P, PAIR, GROUPS, 2])
                        ix = gidx[:, :, 0:2].unsqueeze(2).broadcast_to([P, PAIR, GROUPS, 2])
                        chain.link(tt(ghot, io, ix, ALU.is_equal))
                        chain.link(V.tensor_reduce(gmask, ghot.rearrange("p t g k -> p (t g) k"), AX.X, ALU.add))
                        gm = gmask.unsqueeze(2).broadcast_to([P, PAIR * GROUPS, 4])
                        chain.link(tt(kept.rearrange("p (g x) -> p g x", x=4), four, gm, ALU.mult))
                        V.tensor_copy(carrier, ones[:, 0:1])
                        for u in range(PAIR):
                            last = V.max(kval[:, u, :], kept[:, EXPERTS * u:EXPERTS * (u + 1)])
                        chain.link(last)
                        V.tensor_copy(carrier, ones[:, 0:1])
                        for u in range(PAIR):
                            last = V.max_index(kidx[:, u, :], kval[:, u, :], kept[:, EXPERTS * u:EXPERTS * (u + 1)])
                        chain.link(last)
                        io = iota[:, :].unsqueeze(2).broadcast_to([P, EXPERTS, TOPK])
                        for u in range(PAIR):
                            ix = kidx[:, u, 0:TOPK].unsqueeze(1).broadcast_to([P, EXPERTS, TOPK])
                            last = tt(khot[:, u], io, ix, ALU.is_equal)
                        chain.link(last)
                        chain.link(V.tensor_reduce(chosen, khot.rearrange("p t e k -> p (t e) k"), AX.X, ALU.add))
                        chain.link(tt(weight, scores, chosen, ALU.mult))
                        chain.link(V.tensor_reduce(den, by_tile(weight), AX.X, ALU.add))
                        chain.link(V.tensor_scalar(den, den, 1e-20, None, ALU.add))
                        chain.link(V.reciprocal(den, den))
                        chain.link(V.tensor_scalar(den, den, 2.5, None, ALU.mult))
                        chain.link(tt(by_tile(weight), by_tile(weight), den.unsqueeze(2).broadcast_to([P, PAIR, EXPERTS]), ALU.mult))
                        if not is_first(i):
                            dve.wait_ge(s_tw, PAIR * i)
                        chain.link(V.tensor_copy(w_part[:, :, 0, :], by_tile(weight)))
                        chain.link(tt(by_tile(rest), by_tile(weight), w_part[:, :, 0, :], ALU.subtract))
                        chain.link(V.tensor_copy(w_part[:, :, 1, :], by_tile(rest)))
                        tt(w_part[:, :, 2, :], by_tile(rest), w_part[:, :, 1, :], ALU.subtract).then_inc(s_w, 1)
                        links[0] = links[0] or chain.n
                    for_each(dve, PASSES, body)

        select = sb("select", [P, EXPERTS, P], BF16)

        def expert_phase():
            s_sel, s_g, s_u, s_wb = sem("m_sel"), sem("m_g"), sem("m_u"), sem("m_wb")
            s_silu, s_prod, s_in, s_dn, s_y = (sem("m_" + x) for x in ("silu", "prod", "in", "dn", "y"))
            s_st = sem("m_stats")
            order = [EXPERTS] + list(range(EXPERTS))
            silu = work[:, :, 0:CHUNK]
            prod = work[:, :, CHUNK:2 * CHUNK]
            inter = work[:, :, 2 * CHUNK:3 * CHUNK]
            with nc.Block() as block:
                @block.gpsimd
                def _(pool):
                    sel0 = select[:, :, :]
                    pool.memset(sel0, 0.0).then_inc(s_sel, 1)
                    for a in range(3):
                        pool.wait_ge(s_sel, a + 1)
                        pool.affine_select(out=sel0, in_=sel0, compare_op=ALU.not_equal, fill=1.0, base=-EXPERTS * a,
                                           pattern=[[-1, EXPERTS], [0, P]], channel_multiplier=1).then_inc(s_sel, 1)

                @block.tensor
                def _(pe):
                    pe.wait_ge(s_sel, 4)

                    def body(c):
                        x = [qT[:, k, bass.ds(CHUNK * c, CHUNK)] for k in range(KT)]

                        def up(s):
                            e, n = order[s], BRANCHES * c + s
                            if e < EXPERTS:
                                m = EXPERTS * c + s - 1
                                if not (is_first(c) and s == 1):
                                    pe.wait_ge(s_in, n)
                                nc.tensor.matmul(bank[4][:, 0:CHUNK], select[:, e, :], w_rows[:, bass.ds(CHUNK * c, CHUNK)],
                                                 start=True, stop=True).then_inc(s_wb, 1)
                            for half, done in ((0, s_g), (1, s_u)):
                                if not (is_first(c) and s < 2):
                                    pe.wait_ge(s_silu if half == 0 else s_prod, n - 1)
                                for k in range(KT):
                                    mm = nc.tensor.matmul(bank[2 * half + s % 2][:, 0:CHUNK], gu_sb[:, k, e, INTER * half:INTER * (half + 1)],
                                                          x[k], start=(k == 0), stop=(k == KT - 1))
                                mm.then_inc(done, 1)

                        def down(s):
                            e, n = order[s], BRANCHES * c + s
                            pe.wait_ge(s_in, n + 1)
                            for j in range(3):
                                if s == 0 and not is_first(c):
                                    pe.wait_ge(s_y, 3 * c - 2 + j)
                                mm = nc.tensor.matmul(bank[5 + j][:, 0:D], inter[:, s % 2, P * j:P * (j + 1)], down_sb[:, e, :],
                                                      start=(s == 0), stop=(s == BRANCHES - 1))
                            mm.then_inc(s_dn, 1)

                        for s in range(BRANCHES):
                            up(s)
                            if s >= 1:
                                down(s - 1)
                        down(BRANCHES - 1)
                    for_each(pe, CHUNKS, body)


                @block.scalar
                def _(act):
                    def body(c):
                        for s in range(BRANCHES):
                            n = BRANCHES * c + s
                            act.wait_ge(s_g, n + 1)
                            if not (is_first(c) and s < 2):
                                act.wait_ge(s_prod, n - 1)
                            nc.scalar.activation(silu[:, s % 2, :], bank[s % 2][:, 0:CHUNK], ACT.Silu).then_inc(s_silu, 1)
                    for_each(act, CHUNKS, body)

                @block.vector
                def _(dve):
                    def body(c):
                        for s in range(BRANCHES):
                            e, n = order[s], BRANCHES * c + s
                            dve.wait_ge(s_silu, n + 1)
                            dve.wait_ge(s_u, n + 1)
                            if s == 0:
                                if not is_first(c):
                                    dve.wait_ge(s_dn, n - 1)
                                nc.vector.tensor_tensor(inter[:, 0, :], silu[:, 0, :], bank[2][:, 0:CHUNK], ALU.mult).then_inc(s_prod, 1)
                                dve.wait_ge(s_prod, n + 1)
                                nc.vector.tensor_copy(prod[:, 0, 0:1], inter[:, 0, 0:1]).then_inc(s_in, 1)
                                continue
                            nc.vector.tensor_tensor(prod[:, s % 2, :], silu[:, s % 2, :], bank[2 + s % 2][:, 0:CHUNK], ALU.mult).then_inc(s_prod, 1)
                            dve.wait_ge(s_prod, n + 1)
                            dve.wait_ge(s_wb, EXPERTS * c + s)
                            if not (is_first(c) and s < 2):
                                dve.wait_ge(s_dn, n - 1)
                            nc.vector.tensor_tensor(inter[:, s % 2, :], prod[:, s % 2, :], bank[4][:, 0:CHUNK], ALU.mult).then_inc(s_in, 1)
                        dve.wait_ge(s_dn, BRANCHES * c + BRANCHES)
                        for j in range(3):
                            t = 3 * c + j
                            nc.vector.tensor_tensor(col(t)(h), bank[5 + j][:, 0:D], col(t)(h), ALU.add).then_inc(s_y, 1)
                        for j in range(3):
                            t = 3 * c + j
                            dve.wait_ge(s_y, t + 1)
                            nc.vector.bn_stats(col(t)(stats), col(t)(h)).then_inc(s_st, 1)
                    for_each(dve, CHUNKS, body)
                    dve.wait_ge(s_st, TILES)

        def ffn_phase():
            names = ("xn", "q", "tq", "qT", "g0", "u0", "sl0", "p0", "g1", "u1", "sl1", "p1", "q2", "t2", "q2T", "dn", "out")
            s = {x: sem("f_" + x) for x in names}
            s_chain, s_var, s_rstd, s_ln, s_sc = (sem("f_" + x) for x in ("chain", "var", "rstd", "ln", "sc"))
            s_st = [sem(f"f_st{u}") for u in range(PAIR)]
            full = ROWS // P
            silu = work[:, 0, 0:INNER].rearrange("p (b c) -> p b c", b=2)
            prod = work[:, 0, INNER:2 * INNER]
            rnd = work[:, 1, 0:INNER]
            q2 = work[:, 1, INNER:INNER + INNER // 2].bitcast(BF16)
            q2T = qT[:, 0, 0:PAIR * INNER // 2].bitcast(BF16).rearrange("p (u k r) -> p u k r", u=PAIR, r=P)
            q1 = kT[:, 0, 0:PAIR * D // 2].bitcast(BF16).rearrange("p (u c) -> p u c", u=PAIR)
            q1T = kT[:, 0, PAIR * D // 2:PAIR * D].bitcast(BF16).rearrange("p (u c) -> p u c", u=PAIR)
            rnd1 = kT[:, 1, 0:D]
            res = kT[:, 1, D:3 * D].rearrange("p (u c) -> p u c", u=PAIR)
            am = kT[:, 1, 3 * D:3 * D + 16]
            sc1 = kT[:, 1, 3 * D + 16:3 * D + 20].rearrange("p (u c) -> p u c", u=PAIR)
            with nc.Block() as block:
                @block.gpsimd
                def _(pool):
                    raise_power(pool, s_var, s_rstd)

                @block.sync
                def _(sp):
                    def body(i):
                        for u in range(PAIR):
                            t = PAIR * i + u
                            sp.wait_ge(s["out"], t + 1)
                            sp.dma_start(out[bass.ds(P * t, P), :], res[:, u, :]).then_inc(s_st[u], 16)
                    body(0)
                    with sp.Fori(1, PASSES - 1) as i:
                        body(i)
                    for t in range(TILES - PAIR, TILES):
                        rows = min(P, ROWS - P * t)
                        sp.wait_ge(s["out"], t + 1)
                        sp.dma_start(out[P * t:P * t + rows, :], res[0:rows, t % PAIR, :]).then_inc(s_st[t % PAIR], 16)
                    for u in range(PAIR):
                        sp.wait_ge(s_st[u], 16 * PASSES)

                @block.scalar
                def _(act):
                    act.wait_ge(s_ln, 1)

                    def norm(t, u, first):
                        if not first:
                            act.wait_ge(s["q"], t - 1)
                        nc.scalar.activation(xn[:, u, :], col(t)(h), ACT.Identity, bias=shift[:, bass.ds(t, 1)],
                                             scale=rstd[:, bass.ds(t, 1)]).then_inc(s["xn"], 1)

                    def body(i):
                        first = is_first(i)
                        for u in range(PAIR):
                            norm(PAIR * i + u, u, first)
                        for u in range(PAIR):
                            t = PAIR * i + u
                            act.wait_ge(s["tq"], t + 1)
                            if not first:
                                act.wait_ge(s["u1"], t - 1)
                            src = bank[6 + u][:, :].bitcast(BF16)[:, 2 * D:3 * D]
                            nc.scalar.activation(q1T[:, u, :], src, ACT.Copy).then_inc(s["qT"], 1)
                        for u in range(PAIR):
                            t = PAIR * i + u
                            act.wait_ge(s_sc, t + 1)
                            for b in range(2):
                                act.wait_ge(s[f"g{b}"], t + 1)
                                if not (first and u == 0):
                                    act.wait_ge(s[f"p{b}"], t)
                                nc.scalar.activation(silu[:, b, :], bank[2 * b][:, :], ACT.Silu, scale=sc1[:, u, 0:1]).then_inc(s[f"sl{b}"], 1)
                            act.wait_ge(s["t2"], t + 1)
                            if not first:
                                act.wait_ge(s["dn"], t - 1)
                            src = bank[5][:, :].bitcast(BF16).rearrange("p (k r) -> p k r", r=P)
                            nc.scalar.activation(q2T[:, u], src, ACT.Copy).then_inc(s["q2T"], 1)
                    for_each(act, PASSES, body)

                @block.tensor
                def _(pe):
                    def down(t, u, first):
                        pe.wait_ge(s["q2T"], t + 1)
                        if not first:
                            pe.wait_ge(s["out"], t - 1)
                        for k in range(IB):
                            mm = nc.tensor.matmul(bank[6 + u][:, 0:D], q2T[:, u, k, :], ffn_down_q[:, k, :],
                                                  start=(k == 0), stop=(k == IB - 1))
                        mm.then_inc(s["dn"], 1)

                    def body(i):
                        first = is_first(i)
                        for u in range(PAIR):
                            t = PAIR * i + u
                            pe.wait_ge(s["q"], t + 1)
                            if not first:
                                pe.wait_ge(s["qT"], t - 1)
                            for k in range(KT):
                                mm = nc.tensor.transpose(bank[6 + u][:, :].bitcast(BF16)[:, 2 * D + P * k:2 * D + P * (k + 1)],
                                                         q1[:, u, P * k:P * (k + 1)], ident_bf[:, :])
                            mm.then_inc(s["tq"], 1)
                        for u in range(PAIR):
                            t = PAIR * i + u
                            pe.wait_ge(s["qT"], t + 1)
                            for b in range(2):
                                for half in range(2):
                                    if not (first and u == 0):
                                        pe.wait_ge(s[f"sl{b}" if half == 0 else f"p{b}"], t)
                                    w0 = INNER * half + BANK * b
                                    for k in range(KT):
                                        mm = nc.tensor.matmul(bank[2 * b + half][:, :], q1T[:, u, P * k:P * (k + 1)],
                                                              ffn_up_q[:, k, w0:w0 + BANK], start=(k == 0), stop=(k == KT - 1))
                                    mm.then_inc(s[f"{'gu'[half]}{b}"], 1)
                            pe.wait_ge(s["q2"], t + 1)
                            if not (first and u == 0):
                                pe.wait_ge(s["q2T"], t)
                            for k in range(IB):
                                mm = nc.tensor.transpose(bank[5][:, :].bitcast(BF16)[:, P * k:P * (k + 1)], q2[:, P * k:P * (k + 1)], ident_bf[:, :])
                            mm.then_inc(s["t2"], 1)
                            down(t, u, first)
                    for_each(pe, PASSES, body)

                @block.vector
                def _(dve):
                    chain = Chain(dve, s_chain)
                    finish_stats(dve, chain, s_var, s_rstd)
                    nc.vector.tensor_copy(am[:, 0:1], shift[:, 0:1]).then_inc(s_ln, 1)
                    base = chain.n
                    links = [0]
                    V = nc.vector

                    def body(i):
                        first = is_first(i)
                        chain.n = 0
                        chain.base = base + i * links[0]
                        for u in range(PAIR):
                            t = PAIR * i + u
                            dve.wait_ge(s["xn"], t + 1)
                            a = am[:, 4 * u:4 * u + 4]
                            chain.link(V.tensor_reduce(a[:, 0:1], xn[:, u, :], AX.X, ALU.max, apply_absolute_value=True))
                            chain.link(V.tensor_scalar(a[:, 0:1], a[:, 0:1], 1e-5, None, ALU.max))
                            V.reciprocal(a[:, 1:2], a[:, 0:1])
                            chain.link(V.tensor_scalar(a[:, 2:3], a[:, 0:1], 1.0 / 127.0, None, ALU.mult))
                            if not first:
                                dve.wait_ge(s["sl1"], t - 1)
                            V.tensor_scalar(sc1[:, u, :], w_scale[:, 0:2], a[:, 2:3], None, ALU.mult).then_inc(s_sc, 1)
                            chain.link(V.tensor_scalar(a[:, 1:2], a[:, 1:2], 127.0, None, ALU.mult))
                            chain.link(V.tensor_scalar(rnd1, xn[:, u, :], a[:, 1:2], ROUND, ALU.mult, ALU.add))
                            if not first:
                                dve.wait_ge(s["tq"], t - 1)
                            V.tensor_scalar(q1[:, u, :], rnd1, ROUND, 127.0, ALU.subtract, ALU.min).then_inc(s["q"], 1)
                        for u in range(PAIR):
                            t = PAIR * i + u
                            dve.wait_ge(s_sc, t + 1)
                            for b in range(2):
                                dve.wait_ge(s[f"sl{b}"], t + 1)
                                dve.wait_ge(s[f"u{b}"], t + 1)
                                V.scalar_tensor_tensor(prod[:, BANK * b:BANK * (b + 1)], bank[2 * b + 1][:, :], sc1[:, u, 1:2],
                                                       silu[:, b, :], ALU.mult, ALU.mult).then_inc(s[f"p{b}"], 1)
                            dve.wait_ge(s["p1"], t + 1)
                            a = am[:, 8 + 4 * u:12 + 4 * u]
                            chain.link(V.tensor_reduce(a[:, 0:1], prod, AX.X, ALU.max, apply_absolute_value=True))
                            chain.link(V.tensor_scalar(a[:, 0:1], a[:, 0:1], 1e-5, None, ALU.max))
                            chain.link(V.reciprocal(a[:, 1:2], a[:, 0:1]))
                            chain.link(V.tensor_scalar(a[:, 1:2], a[:, 1:2], 127.0, None, ALU.mult))
                            V.tensor_scalar(a[:, 2:3], a[:, 0:1], 1.0 / 127.0, w_scale[:, 2:3], ALU.mult, ALU.mult)
                            chain.link(V.tensor_scalar(rnd, prod, a[:, 1:2], ROUND, ALU.mult, ALU.add))
                            if not (first and u == 0):
                                dve.wait_ge(s["t2"], t)
                            V.tensor_scalar(q2, rnd, ROUND, 127.0, ALU.subtract, ALU.min).then_inc(s["q2"], 1)
                            dve.wait_ge(s["dn"], t + 1)
                            if not first:
                                dve.wait_ge(s_st[u], 16 * i)
                            V.scalar_tensor_tensor(res[:, u, :], bank[6 + u][:, 0:D], a[:, 2:3], col(t)(h), ALU.mult, ALU.add).then_inc(s["out"], 1)
                        links[0] = links[0] or chain.n
                    for_each(dve, PASSES, body)

        phases = [embed_phase, stats_phase, lambda: project_phase(0), lambda: attention_phase(0), lambda: output_phase(0),
                  route_phase, expert_phase, lambda: project_phase(1), lambda: attention_phase(1),
                  lambda: output_phase(1), ffn_phase]
        for phase in phases:
            with nc.cleanup_on_exit():
                phase()


def _tables():
    angle_of = 1.0 / 10000.0 ** (np.arange(0, DH, 2, dtype=np.float32) / np.float32(DH))
    pos = np.arange(PADDED) % SEQ
    freqs = pos.astype(np.float32)[:, None] * angle_of.astype(np.float32)[None, :]
    ang = np.concatenate((freqs, freqs), axis=-1)[:, ::2]
    c, s = np.cos(ang), np.sin(ang)
    cos = np.repeat(c, 2, axis=1)
    sin = np.stack((-s, s), axis=-1).reshape(PADDED, DH)
    quarter = np.float32(1.0 / DH ** 0.5)
    cos = np.concatenate((cos * quarter, cos), axis=1).astype(np.float32)
    sin = np.concatenate((sin * quarter, sin), axis=1).astype(np.float32)
    mask = (np.arange(P)[:, None] // DH == np.arange(HH)[None, :]).astype(np.float32)
    rem = (np.arange(HR)[:, None] // REM == np.arange(HH)[None, :]).astype(np.float32)
    iota = np.tile(np.arange(EXPERTS, dtype=np.float32), (P, 1))
    return {"rope_cos": cos, "rope_sin": sin, "head_mask": mask, "rem_mask": rem, "ident_in": np.eye(P, dtype=np.float32), "iota_in": iota}


def _layout(i):
    i = {k: np.asarray(v) for k, v in i.items()}
    x = i["x"].reshape(IMAGES, 3, 8, 16, 8, 16)
    gu = np.concatenate([
        np.concatenate((i["L0_ffn_gate_proj"], i["L0_ffn_shared_gate_w"][None]), axis=0),
        np.concatenate((i["L0_ffn_up_proj"], i["L0_ffn_shared_up_w"][None]), axis=0)], axis=1)
    down = np.concatenate((i["L0_ffn_down_proj"], i["L0_ffn_shared_down_w"][None]), axis=0)
    arrays = {
        "patches_t": x.transpose(3, 5, 1, 0, 2, 4).reshape(768, IMAGES * PATCHES),
        "txt": i["txt"],
        "w_emb_t": i["L0_tok_W"].T,
        "b_emb": i["L0_tok_b"],
        "w_qkv": np.concatenate((i["L0_attn_Wq"], i["L0_attn_Wk"], i["L0_attn_Wv"]), axis=1),
        "b_qkv": np.concatenate((i["L0_attn_bq"], i["L0_attn_bk"], i["L0_attn_bv"])),
        "w_o0": i["L0_attn_Wo"],
        "b_o0": i["L0_attn_bo"],
        "w_gate_t": i["L0_ffn_gate_w"].T,
        "e_bias": i["L0_ffn_e_bias"],
        "w_gu_t": gu.transpose(2, 0, 1),
        "w_down_t": down.transpose(2, 0, 1),
        "w_v1_t": i["L1_attn_Wv"].T,
        "b_v1": i["L1_attn_bv"],
        "w_o1_t": i["L1_attn_Wo"].T,
        "b_o1": i["L1_attn_bo"],
        "ffn_up_t": np.concatenate((i["L1_ffn_w_gate"], i["L1_ffn_w_up"]), axis=0).T,
        "ffn_down_t": i["L1_ffn_w_down"].T,
    }
    arrays.update(_tables())
    return {k: np.ascontiguousarray(v) for k, v in arrays.items()}


def build(nc, arrays):
    args = [nc.dram_tensor(f"in_{k}_dram", v.shape, mybir.dt.from_np(v.dtype), kind="ExternalInput").ap() for k, v in arrays.items()]
    out = nc.dram_tensor("out_0_dram", (ROWS, D), F32, kind="ExternalOutput").ap()
    fusion_kernel(nc, *args, out)


def kernel(**inputs):
    import concourse.bacc as _bacc
    from concourse.bass_utils import run_bass_kernel_spmd as _run

    nc = _bacc.Bacc("TRN2", target_bir_lowering=False, num_devices=1)
    arrays = _layout(inputs)
    build(nc, arrays)
    r = _run(nc, [{f"in_{k}_dram": v for k, v in arrays.items()}], core_ids=[0])
    return r.results[0]["out_0_dram"].reshape(IMAGES, SEQ, D)
```

```python
from contextlib import ExitStack

import numpy as np

import concourse.bass as bass
from concourse import mybir

ALU = mybir.AluOpType
ACT = mybir.ActivationFunctionType
AX = mybir.AxisListType
F32 = mybir.dt.float32
BF16 = mybir.dt.bfloat16
F16 = mybir.dt.float16
U32 = mybir.dt.uint32

P = 128
D = 256
KT = D // P
IMAGES = 16
PATCHES = 64
TEXT = 77
SEQ = PATCHES + TEXT
ROWS = IMAGES * SEQ
TILES = -(-ROWS // P)
PADDED = TILES * P
EMB_K = 768 // P
EMB_TILES = IMAGES * PATCHES // P
PAIR = 2
PASSES = TILES // PAIR
HEADS = 16
DH = D // HEADS
HH = HEADS // KT
REM = SEQ - P
HR = HH * REM
VC = 3 * DH + 1
SLOTS = HEADS + KT
SGROUPS = SLOTS // 3
TGROUPS = 6
EXPERTS = 16
BRANCHES = EXPERTS + 1
INTER = 128
GROUPS = 4
TOPK = 4
CHUNK = 3 * P
CHUNKS = PADDED // CHUNK
INNER = 1024
IB = INNER // P
BANK = 512
ROUND = 12582912.0
LN_EPS = 1e-5
LOWEST = -3.0e38


def for_each(eng, count, body):
    body(0)
    with eng.Fori(1, count) as i:
        body(i)


def steps(eng, step, peeled, lag):
    for tau in range(PAIR * peeled):
        step(tau, tau % PAIR)
    if peeled < PASSES:
        with eng.Fori(peeled, PASSES) as i:
            for u in range(PAIR):
                step(PAIR * i + u, u)
    for tau in range(TILES, TILES + lag):
        step(tau, tau % PAIR)


def exists(t):
    return not isinstance(t, int) or 0 <= t < TILES


def reuses(t, slots=PAIR):
    return not isinstance(t, int) or t >= slots


def is_first(i):
    return isinstance(i, int) and i == 0


class Chain:

    def __init__(self, eng, semaphore):
        self.eng, self.semaphore, self.base, self.n, self.per_pass = eng, semaphore, 0, 0, 0

    def at(self, i):
        if not is_first(i):
            self.per_pass = self.per_pass or self.n
            self.base = i * self.per_pass
        self.n = 0

    def link(self, instruction):
        instruction.then_inc(self.semaphore, 1)
        self.n += 1
        self.eng.wait_ge(self.semaphore, self.base + self.n)


def fusion_kernel(nc, patches_t, txt, w_emb_t, b_emb, w_qkv, b_qkv, w_o0, b_o0, w_gate_t, e_bias,
                  w_gu_t, w_down_t, w_v1_t, b_v1, w_o1_t, b_o1, ffn_up_t, ffn_down_t,
                  rope_cos, rope_sin, head_mask, rem_mask, ident_in, iota_in, out):
    ctx = ExitStack()
    with ctx:
        def sb(name, shape, dt=F32):
            return ctx.enter_context(nc.sbuf_tensor(name, shape, dt))

        def sem(name):
            return nc.alloc_semaphore(name=name)

        def dram(name, shape, dt=F32):
            return nc.dram_tensor(name, shape, dt, kind="Internal").ap()

        h0_dram = dram("h0_dram", [PADDED, D])
        v_dram = dram("v_dram", [PADDED, HEADS * VC], BF16)
        o_dram = dram("o_dram", [PADDED, D])

        h = sb("h", [P, TILES, D])
        qT = sb("qT", [P, KT, PADDED])
        kT = sb("kT", [P, KT, PADDED])
        stats = sb("stats", [P, TILES, 6])
        mean_var = sb("mean_var", [P, TILES, 2])
        rstd = sb("rstd", [P, TILES])
        shift = sb("shift", [P, TILES])
        expo = sb("expo", [P, TILES])
        ident = sb("ident", [P, P])
        ident_bf = sb("ident_bf", [P, P], BF16)
        iota = sb("iota", [P, EXPERTS])
        ones = sb("ones", [P, P])
        carrier = sb("carrier", [P, 4])

        wqkv_sb = sb("wqkv_sb", [P, KT, 3 * D])
        wo_sb = [sb(f"wo{n}_sb", [P, KT, D]) for n in range(2)]
        wv1_sb = sb("wv1_sb", [P, KT, D])
        wgate_sb = sb("wgate_sb", [P, KT, EXPERTS])
        bqkv_sb = sb("bqkv_sb", [P, 3 * D])
        bo_sb = [sb(f"bo{n}_sb", [P, D]) for n in range(2)]
        bv1_sb = sb("bv1_sb", [P, D])
        bemb_sb = sb("bemb_sb", [P, D])
        ebias_sb = sb("ebias_sb", [P, EXPERTS])
        ffn_up_q = sb("ffn_up_q", [P, KT, 2 * INNER], BF16)
        ffn_down_q = sb("ffn_down_q", [P, IB, D], BF16)
        w_scale = sb("w_scale", [P, 3])
        cos_sb = sb("cos_sb", [P, TILES, 2 * DH])
        sin_sb = sb("sin_sb", [P, TILES, 2 * DH])
        mask_sb = sb("mask_sb", [P, HH])
        rmask_sb = sb("rmask_sb", [HR, HH])
        rmask_bf = sb("rmask_bf", [HR, HH], BF16)

        s_moe = nc.alloc_semaphore(name="moe")

        xn = sb("xn", [P, PAIR, D])
        xT = sb("xT", [P, PAIR, D])
        work = sb("work", [P, PAIR, 2 * INNER])

        moe_up = BRANCHES * 2 * INTER
        region = sb("region", [P, 18600])
        used = [0]

        def piece(n, dt=F32):
            words = n if dt == F32 else n // 2
            a = used[0]
            used[0] += words
            v = region[:, a:a + words]
            return v if dt == F32 else v.bitcast(dt)

        q_masked = piece(PAIR * KT * HH * P).rearrange("p (s t h q) -> p s t h q", s=PAIR, t=KT, h=HH)
        q_rem = piece(PAIR * KT * P).rearrange("p (s t q) -> p s t q", s=PAIR, t=KT)
        prob = piece(PAIR * SLOTS * SEQ).rearrange("p (s n k) -> p s n k", s=PAIR, n=SLOTS)
        pT = piece(2 * HEADS * P, F16).rearrange("p (a h q) -> p a h q", a=2, h=HEADS)
        pT_rem = piece(2 * 2 * KT * P, F16).rearrange("p (a n q) -> p a n q", a=2, n=2 * KT)
        pT_corner = piece(KT * P, F16).rearrange("p (t q) -> p t q", t=KT)
        v_main = piece(PAIR * HEADS * VC, BF16).rearrange("p (s c) -> p s c", s=PAIR)
        v_rem = piece(PAIR * HEADS * VC, BF16).rearrange("p (s c) -> p s c", s=PAIR)
        v_rep = piece(PAIR * HEADS * VC, BF16).rearrange("p (s c) -> p s c", s=PAIR)
        v_diag = piece(PAIR * HEADS * VC, BF16).rearrange("p (s c) -> p s c", s=PAIR)
        prob_last = piece(PAIR * HEADS * REM).rearrange("p (s c) -> p s c", s=PAIR)
        neg_max = piece(PAIR * SLOTS).rearrange("p (s n) -> p s n", s=PAIR)
        o_sum = piece(D)
        o_den = piece(HEADS)
        o_out = piece(PAIR * D).rearrange("p (s c) -> p s c", s=PAIR)
        r_raw = piece(HEADS * VC)
        r_sum = piece(D)
        r_den = piece(HEADS)
        r_out = piece(PAIR * D).rearrange("p (s c) -> p s c", s=PAIR)
        assert used[0] <= 18600 and KT * moe_up + BRANCHES * D <= 18600
        gu_sb = region[:, 0:KT * moe_up].rearrange("p (t e c) -> p t e c", t=KT, e=BRANCHES)
        down_sb = region[:, KT * moe_up:KT * moe_up + BRANCHES * D].rearrange("p (e c) -> p e c", e=BRANCHES)
        ffn_raw = region[:, 0:KT * 2 * INNER + IB * D]

        bank = [ctx.enter_context(nc.psum_tensor(f"bank{n}", [P, BANK], F32)) for n in range(8)]

        def col(t, n=1):
            return lambda x: x[:, bass.ds(t, 1), :].rearrange("p a c -> p (a c)")

        def tile_cols(x, t):
            return x[:, :, bass.ds(P * t, P)]

        def embed_phase():
            s_const = sem("e_const")
            s_late = sem("e_late")
            s_raw = sem("e_raw")
            s_patch = [sem(f"e_patch{u}") for u in range(PAIR)]
            s_mm = sem("e_mm")
            s_add = sem("e_add")
            s_st = [sem(f"e_st{u}") for u in range(PAIR)]
            s_zero = sem("e_zero")
            s_pad = sem("e_pad")
            s_ones = sem("e_ones")
            s_chain = sem("e_chain")
            s_sum = sem("e_sum")
            s_tot = sem("e_tot")
            s_h = sem("e_h")
            s_id = sem("e_id")
            w_emb = work[:, 0, 0:EMB_K * D].rearrange("p (k c) -> p k c", k=EMB_K)
            patch = [xT_patch[:, u] for u in range(PAIR)]
            abs_sum = stats[:, 0, 0:3]
            zero = v_zero
            n_const = 7
            with nc.Block() as block:
                @block.sync
                def _(sp):
                    sp.dma_start(w_emb, w_emb_t.rearrange("(k p) c -> p k c", p=P)).then_inc(s_const, 16)
                    sp.dma_start(bemb_sb[:, :], b_emb.rearrange("(a c) -> a c", a=1).broadcast_to([P, D])).then_inc(s_const, 16)
                    sp.dma_start(ident[:, :], ident_in).then_inc(s_const, 16)
                    sp.dma_start(iota[:, :], iota_in).then_inc(s_const, 16)
                    sp.dma_start(mask_sb[:, :], head_mask).then_inc(s_const, 16)
                    sp.dma_start(rmask_sb[:, :], rem_mask).then_inc(s_const, 16)
                    sp.dma_start(ebias_sb[:, :], e_bias.rearrange("(a c) -> a c", a=1).broadcast_to([P, EXPERTS])).then_inc(s_const, 16)

                    def body(i):
                        for u in range(PAIR):
                            t = PAIR * i + u
                            if not is_first(i):
                                sp.wait_ge(s_mm, t - 1)
                            sp.dma_start(patch[u], patches_t.rearrange("(k p) r -> p k r", p=P)[:, :, bass.ds(P * t, P)]).then_inc(s_patch[u], 16)
                        for u in range(PAIR):
                            t = PAIR * i + u
                            sp.wait_ge(s_add, t + 1)
                            for j in range(2):
                                dst = h0_dram[bass.ds(SEQ * (2 * t + j), PATCHES), :]
                                sp.dma_start(dst, xn[PATCHES * j:PATCHES * (j + 1), u, :]).then_inc(s_st[u], 16)
                    for_each(sp, EMB_TILES // PAIR, body)
                    for u in range(PAIR):
                        sp.wait_ge(s_st[u], 16 * 2 * EMB_TILES // PAIR)
                    sp.wait_ge(s_pad, 16 * 3)
                    sp.dma_start(h[:, :, :], h0_dram.rearrange("(t p) c -> p t c", p=P)).then_inc(s_h, 16)
                    sp.wait_ge(s_h, 16)

                @block.gpsimd
                def _(pool):
                    pool.memset(zero, 0.0).then_inc(s_zero, 1)
                    pool.memset(ones[:, :], 1.0).then_inc(s_ones, 1)
                    pool.memset(expo[:, :], -0.5).then_inc(s_ones, 1)
                    pool.wait_ge(s_zero, 1)
                    pad = PADDED - ROWS
                    pool.dma_start(h0_dram[ROWS:PADDED, :], zero[0:pad, :]).then_inc(s_pad, 16)
                    pool.dma_start(o_dram[ROWS:PADDED, :], zero[0:pad, :]).then_inc(s_pad, 16)
                    rows = h0_dram[0:ROWS, :].rearrange("(b s) c -> b s c", s=SEQ)
                    pool.dma_start(rows[:, PATCHES:SEQ, :], txt).then_inc(s_pad, 16)
                    pool.wait_ge(s_pad, 16 * 3)
                    pool.wait_ge(s_ones, 2)

                @block.scalar
                def _(act):
                    def up(dst, src):
                        act.dma_start(dst, src).then_inc(s_late, 16)
                    raw_up = ffn_raw[:, 0:KT * 2 * INNER].rearrange("p (k c) -> p k c", k=KT)
                    raw_down = ffn_raw[:, KT * 2 * INNER:].rearrange("p (k c) -> p k c", k=IB)
                    act.dma_start(raw_up, ffn_up_t.rearrange("(k p) c -> p k c", p=P)).then_inc(s_raw, 16)
                    act.dma_start(raw_down, ffn_down_t.rearrange("(k p) c -> p k c", p=P)).then_inc(s_raw, 16)
                    up(wqkv_sb[:, :, :], w_qkv.rearrange("(k p) c -> p k c", p=P))
                    up(bqkv_sb[:, :], b_qkv.rearrange("(a c) -> a c", a=1).broadcast_to([P, 3 * D]))
                    up(cos_sb[:, :, :], rope_cos.rearrange("(t p) c -> p t c", p=P))
                    up(sin_sb[:, :, :], rope_sin.rearrange("(t p) c -> p t c", p=P))
                    for n, (w, b) in enumerate(((w_o0, b_o0), (w_o1_t, b_o1))):
                        up(wo_sb[n][:, :, :], w.rearrange("(k p) c -> p k c", p=P))
                        up(bo_sb[n][:, :], b.rearrange("(a c) -> a c", a=1).broadcast_to([P, D]))
                    up(wv1_sb[:, :, :], w_v1_t.rearrange("(k p) c -> p k c", p=P))
                    up(bv1_sb[:, :], b_v1.rearrange("(a c) -> a c", a=1).broadcast_to([P, D]))
                    up(wgate_sb[:, :, :], w_gate_t.rearrange("(k p) c -> p k c", p=P))
                    act.wait_ge(s_const, 16 * n_const)
                    act.activation(ident_bf[:, :], ident[:, :], ACT.Copy).then_inc(s_id, 1)
                    act.activation(rmask_bf[:, :], rmask_sb[:, :], ACT.Copy).then_inc(s_id, 1)
                    act.wait_ge(s_id, 2)
                    act.wait_ge(s_late, 16 * 11)

                @block.tensor
                def _(pe):
                    pe.wait_ge(s_const, 16 * n_const)

                    def body(i):
                        for u in range(PAIR):
                            t = PAIR * i + u
                            pe.wait_ge(s_patch[u], 16 * i + 16)
                            if not is_first(i):
                                pe.wait_ge(s_add, t - 1)
                            for k in range(EMB_K):
                                mm = nc.tensor.matmul(bank[u][:, 0:D], patch[u][:, k, :], w_emb[:, k, :],
                                                      start=(k == 0), stop=(k == EMB_K - 1))
                            mm.then_inc(s_mm, 1)
                    for_each(pe, EMB_TILES // PAIR, body)
                    pe.wait_ge(s_ones, 2)
                    pe.wait_ge(s_sum, 1)
                    nc.tensor.matmul(bank[2][:, 0:3], ones[:, :], abs_sum, start=True, stop=True).then_inc(s_tot, 1)

                @block.vector
                def _(dve):
                    dve.wait_ge(s_const, 16 * n_const)

                    def body(i):
                        for u in range(PAIR):
                            t = PAIR * i + u
                            dve.wait_ge(s_mm, t + 1)
                            if not is_first(i):
                                dve.wait_ge(s_st[u], 32 * i)
                            nc.vector.tensor_tensor(xn[:, u, :], bank[u][:, 0:D], bemb_sb[:, :], ALU.add).then_inc(s_add, 1)
                    for_each(dve, EMB_TILES // PAIR, body)

                    chain = Chain(dve, s_chain)
                    dve.wait_ge(s_raw, 32)
                    up = KT * 2 * INNER
                    both = ffn_raw[:, 0:up].rearrange("p (k g c) -> p g k c", k=KT, g=2)
                    for g in range(2):
                        ins = nc.vector.tensor_reduce(abs_sum[:, g:g + 1], both[:, g], AX.XY, ALU.add, apply_absolute_value=True)
                    ins = nc.vector.tensor_reduce(abs_sum[:, 2:3], ffn_raw[:, up:], AX.X, ALU.add, apply_absolute_value=True)
                    ins.then_inc(s_sum, 1)
                    dve.wait_ge(s_tot, 1)
                    chain.link(nc.vector.tensor_scalar(w_scale[:, :], bank[2][:, 0:3], 1.0 / (D * INNER), 1e-5, ALU.mult, ALU.max))
                    inverse = stats[:, 1, 0:3]
                    chain.link(nc.vector.reciprocal(inverse, w_scale[:, :]))
                    quant = ffn_up_q[:, :, :].rearrange("p k (g c) -> p g k c", g=2)
                    parts = [(both[:, 0], quant[:, 0]), (both[:, 1], quant[:, 1]),
                             (ffn_raw[:, up:], ffn_down_q[:, :, :].rearrange("p k c -> p (k c)"))]
                    for g, (raw, q) in enumerate(parts):
                        chain.link(nc.vector.tensor_scalar(raw, raw, inverse[:, g:g + 1], ROUND, ALU.mult, ALU.add))
                        chain.link(nc.vector.tensor_scalar(raw, raw, ROUND, 1.0, ALU.subtract, ALU.min))
                        chain.link(nc.vector.tensor_scalar(q, raw, -1.0, None, ALU.max))

        xT_patch = qT[:, :, 0:PAIR * EMB_K * P // KT].rearrange("p k (a r) -> p k a r", r=P)
        v_zero = kT[:, 0, 0:D]
        v_all = region[:, 0:TILES * HEADS * VC // 2].bitcast(BF16).rearrange("p (t c) -> p t c", t=TILES)

        def carry(k=0):
            nc.vector.tensor_copy(carrier[:, k:k + 1], ones[:, 0:1])

        def means(dve, slot, n, ready, count, done):
            dve.wait_ge(ready, count)
            carry(3)
            for j in range(slot, slot + n):
                last = nc.vector.bn_aggr(mean_var[:, j, :], stats[:, j, :])
            last.then_inc(done, 1)

        def variances(dve, t, slot, n, ready, count, done):
            dve.wait_ge(ready, count)
            nc.vector.tensor_scalar(rstd[:, bass.ds(t, n)], mean_var[:, slot:slot + n, 1], LN_EPS, None, ALU.add).then_inc(done, 1)

        def raise_power(pool, t, n, ready, count, done):
            pool.wait_ge(ready, count)
            r = rstd[:, bass.ds(t, n)]
            nc.gpsimd.tensor_tensor(r, r, expo[:, 0:n], ALU.pow).then_inc(done, 1)

        def shifts(dve, t, slot, n, ready, count, done):
            dve.wait_ge(ready, count)
            nc.vector.scalar_tensor_tensor(shift[:, bass.ds(t, n)], mean_var[:, slot:slot + n, 0], -1.0, rstd[:, bass.ds(t, n)],
                                           ALU.mult, ALU.mult).then_inc(done, 1)

        def stats_phase():
            s_st, s_mv, s_var, s_rstd, s_shift = (sem("st_" + x) for x in ("stats", "mv", "var", "rstd", "shift"))
            with nc.Block() as block:
                @block.vector
                def _(dve):
                    for t in range(TILES):
                        nc.vector.bn_stats(stats[:, t, :], h[:, t, :]).then_inc(s_st, 1)
                    means(dve, 0, TILES, s_st, TILES, s_mv)
                    variances(dve, 0, 0, TILES, s_mv, 1, s_var)
                    shifts(dve, 0, 0, TILES, s_rstd, 1, s_shift)
                    dve.wait_ge(s_shift, 1)

                @block.gpsimd
                def _(pool):
                    raise_power(pool, 0, TILES, s_var, 1, s_rstd)

        def project_phase(layer):
            n = f"p{layer}_"
            s_xn, s_tx, s_xT = sem(n + "xn"), sem(n + "tx"), sem(n + "xT")
            s_qk, s_v = sem(n + "qk"), sem(n + "v")
            s_qkb, s_vb = sem(n + "qkb"), sem(n + "vb")
            s_cos, s_sin, s_rot = sem(n + "cos"), sem(n + "sin"), sem(n + "rot")
            s_tq, s_qT = sem(n + "tq"), sem(n + "qT")
            s_v0, s_r1, s_v1, s_v2 = sem(n + "v0"), sem(n + "r1"), sem(n + "v1"), sem(n + "v2")
            s_one, s_st = sem(n + "one"), sem(n + "st")
            qk_cols = 2 * D if layer == 0 else 0
            qk = work[:, :, 0:2 * D]
            qk_cos = work[:, :, 2 * D:4 * D]
            qk_rot = work[:, :, 4 * D:6 * D]
            v = work[:, :, 6 * D:7 * D]
            v_res = work[:, :, 7 * D:8 * D]
            w = wqkv_sb if layer == 0 else wv1_sb
            bias = bqkv_sb if layer == 0 else bv1_sb
            turned = qk_rot if layer == 0 else v
            turns = 4 if layer == 0 else 2
            s_turned = s_rot if layer == 0 else s_vb

            def v_parts(t):
                return col(t)(v_all).rearrange("p (h c) -> p h c", c=VC)
            PRODUCT, ROTATE, TURN = 2, 3, 4
            PEELED = 3

            def heads(x):
                return x.rearrange("p (h c) -> p h c", c=DH)

            with nc.Block() as block:
                @block.gpsimd
                def _(pool):
                    columns = v_all.rearrange("p t (h c) -> p (t h) c", c=VC)
                    pool.memset(columns[:, :, VC - 1:VC], 1.0).then_inc(s_one, 1)

                    def step(tau, u):
                        t = tau - ROTATE
                        if exists(t):
                            if layer == 0:
                                pool.wait_ge(s_qkb, t + 1)
                                if reuses(t):
                                    pool.wait_ge(s_rot, t - 1)
                                x = qk[:, 1 - u, :].rearrange("p (a h c) -> p a h c", a=2, c=DH)
                                o = qk_cos[:, 1 - u, :].rearrange("p (a h c) -> p a h c", a=2, c=DH)
                                c = cos_sb[:, bass.ds(t, 1), :].rearrange("p x (a c) -> p (x a) c", a=2)
                                c = c.unsqueeze(2).broadcast_to([P, 2, HEADS, DH])
                                nc.gpsimd.tensor_tensor(o, x, c, ALU.mult).then_inc(s_cos, 1)
                            pool.wait_ge(s_v0, t + 1)
                            if reuses(t):
                                pool.wait_ge(s_v2, t - 1)
                            nc.gpsimd.tensor_tensor(heads(v_res[:, 1 - u, :]), heads(v[:, 1 - u, :]), v_parts(t)[:, :, 0:DH],
                                                    ALU.subtract).then_inc(s_r1, 1)
                        t = tau - TURN
                        if exists(t):
                            pool.wait_ge(s_v1, t + 1)
                            nc.gpsimd.tensor_tensor(v_parts(t)[:, :, 2 * DH:3 * DH], heads(v_res[:, u, :]),
                                                    v_parts(t)[:, :, DH:2 * DH], ALU.subtract).then_inc(s_v2, 1)
                    steps(pool, step, PEELED, TURN)

                @block.scalar
                def _(act):
                    def step(tau, u):
                        t = tau
                        if exists(t):
                            if reuses(t):
                                act.wait_ge(s_tx, t - 1)
                            nc.scalar.activation(xn[:, u, :], col(t)(h), ACT.Identity, bias=shift[:, bass.ds(t, 1)],
                                                 scale=rstd[:, bass.ds(t, 1)]).then_inc(s_xn, 1)
                        t = tau - 1
                        if exists(t):
                            act.wait_ge(s_tx, t + 1)
                            if reuses(t):
                                act.wait_ge(s_v, t - 1)
                            nc.scalar.activation(xT[:, 1 - u, :], bank[1 - u][:, 0:D], ACT.Copy).then_inc(s_xT, 1)
                        t = tau - ROTATE
                        if exists(t):
                            act.wait_ge(s_vb, t + 1)
                            nc.scalar.activation(v_parts(t)[:, :, 0:DH], heads(v[:, 1 - u, :]), ACT.Copy).then_inc(s_v0, 1)
                        t = tau - TURN
                        if exists(t):
                            act.wait_ge(s_r1, t + 1)
                            nc.scalar.activation(v_parts(t)[:, :, DH:2 * DH], heads(v_res[:, u, :]), ACT.Copy).then_inc(s_v1, 1)
                            act.wait_ge(s_tq, t + 1)
                            src = bank[6 + u][:, 0:turns * P].rearrange("p (k q) -> p k q", q=P)
                            if layer == 0:
                                nc.scalar.activation(tile_cols(qT, t), src[:, 0:KT], ACT.Copy)
                                nc.scalar.activation(tile_cols(kT, t), src[:, KT:2 * KT], ACT.Copy).then_inc(s_qT, 1)
                            else:
                                nc.scalar.activation(tile_cols(qT, t), src, ACT.Copy, scale=0.5).then_inc(s_qT, 1)
                    steps(act, step, PEELED, TURN)

                @block.tensor
                def _(pe):
                    def step(tau, u):
                        t = tau - 1
                        if exists(t):
                            pe.wait_ge(s_xn, t + 1)
                            if reuses(t):
                                pe.wait_ge(s_xT, t - 1)
                            for k in range(KT):
                                mm = nc.tensor.transpose(bank[1 - u][:, P * k:P * (k + 1)], xn[:, 1 - u, P * k:P * (k + 1)], ident[:, :])
                            mm.then_inc(s_tx, 1)
                        t = tau - PRODUCT
                        if exists(t):
                            pe.wait_ge(s_xT, t + 1)
                            if layer == 0:
                                if reuses(t):
                                    pe.wait_ge(s_qkb, t - 1)
                                for k in range(KT):
                                    mm = nc.tensor.matmul(bank[4 + u][:, :], xT[:, u, P * k:P * (k + 1)], w[:, k, 0:2 * D],
                                                          start=(k == 0), stop=(k == KT - 1))
                                mm.then_inc(s_qk, 1)
                            if reuses(t):
                                pe.wait_ge(s_vb, t - 1)
                            for k in range(KT):
                                mm = nc.tensor.matmul(bank[2 + u][:, 0:D], xT[:, u, P * k:P * (k + 1)], w[:, k, qk_cols:qk_cols + D],
                                                      start=(k == 0), stop=(k == KT - 1))
                            mm.then_inc(s_v, 1)
                        t = tau - TURN
                        if exists(t):
                            pe.wait_ge(s_turned, t + 1)
                            if reuses(t):
                                pe.wait_ge(s_qT, t - 1)
                            for k in range(turns):
                                mm = nc.tensor.transpose(bank[6 + u][:, P * k:P * (k + 1)], turned[:, u, P * k:P * (k + 1)], ident[:, :])
                            mm.then_inc(s_tq, 1)
                    steps(pe, step, PEELED, TURN)

                @block.vector
                def _(dve):
                    def step(tau, u):
                        t = tau - ROTATE
                        if exists(t) and layer == 0:
                            dve.wait_ge(s_qkb, t + 1)
                            if reuses(t):
                                dve.wait_ge(s_tq, t - 1)
                            x = qk[:, 1 - u, :].rearrange("p (a h j w) -> p a h j w", a=2, h=HEADS, w=2)
                            o = qk_rot[:, 1 - u, :].rearrange("p (a h j w) -> p a h j w", a=2, h=HEADS, w=2)
                            s = sin_sb[:, bass.ds(t, 1), :].rearrange("p x (a j w) -> p (x a) j w", a=2, w=2)
                            for a in range(2):
                                for w2 in range(2):
                                    sw = s[:, a, :, w2].unsqueeze(1).broadcast_to([P, HEADS, DH // 2])
                                    last = nc.vector.tensor_tensor(o[:, a, :, :, w2], x[:, a, :, :, 1 - w2], sw, ALU.mult)
                            last.then_inc(s_sin, 1)
                            dve.wait_ge(s_sin, t + 1)
                            dve.wait_ge(s_cos, t + 1)
                            nc.vector.tensor_tensor(qk_rot[:, 1 - u, :], qk_rot[:, 1 - u, :], qk_cos[:, 1 - u, :], ALU.add).then_inc(s_rot, 1)
                        t = tau - PRODUCT
                        if exists(t):
                            if layer == 0:
                                dve.wait_ge(s_qk, t + 1)
                                if reuses(t):
                                    dve.wait_ge(s_cos, t - 1)
                                nc.vector.tensor_tensor(qk[:, u, :], bank[4 + u][:, :], bias[:, 0:2 * D], ALU.add).then_inc(s_qkb, 1)
                            dve.wait_ge(s_v, t + 1)
                            if reuses(t):
                                dve.wait_ge(s_r1, t - 1)
                                if layer == 1:
                                    dve.wait_ge(s_tq, t - 1)
                            nc.vector.tensor_tensor(v[:, u, :], bank[2 + u][:, 0:D], bias[:, qk_cols:qk_cols + D], ALU.add).then_inc(s_vb, 1)
                    steps(dve, step, PEELED, TURN)

                @block.sync
                def _(sp):
                    sp.wait_ge(s_one, 1)

                    def body(i):
                        sp.wait_ge(s_v2, PAIR * i + PAIR)
                        dst = v_dram[bass.ds(PAIR * P * i, PAIR * P), :].rearrange("(u p) c -> p u c", p=P)
                        sp.dma_start(dst, v_all[:, bass.ds(PAIR * i, PAIR), :]).then_inc(s_st, 16)
                    for_each(sp, PASSES, body)
                    sp.wait_ge(s_st, 16 * PASSES)

        def attention_phase(layer):
            n = f"a{layer}_"
            keys = kT if layer == 0 else qT
            s_zero = sem(n + "zero")
            s_ld = [sem(n + f"ld{u}") for u in range(PAIR)]
            s_qm = sem(n + "qm")
            s_s = sem(n + "s")
            s_max = sem(n + "max")
            s_exp = sem(n + "exp")
            s_t = sem(n + "t")
            s_hi, s_lo = sem(n + "hi"), sem(n + "lo")
            s_pl = sem(n + "pl")
            s_vd = sem(n + "vd")
            s_o, s_oe = sem(n + "o"), sem(n + "oe")
            s_r, s_rc = sem(n + "r"), sem(n + "rc")
            s_rs, s_rd, s_ro = sem(n + "rs"), sem(n + "rd"), sem(n + "ro")
            s_oo = sem(n + "oo")
            s_chain, s_pchain = sem(n + "chain"), sem(n + "pchain")
            s_st = [sem(n + f"st{u}") for u in range(PAIR)]
            passes = IMAGES // PAIR
            LOADS = 4
            hc = HH * VC
            turn_needs = [2, 3, 4, 6, 6, 6]

            def o_rows(b, lo, count):
                if layer == 0:
                    return o_dram[bass.ds(SEQ * b + lo, count), :]
                flat = o_dram[bass.ds(SEQ * b, SEQ), :].rearrange("s c -> (s c)")
                return flat.rearrange("(h s d) -> s h d", h=HEADS, d=DH)[lo:lo + count]

            with nc.Block() as block:
                @block.sync
                def _(sp):
                    def load(b, u):
                        rows, rem = v_dram[bass.ds(SEQ * b, P), :], v_dram[bass.ds(SEQ * b + P, REM), :]
                        sp.dma_start(v_main[:, u, :], rows).then_inc(s_ld[u], 16)
                        sp.dma_start(v_rem[0:REM, u, :], rem).then_inc(s_ld[u], 16)
                        sp.dma_start(v_rem[32:32 + REM, u, :], rem).then_inc(s_ld[u], 16)
                        sp.dma_start(v_rep[0:HR, u, :], rem.unsqueeze(0).broadcast_to([HH, REM, HEADS * VC])).then_inc(s_ld[u], 16)

                    def store(b, u):
                        sp.wait_ge(s_oo, b + 1)
                        src, rsrc = o_out[:, u, :], r_out[0:REM, u, :]
                        if layer == 1:
                            src, rsrc = (x.rearrange("p (h d) -> p h d", d=DH) for x in (src, rsrc))
                        sp.dma_start(o_rows(b, 0, P), src).then_inc(s_st[u], 16)
                        sp.wait_ge(s_ro, b + 1)
                        sp.dma_start(o_rows(b, P, REM), rsrc).then_inc(s_st[u], 16)

                    sp.wait_ge(s_zero, 3)
                    for u in range(PAIR):
                        load(u, u)

                    def body(i, last=False):
                        for u in range(PAIR):
                            b = PAIR * i + u
                            sp.wait_ge(s_r, b + 1)
                            if not last:
                                load(b + PAIR, u)
                            store(b, u)
                    body(0)
                    with sp.Fori(1, passes - 1) as i:
                        body(i)
                    body(passes - 1, last=True)
                    for u in range(PAIR):
                        sp.wait_ge(s_st[u], 32 * passes)

                @block.gpsimd
                def _(pool):
                    pool.memset(q_rem[:, :, :, :], 0.0).then_inc(s_zero, 1)
                    pool.memset(pT_corner, 0.0).then_inc(s_zero, 1)
                    pool.memset(v_rem, 0.0).then_inc(s_zero, 1)
                    pool.wait_ge(s_zero, 3)

                    def masks(b, u, first):
                        if not first:
                            pool.wait_ge(s_s, SGROUPS * b - SGROUPS * (PAIR - 1))
                        m = mask_sb[:, :]
                        for k in range(KT):
                            q = qT[:, k, bass.ds(SEQ * b, P)].unsqueeze(1).broadcast_to([P, HH, P])
                            nc.gpsimd.tensor_tensor(q_masked[:, u, k], q, m.unsqueeze(2).broadcast_to([P, HH, P]), ALU.mult).then_inc(s_qm, 1)
                        for k in range(KT):
                            q = qT[:, k, bass.ds(SEQ * b + P, REM)].unsqueeze(1).broadcast_to([P, HH, REM])
                            o = q_rem[:, u, k, 0:HR].rearrange("p (h q) -> p h q", h=HH)
                            nc.gpsimd.tensor_tensor(o, q, m.unsqueeze(2).broadcast_to([P, HH, REM]), ALU.mult).then_inc(s_qm, 1)

                    def last_keys(b, u, first):
                        pool.wait_ge(s_exp, SGROUPS * b + SGROUPS)
                        if not first:
                            pool.wait_ge(s_t, TGROUPS * b - TGROUPS * (PAIR - 1))
                        one = ones[:, 0:1].unsqueeze(2).broadcast_to([P, HEADS, REM])
                        nc.gpsimd.tensor_tensor(prob_last[:, u, :].rearrange("p (h k) -> p h k", k=REM), prob[:, u, 0:HEADS, P:SEQ], one,
                                                ALU.mult).then_inc(s_pl, 1)

                    def last_rows(b, u, first, base):
                        pool.wait_ge(s_rc, b + 1)
                        parts = r_raw[0:REM, :].rearrange("p (h c) -> p h c", c=VC)
                        total = r_sum[0:REM, :].rearrange("p (h c) -> p h c", c=DH)
                        nc.gpsimd.tensor_tensor(total, parts[:, :, 0:DH], parts[:, :, DH:2 * DH], ALU.add).then_inc(s_pchain, 1)
                        pool.wait_ge(s_pchain, base + 1)
                        nc.gpsimd.tensor_tensor(total, total, parts[:, :, 2 * DH:3 * DH], ALU.add).then_inc(s_pchain, 1)
                        pool.wait_ge(s_pchain, base + 2)
                        pool.wait_ge(s_rd, b + 1)
                        if not first:
                            pool.wait_ge(s_st[u], 16 * b - 16 * u)
                        o = r_out[0:REM, u, :].rearrange("p (h c) -> p h c", c=DH)
                        den = r_den[0:REM, :].unsqueeze(2).broadcast_to([REM, HEADS, DH])
                        nc.gpsimd.tensor_tensor(o, total, den, ALU.mult).then_inc(s_ro, 1)

                    for u in range(PAIR):
                        masks(u, u, True)

                    def body(i, last=False):
                        for u in range(PAIR):
                            last_keys(PAIR * i + u, u, is_first(i))
                            if not last:
                                masks(PAIR * i + PAIR + u, u, False)
                        for u in range(PAIR):
                            b = PAIR * i + u
                            last_rows(b, u, is_first(i), 2 * b)
                    body(0)
                    with pool.Fori(1, passes - 1) as i:
                        body(i)
                    body(passes - 1, last=True)

                @block.tensor
                def _(pe):
                    def scores(b, u, g, first):
                        n = SGROUPS * b + g
                        if not (first and u == 0 and g < 2):
                            pe.wait_ge(s_exp, n - 1)
                        for j in range(3):
                            s = 3 * g + j
                            k = s // HH if s < HEADS else s - HEADS
                            q = q_masked[:, u, k, s % HH, :] if s < HEADS else q_rem[:, u, k, :]
                            mm = nc.tensor.matmul(bank[g % 2][:, SEQ * j:SEQ * (j + 1)], q, keys[:, k, bass.ds(SEQ * b, SEQ)],
                                                  start=True, stop=True)
                        mm.then_inc(s_s, 1)

                    def turn(b, u, g, first):
                        n = TGROUPS * b + g
                        pe.wait_ge(s_exp, SGROUPS * b + turn_needs[g])
                        if not (first and u == 0 and g < 2):
                            pe.wait_ge(s_lo, n - 1)
                        ps = bank[2 + g % 2]
                        if g < 4:
                            for j in range(4):
                                mm = nc.tensor.transpose(ps[:, P * j:P * (j + 1)], prob[:, u, 4 * g + j, 0:P], ident[:, :])
                        elif g == 4:
                            for k in range(KT):
                                nc.tensor.transpose(ps[:, P * k:P * (k + 1)], prob[:, u, HEADS + k, 0:P], ident[:, :])
                            pe.wait_ge(s_pl, b + 1)
                            for k in range(KT):
                                mm = nc.tensor.transpose(ps[0:HR, P * (KT + k):P * (KT + k + 1)],
                                                         prob_last[:, u, HR * k:HR * (k + 1)], ident[:, :])
                        else:
                            for k in range(KT):
                                mm = nc.tensor.transpose(ps[0:REM, P * k:P * (k + 1)], prob[:, u, HEADS + k, P:SEQ], ident[:, :])
                        mm.then_inc(s_t, 1)

                    def values(b, u, g, first):
                        n = TGROUPS * b + g
                        pe.wait_ge(s_lo, n + 1)
                        for hd in range(4 * g, 4 * g + 4) if g < 4 else ():
                            k, j = hd // HH, hd % HH
                            if j == 0 and not (first and u == 0):
                                pe.wait_ge(s_oe, KT * b + k - 1)
                            for a in range(2):
                                nc.tensor.matmul(bank[4 + k][:, VC * j:VC * (j + 1)], pT[:, a, hd, :], v_main[:, u, VC * hd:VC * (hd + 1)],
                                                 start=(j == 0 and a == 0), stop=False, skip_group_check=True)
                        if g == 4:
                            pe.wait_ge(s_vd, b + 1)
                            for k in range(KT):
                                for a in range(2):
                                    mm = nc.tensor.matmul(bank[4 + k][:, 0:hc], pT_rem[0:HR, a, KT + k, :], v_diag[0:HR, u, hc * k:hc * (k + 1)],
                                                          start=False, stop=(a == 1), skip_group_check=True)
                            mm.then_inc(s_o, 1)
                            if not (first and u == 0):
                                pe.wait_ge(s_rc, b)
                            for hd in range(HEADS):
                                k, j = hd // HH, hd % HH
                                for a in range(2):
                                    nc.tensor.matmul(bank[6 + k][0:REM, VC * j:VC * (j + 1)], pT_rem[:, a, k, REM * j:REM * (j + 1)],
                                                     v_main[:, u, VC * hd:VC * (hd + 1)], start=(j == 0 and a == 0), stop=False,
                                                     skip_group_check=True)
                        if g == 5:
                            for hd in range(HEADS):
                                k, j = hd // HH, hd % HH
                                mm = nc.tensor.matmul(bank[6 + k][0:REM, VC * j:VC * (j + 1)], pT_corner[:, k, REM * j:REM * (j + 1)],
                                                      v_rem[:, u, VC * hd:VC * (hd + 1)], start=False, stop=(j == HH - 1),
                                                      skip_group_check=True)
                            mm.then_inc(s_r, 1)

                    pe.wait_ge(s_zero, 3)

                    pe.wait_ge(s_qm, 4)
                    for g in range(SGROUPS):
                        scores(0, 0, g, True)

                    def body(i, last=False):
                        first = is_first(i)
                        for u in range(PAIR):
                            b = PAIR * i + u
                            ahead = not (last and u == PAIR - 1)
                            if ahead:
                                pe.wait_ge(s_qm, 4 * b + 8)
                            for g in range(TGROUPS):
                                if ahead:
                                    scores(b + 1, 1 - u, g, False)
                                if g == 0 and not (first and u == 0):
                                    values(b - 1, 1 - u, TGROUPS - 1, first)
                                turn(b, u, g, first)
                                if g == 1:
                                    pe.wait_ge(s_ld[u], 16 * LOADS * i + 16 * LOADS)
                                if g >= 1:
                                    values(b, u, g - 1, first)
                    body(0)
                    with pe.Fori(1, passes - 1) as i:
                        body(i)
                    body(passes - 1, last=True)
                    values(IMAGES - 1, 1, TGROUPS - 1, False)

                @block.scalar
                def _(act):
                    def exps(b, u, g, first):
                        if g == 0 and not first:
                            act.wait_ge(s_t, TGROUPS * b - TGROUPS * (PAIR - 1))
                        act.wait_ge(s_max, SGROUPS * b + g + 1)
                        for j in range(3):
                            s = 3 * g + j
                            e = nc.scalar.activation(prob[:, u, s, :], bank[g % 2][:, SEQ * j:SEQ * (j + 1)], ACT.Exp,
                                                     bias=neg_max[:, u, s:s + 1])
                        e.then_inc(s_exp, 1)

                    def high(b, u, g):
                        act.wait_ge(s_t, TGROUPS * b + g + 1)
                        ps = bank[2 + g % 2]
                        if g < 4:
                            c = nc.scalar.activation(pT[:, 0, 4 * g:4 * g + 4, :], ps[:, :].rearrange("p (h q) -> p h q", q=P), ACT.Copy)
                        elif g == 4:
                            both = ps[:, :].rearrange("p (n q) -> p n q", q=P)
                            nc.scalar.activation(pT_rem[:, 0, 0:KT, :], both[:, 0:KT], ACT.Copy)
                            c = nc.scalar.activation(pT_rem[0:HR, 0, KT:2 * KT, :], both[0:HR, KT:2 * KT], ACT.Copy)
                        else:
                            if not (isinstance(b, int) and b == 0):
                                act.wait_ge(s_r, b)
                            c = nc.scalar.activation(pT_corner[0:REM, :, :], ps[0:REM, 0:KT * P].rearrange("p (n q) -> p n q", q=P), ACT.Copy)
                        c.then_inc(s_hi, 1)

                    def last_rows(b, first):
                        act.wait_ge(s_r, b + 1)
                        if not first:
                            act.wait_ge(s_ro, b)
                        for k in range(KT):
                            c = nc.scalar.activation(r_raw[0:REM, hc * k:hc * (k + 1)], bank[6 + k][0:REM, 0:hc], ACT.Copy)
                        c.then_inc(s_rc, 1)

                    for g in range(SGROUPS):
                        exps(0, 0, g, True)

                    def body(i, last=False):
                        first = is_first(i)
                        for u in range(PAIR):
                            b = PAIR * i + u
                            for g in range(TGROUPS):
                                high(b, u, g)
                                if not (last and u == PAIR - 1):
                                    exps(b + 1, 1 - u, g, first and u == 0)
                                if g == 1 and not (first and u == 0):
                                    last_rows(b - 1, first and u == 1)
                    body(0)
                    with act.Fori(1, passes - 1) as i:
                        body(i)
                    body(passes - 1, last=True)
                    last_rows(IMAGES - 1, False)

                @block.vector
                def _(dve):
                    dve.wait_ge(s_zero, 3)

                    def diagonal(b, u):
                        dve.wait_ge(s_ld[u], (16 * LOADS // PAIR) * (b - u) + 16 * LOADS)
                        m = rmask_bf[:, :].unsqueeze(2).broadcast_to([HR, HH, VC])
                        for k in range(KT):
                            o = v_diag[0:HR, u, hc * k:hc * (k + 1)].rearrange("p (h c) -> p h c", c=VC)
                            x = v_rep[0:HR, u, hc * k:hc * (k + 1)].rearrange("p (h c) -> p h c", c=VC)
                            c = nc.vector.tensor_tensor(o, x, m, ALU.mult)
                        c.then_inc(s_vd, 1)

                    def maxima(b, u, g):
                        dve.wait_ge(s_s, SGROUPS * b + g + 1)
                        nc.vector.tensor_reduce(neg_max[:, u, 3 * g:3 * g + 3], bank[g % 2][:, 0:3 * SEQ].rearrange("p (n k) -> p n k", n=3),
                                                AX.X, ALU.max, negate=True).then_inc(s_max, 1)

                    def low(b, u, g):
                        dve.wait_ge(s_hi, TGROUPS * b + g + 1)
                        ps = bank[2 + g % 2][:, :].rearrange("p (n q) -> p n q", q=P)
                        if g < 4:
                            c = nc.vector.tensor_tensor(pT[:, 1, 4 * g:4 * g + 4, :], ps, pT[:, 0, 4 * g:4 * g + 4, :], ALU.subtract)
                        elif g == 4:
                            nc.vector.tensor_tensor(pT_rem[:, 1, 0:KT, :], ps[:, 0:KT], pT_rem[:, 0, 0:KT, :], ALU.subtract)
                            c = nc.vector.tensor_tensor(pT_rem[0:HR, 1, KT:2 * KT, :], ps[0:HR, KT:2 * KT], pT_rem[0:HR, 0, KT:2 * KT, :], ALU.subtract)
                        else:
                            c = nc.vector.tensor_tensor(pT_corner[32:32 + REM, :, :], ps[0:REM, 0:KT], pT_corner[0:REM, :, :], ALU.subtract)
                        c.then_inc(s_lo, 1)

                    def rows(b, u):
                        dve.wait_ge(s_o, b + 1)
                        for k in range(KT):
                            parts = bank[4 + k][:, 0:hc].rearrange("p (h c) -> p h c", c=VC)
                            nc.vector.reciprocal(o_den[:, HH * k:HH * (k + 1)], parts[:, :, VC - 1])
                            three = parts[:, :, 0:3 * DH].rearrange("p h (a d) -> p h d a", a=3)
                            nc.vector.tensor_reduce(o_sum[:, P * k:P * (k + 1)].rearrange("p (h d) -> p h d", d=DH),
                                                    three, AX.X, ALU.add).then_inc(s_oe, 1)
                        dve.wait_ge(s_oe, KT * b + KT)
                        if not (isinstance(b, int) and b < PAIR):
                            dve.wait_ge(s_st[u], 16 * b - 16 * u)
                        den = o_den[:, :].unsqueeze(2).broadcast_to([P, HEADS, DH])
                        nc.vector.tensor_tensor(o_out[:, u, :].rearrange("p (h d) -> p h d", d=DH),
                                                o_sum[:, :].rearrange("p (h d) -> p h d", d=DH), den, ALU.mult).then_inc(s_oo, 1)

                    def last_sums(b):
                        dve.wait_ge(s_rc, b + 1)
                        nc.vector.reciprocal(r_den[0:REM, :], r_raw[0:REM, :].rearrange("p (h c) -> p h c", c=VC)[:, :, VC - 1]).then_inc(s_rd, 1)

                    for g in range(SGROUPS):
                        maxima(0, 0, g)

                    def body(i, last=False):
                        first = is_first(i)
                        for u in range(PAIR):
                            b = PAIR * i + u
                            for g in range(TGROUPS):
                                if not (last and u == PAIR - 1):
                                    maxima(b + 1, 1 - u, g)
                                if g == 0 and not (first and u == 0):
                                    rows(b - 1, 1 - u)
                                low(b, u, g)
                                if g == 1:
                                    diagonal(b, u)
                                if g == 2 and not (first and u == 0):
                                    last_sums(b - 1)
                    body(0)
                    body(1)
                    with dve.Fori(2, passes - 1) as i:
                        body(i)
                    body(passes - 1, last=True)
                    rows(IMAGES - 1, 1)
                    last_sums(IMAGES - 1)

        def output_phase(layer):
            n = f"o{layer}_"
            slots = 2 * PAIR
            s_ld = [sem(n + f"ld{u}") for u in range(slots)]
            s_t, s_T, s_mm, s_bias, s_add = (sem(n + x) for x in ("t", "T", "mm", "bias", "add"))
            s_st, s_mv, s_var, s_rstd, s_shift = (sem(n + x) for x in ("stats", "mv", "var", "rstd", "shift"))
            o_in = work[:, 0, 0:slots * D].rearrange("p (u c) -> p u c", u=slots)
            LAG = 4
            with nc.Block() as block:
                @block.sync
                def _(sp):
                    def load(t, slot):
                        sp.dma_start(o_in[:, slot, :], o_dram[bass.ds(P * t, P), :]).then_inc(s_ld[slot], 16)
                    for t in range(slots):
                        load(t, t)
                    if layer == 0:
                        sp.dma_start(gu_sb, w_gu_t.rearrange("(k p) e c -> p k e c", p=P)).then_inc(s_moe, 16)
                        sp.dma_start(down_sb, w_down_t).then_inc(s_moe, 16)
                    with sp.Fori(1, TILES // slots) as i:
                        for u in range(slots):
                            sp.wait_ge(s_t, slots * i - slots + u + 1)
                            load(slots * i + u, u)
                    for t in range(TILES // slots * slots, TILES):
                        sp.wait_ge(s_t, t - slots + 1)
                        load(t, t % slots)
                @block.gpsimd
                def _(pool):
                    def step(tau, u):
                        t = tau
                        if exists(t):
                            nc.gpsimd.tensor_tensor(col(t)(h), col(t)(h), bo_sb[layer][:, :], ALU.add).then_inc(s_bias, 1)
                        t = tau - LAG + 1
                        if exists(t):
                            raise_power(pool, t, 1, s_var, t + 1, s_rstd)
                    steps(pool, step, 3, LAG)

                @block.tensor
                def _(pe):
                    def turn(t, u, slot, loaded):
                        pe.wait_ge(s_ld[slot], loaded)
                        if reuses(t):
                            pe.wait_ge(s_T, t - 1)
                        for k in range(KT):
                            mm = nc.tensor.transpose(bank[u][:, P * k:P * (k + 1)], o_in[:, slot, P * k:P * (k + 1)], ident[:, :])
                        mm.then_inc(s_t, 1)

                    def product(t, u):
                        pe.wait_ge(s_T, t + 1)
                        if reuses(t):
                            pe.wait_ge(s_add, t - 1)
                        for k in range(KT):
                            mm = nc.tensor.matmul(bank[2 + u][:, 0:D], xT[:, u, P * k:P * (k + 1)], wo_sb[layer][:, k, :],
                                                  start=(k == 0), stop=(k == KT - 1))
                        mm.then_inc(s_mm, 1)

                    for t in range(slots):
                        turn(t, t % PAIR, t, 16)
                        if t >= 1:
                            product(t - 1, (t - 1) % PAIR)
                    with pe.Fori(1, TILES // slots) as i:
                        for j in range(slots):
                            t = slots * i + j
                            turn(t, j % PAIR, j, 16 * i + 16)
                            product(t - 1, (j + 1) % PAIR)
                    for t in range(TILES // slots * slots, TILES):
                        turn(t, t % PAIR, t % slots, 16 * (t // slots) + 16)
                        product(t - 1, (t - 1) % PAIR)
                    product(TILES - 1, (TILES - 1) % PAIR)

                @block.scalar
                def _(act):
                    def body(i):
                        for u in range(PAIR):
                            t = PAIR * i + u
                            act.wait_ge(s_t, t + 1)
                            if not is_first(i):
                                act.wait_ge(s_mm, t - 1)
                            nc.scalar.activation(xT[:, u, :], bank[u][:, 0:D], ACT.Copy).then_inc(s_T, 1)
                    for_each(act, PASSES, body)

                @block.vector
                def _(dve):
                    def step(tau, u):
                        t = tau
                        if exists(t):
                            dve.wait_ge(s_mm, t + 1)
                            dve.wait_ge(s_bias, t + 1)
                            nc.vector.tensor_tensor(col(t)(h), bank[2 + u][:, 0:D], col(t)(h), ALU.add).then_inc(s_add, 1)
                        t = tau - 4
                        if exists(t):
                            shifts(dve, t, u, 1, s_rstd, t + 1, s_shift)
                        t = tau - 3
                        if exists(t):
                            variances(dve, t, 1 - u, 1, s_mv, t + 1, s_var)
                        t = tau - 2
                        if exists(t):
                            if reuses(t):
                                dve.wait_ge(s_shift, t - 1)
                            means(dve, u, 1, s_st, t + 1, s_mv)
                        t = tau - 1
                        if exists(t):
                            dve.wait_ge(s_add, t + 1)
                            carry()
                            nc.vector.bn_stats(stats[:, 1 - u, :], col(t)(h)).then_inc(s_st, 1)
                    steps(dve, step, 3, LAG)
                    dve.wait_ge(s_shift, TILES)

        w_rows = sb("w_rows", [P, PADDED], BF16)

        def route_phase():
            s_chain = sem("r_chain")
            s_zero = sem("r_zero")
            s_xn, s_tx, s_xT, s_res = sem("r_xn"), sem("r_tx"), sem("r_xT"), sem("r_res")
            s_mm, s_sig, s_w, s_tw, s_wT = (sem("r_" + x) for x in ("mm", "sig", "w", "tw", "wT"))
            at = [KT * moe_up + BRANCHES * D]

            def cut(n):
                at[0] += n
                return region[:, at[0] - n:at[0]]
            BATCH = TILES // 3
            batches = TILES // BATCH
            PEELED, LAG = 2, 2
            scores_all = cut(TILES * EXPERTS)
            w3 = cut(TILES * P // 2).bitcast(BF16).rearrange("p (t c) -> p t c", t=TILES)
            choice = cut(BATCH * EXPERTS)
            hi2 = cut(BATCH * GROUPS * 2)
            lo2 = cut(BATCH * GROUPS * 2)
            top1, mid, low = cut(BATCH * GROUPS), cut(BATCH * GROUPS), cut(BATCH * GROUPS)
            group_pad = cut(BATCH * 8).rearrange("p (t k) -> p t k", t=BATCH)
            gval = cut(BATCH * 8).rearrange("p (t k) -> p t k", t=BATCH)
            gidx = cut(BATCH * 8).bitcast(U32).rearrange("p (t k) -> p t k", t=BATCH)
            ghot = cut(BATCH * GROUPS * 2).rearrange("p (t g k) -> p t g k", t=BATCH, k=2)
            gmask = cut(BATCH * GROUPS)
            kept = cut(BATCH * EXPERTS)
            kval = cut(BATCH * 8).rearrange("p (t k) -> p t k", t=BATCH)
            kidx = cut(BATCH * 8).bitcast(U32).rearrange("p (t k) -> p t k", t=BATCH)
            khot = cut(BATCH * EXPERTS * TOPK).rearrange("p (t e k) -> p t e k", t=BATCH, k=TOPK)
            chosen = cut(BATCH * EXPERTS)
            weight = cut(BATCH * EXPERTS)
            den = cut(BATCH)
            rest = cut(BATCH * EXPERTS)
            assert at[0] <= 18600

            def by_tile(x):
                return x.rearrange("p (t e) -> p t e", t=BATCH)

            with nc.Block() as block:
                @block.gpsimd
                def _(pool):
                    pool.memset(w3[:, :, :], 0.0).then_inc(s_zero, 1)
                    pool.memset(group_pad[:, :, :], LOWEST).then_inc(s_zero, 1)

                @block.scalar
                def _(act):
                    def step(tau, u):
                        t = tau
                        if exists(t):
                            if reuses(t):
                                act.wait_ge(s_tx, t - 1)
                            nc.scalar.activation(xn[:, u, :], col(t)(h), ACT.Identity, bias=shift[:, bass.ds(t, 1)],
                                                 scale=rstd[:, bass.ds(t, 1)]).then_inc(s_xn, 1)
                        t = tau - 1
                        if exists(t):
                            act.wait_ge(s_tx, t + 1)
                            if reuses(t):
                                act.wait_ge(s_mm, t - 1)
                            nc.scalar.activation(xT[:, 1 - u, :], bank[1 - u][:, 0:D], ACT.Copy).then_inc(s_xT, 1)
                            nc.scalar.activation(tile_cols(qT, t), bank[1 - u][:, 0:D].rearrange("p (k q) -> p k q", q=P),
                                                 ACT.Copy).then_inc(s_res, 1)
                        t = tau - 2
                        if exists(t):
                            act.wait_ge(s_mm, t + 1)
                            nc.scalar.activation(scores_all[:, bass.ds(EXPERTS * t, EXPERTS)], bank[2 + u][:, 0:EXPERTS],
                                                 ACT.Sigmoid).then_inc(s_sig, 1)
                    steps(act, step, PEELED, LAG)

                    def copy_out(c):
                        for j in range(BATCH):
                            t = BATCH * c + j
                            act.wait_ge(s_tw, t + 1)
                            src = bank[4 + j % 2][:, :].bitcast(BF16)[:, 0:P]
                            nc.scalar.activation(w_rows[:, bass.ds(P * t, P)], src, ACT.Copy).then_inc(s_wT, 1)
                    for_each(act, batches, copy_out)

                @block.tensor
                def _(pe):
                    def step(tau, u):
                        t = tau
                        if exists(t):
                            pe.wait_ge(s_xn, t + 1)
                            if reuses(t):
                                pe.wait_ge(s_res, t - 1)
                            for k in range(KT):
                                mm = nc.tensor.transpose(bank[u][:, P * k:P * (k + 1)], xn[:, u, P * k:P * (k + 1)], ident[:, :])
                            mm.then_inc(s_tx, 1)
                        t = tau - 1
                        if exists(t):
                            pe.wait_ge(s_xT, t + 1)
                            if reuses(t):
                                pe.wait_ge(s_sig, t - 1)
                            for k in range(KT):
                                mm = nc.tensor.matmul(bank[3 - u][:, 0:EXPERTS], xT[:, 1 - u, P * k:P * (k + 1)], wgate_sb[:, k, :],
                                                      start=(k == 0), stop=(k == KT - 1))
                            mm.then_inc(s_mm, 1)
                    steps(pe, step, PEELED, LAG)

                    def turn(c):
                        for j in range(BATCH):
                            t = BATCH * c + j
                            pe.wait_ge(s_w, c + 1)
                            if not (is_first(c) and j < 2):
                                pe.wait_ge(s_wT, t - 1)
                            nc.tensor.transpose(bank[4 + j % 2][:, :].bitcast(BF16)[:, 0:P],
                                                w3[:, bass.ds(t, 1), :].rearrange("p a c -> p (a c)"), ident_bf[:, :]).then_inc(s_tw, 1)
                    for_each(pe, batches, turn)

                @block.vector
                def _(dve):
                    chain = Chain(dve, s_chain)
                    dve.wait_ge(s_zero, 2)
                    links = [0]

                    def body(c):
                        chain.n, chain.base = 0, c * links[0]
                        V = nc.vector
                        tt = V.tensor_tensor
                        scores = scores_all[:, bass.ds(BATCH * EXPERTS * c, BATCH * EXPERTS)]
                        w_part = w3[:, bass.ds(BATCH * c, BATCH), 0:3 * EXPERTS].rearrange("p t (a e) -> p t a e", a=3)
                        dve.wait_ge(s_sig, BATCH * c + BATCH)
                        eb = ebias_sb[:, :].unsqueeze(1).broadcast_to([P, BATCH, EXPERTS])
                        chain.link(tt(by_tile(choice), by_tile(scores), eb, ALU.add))
                        four = choice.rearrange("p (g x) -> p g x", x=4)
                        a2, b2 = (x.rearrange("p (g x) -> p g x", x=2) for x in (hi2, lo2))
                        tt(a2, four[:, :, 0:2], four[:, :, 2:4], ALU.max)
                        chain.link(tt(b2, four[:, :, 0:2], four[:, :, 2:4], ALU.min))
                        tt(top1, a2[:, :, 0], a2[:, :, 1], ALU.max)
                        tt(mid, a2[:, :, 0], a2[:, :, 1], ALU.min)
                        chain.link(tt(low, b2[:, :, 0], b2[:, :, 1], ALU.max))
                        chain.link(tt(mid, mid, low, ALU.max))
                        g4 = group_pad[:, :, 0:GROUPS]
                        chain.link(tt(g4, top1.rearrange("p (t g) -> p t g", t=BATCH), mid.rearrange("p (t g) -> p t g", t=BATCH), ALU.add))
                        carry()
                        for u in range(BATCH):
                            last = V.max(gval[:, u, :], group_pad[:, u, :])
                        chain.link(last)
                        carry()
                        for u in range(BATCH):
                            last = V.max_index(gidx[:, u, :], gval[:, u, :], group_pad[:, u, :])
                        chain.link(last)
                        io = iota[:, 0:GROUPS].unsqueeze(1).unsqueeze(3).broadcast_to([P, BATCH, GROUPS, 2])
                        ix = gidx[:, :, 0:2].unsqueeze(2).broadcast_to([P, BATCH, GROUPS, 2])
                        chain.link(tt(ghot, io, ix, ALU.is_equal))
                        chain.link(V.tensor_reduce(gmask, ghot.rearrange("p t g k -> p (t g) k"), AX.X, ALU.add))
                        gm = gmask.unsqueeze(2).broadcast_to([P, BATCH * GROUPS, 4])
                        chain.link(tt(kept.rearrange("p (g x) -> p g x", x=4), four, gm, ALU.mult))
                        carry()
                        for u in range(BATCH):
                            last = V.max(kval[:, u, :], kept[:, EXPERTS * u:EXPERTS * (u + 1)])
                        chain.link(last)
                        carry()
                        for u in range(BATCH):
                            last = V.max_index(kidx[:, u, :], kval[:, u, :], kept[:, EXPERTS * u:EXPERTS * (u + 1)])
                        chain.link(last)
                        io = iota[:, :].unsqueeze(1).unsqueeze(3).broadcast_to([P, BATCH, EXPERTS, TOPK])
                        ix = kidx[:, :, 0:TOPK].unsqueeze(2).broadcast_to([P, BATCH, EXPERTS, TOPK])
                        chain.link(tt(khot, io, ix, ALU.is_equal))
                        chain.link(V.tensor_reduce(chosen, khot.rearrange("p t e k -> p (t e) k"), AX.X, ALU.add))
                        chain.link(tt(weight, scores, chosen, ALU.mult))
                        chain.link(V.tensor_reduce(den, by_tile(weight), AX.X, ALU.add))
                        chain.link(V.tensor_scalar(den, den, 1e-20, None, ALU.add))
                        chain.link(V.reciprocal(den, den))
                        chain.link(V.tensor_scalar(den, den, 2.5, None, ALU.mult))
                        chain.link(tt(by_tile(weight), by_tile(weight), den.unsqueeze(2).broadcast_to([P, BATCH, EXPERTS]), ALU.mult))
                        chain.link(V.tensor_copy(w_part[:, :, 0, :], by_tile(weight)))
                        chain.link(tt(by_tile(rest), by_tile(weight), w_part[:, :, 0, :], ALU.subtract))
                        chain.link(V.tensor_copy(w_part[:, :, 1, :], by_tile(rest)))
                        tt(w_part[:, :, 2, :], by_tile(rest), w_part[:, :, 1, :], ALU.subtract).then_inc(s_w, 1)
                        links[0] = links[0] or chain.n
                    for_each(dve, batches, body)

        select = sb("select", [P, EXPERTS, P], BF16)

        def expert_phase():
            s_sel, s_g, s_u, s_wb = sem("m_sel"), sem("m_g"), sem("m_u"), sem("m_wb")
            s_silu, s_prod, s_in, s_dn, s_y = (sem("m_" + x) for x in ("silu", "prod", "in", "dn", "y"))
            s_st, s_mv, s_var, s_rstd, s_shift = (sem("m_" + x) for x in ("stats", "mv", "var", "rstd", "shift"))
            order = [EXPERTS] + list(range(EXPERTS))
            silu = work[:, :, 0:CHUNK]
            prod = work[:, :, CHUNK:2 * CHUNK]
            inter = work[:, :, 2 * CHUNK:3 * CHUNK]
            with nc.Block() as block:
                @block.gpsimd
                def _(pool):
                    sel0 = select[:, :, :]
                    pool.memset(sel0, 0.0).then_inc(s_sel, 1)
                    for a in range(3):
                        pool.wait_ge(s_sel, a + 1)
                        pool.affine_select(out=sel0, in_=sel0, compare_op=ALU.not_equal, fill=1.0, base=-EXPERTS * a,
                                           pattern=[[-1, EXPERTS], [0, P]], channel_multiplier=1).then_inc(s_sel, 1)

                    def powers(c):
                        raise_power(pool, 3 * c, 3, s_var, c + 1, s_rstd)
                    for_each(pool, CHUNKS, powers)

                @block.tensor
                def _(pe):
                    pe.wait_ge(s_sel, 4)
                    pe.wait_ge(s_moe, 32)

                    def body(c):
                        x = [qT[:, k, bass.ds(CHUNK * c, CHUNK)] for k in range(KT)]

                        def up(s):
                            e, n = order[s], BRANCHES * c + s
                            if e < EXPERTS:
                                m = EXPERTS * c + s - 1
                                if not (is_first(c) and s == 1):
                                    pe.wait_ge(s_in, n)
                                nc.tensor.matmul(bank[4][:, 0:CHUNK], select[:, e, :], w_rows[:, bass.ds(CHUNK * c, CHUNK)],
                                                 start=True, stop=True).then_inc(s_wb, 1)
                            for half, done in ((0, s_g), (1, s_u)):
                                if not (is_first(c) and s < 2):
                                    pe.wait_ge(s_silu if half == 0 else s_prod, n - 1)
                                for k in range(KT):
                                    mm = nc.tensor.matmul(bank[2 * half + s % 2][:, 0:CHUNK], gu_sb[:, k, e, INTER * half:INTER * (half + 1)],
                                                          x[k], start=(k == 0), stop=(k == KT - 1))
                                mm.then_inc(done, 1)

                        def down(s):
                            e, n = order[s], BRANCHES * c + s
                            pe.wait_ge(s_in, n + 1)
                            for j in range(3):
                                if s == 0 and not is_first(c):
                                    pe.wait_ge(s_y, 3 * c - 2 + j)
                                mm = nc.tensor.matmul(bank[5 + j][:, 0:D], inter[:, s % 2, P * j:P * (j + 1)], down_sb[:, e, :],
                                                      start=(s == 0), stop=(s == BRANCHES - 1))
                            mm.then_inc(s_dn, 1)

                        for s in range(BRANCHES):
                            up(s)
                            if s >= 1:
                                down(s - 1)
                        down(BRANCHES - 1)
                    for_each(pe, CHUNKS, body)


                @block.scalar
                def _(act):
                    def body(c):
                        for s in range(BRANCHES):
                            n = BRANCHES * c + s
                            act.wait_ge(s_g, n + 1)
                            if not (is_first(c) and s < 2):
                                act.wait_ge(s_prod, n - 1)
                            nc.scalar.activation(silu[:, s % 2, :], bank[s % 2][:, 0:CHUNK], ACT.Silu).then_inc(s_silu, 1)
                    for_each(act, CHUNKS, body)

                @block.vector
                def _(dve):
                    def body(c):
                        for s in range(BRANCHES):
                            e, n = order[s], BRANCHES * c + s
                            dve.wait_ge(s_silu, n + 1)
                            dve.wait_ge(s_u, n + 1)
                            if s == 0:
                                if not is_first(c):
                                    dve.wait_ge(s_dn, n - 1)
                                nc.vector.tensor_tensor(inter[:, 0, :], silu[:, 0, :], bank[2][:, 0:CHUNK], ALU.mult).then_inc(s_prod, 1)
                                dve.wait_ge(s_prod, n + 1)
                                nc.vector.tensor_copy(prod[:, 0, 0:1], inter[:, 0, 0:1]).then_inc(s_in, 1)
                                continue
                            nc.vector.tensor_tensor(prod[:, s % 2, :], silu[:, s % 2, :], bank[2 + s % 2][:, 0:CHUNK], ALU.mult).then_inc(s_prod, 1)
                            dve.wait_ge(s_prod, n + 1)
                            dve.wait_ge(s_wb, EXPERTS * c + s)
                            if not (is_first(c) and s < 2):
                                dve.wait_ge(s_dn, n - 1)
                            nc.vector.tensor_tensor(inter[:, s % 2, :], prod[:, s % 2, :], bank[4][:, 0:CHUNK], ALU.mult).then_inc(s_in, 1)
                        dve.wait_ge(s_dn, BRANCHES * c + BRANCHES)
                        for j in range(3):
                            t = 3 * c + j
                            nc.vector.tensor_tensor(col(t)(h), bank[5 + j][:, 0:D], col(t)(h), ALU.add).then_inc(s_y, 1)
                        for j in range(3):
                            t = 3 * c + j
                            dve.wait_ge(s_y, t + 1)
                            carry(j)
                            nc.vector.bn_stats(stats[:, j, :], col(t)(h)).then_inc(s_st, 1)
                        if not is_first(c):
                            dve.wait_ge(s_shift, c)
                        means(dve, 0, 3, s_st, 3 * c + 3, s_mv)
                        variances(dve, 3 * c, 0, 3, s_mv, c + 1, s_var)
                        shifts(dve, 3 * c, 0, 3, s_rstd, c + 1, s_shift)
                    for_each(dve, CHUNKS, body)
                    dve.wait_ge(s_shift, CHUNKS)

        def ffn_phase():
            names = ("xn", "r1", "q1", "t1", "q1T", "g0", "u0", "sl0", "p0", "g1", "u1", "sl1", "p1", "sc2", "r2", "q2", "t2",
                     "q2T", "dn", "out")
            s = {x: sem("f_" + x) for x in names}
            s_chain, s_sc, s_round = (sem("f_" + x) for x in ("chain", "sc", "round"))
            s_st = [sem(f"f_st{u}") for u in range(PAIR)]
            at = [0]

            def cut(n):
                at[0] += n
                return region[:, at[0] - n:at[0]]
            x_all = cut(TILES * D).rearrange("p (t c) -> p t c", c=D)
            q1 = cut(TILES * D // 2).bitcast(BF16).rearrange("p (t c) -> p t c", c=D)
            q1T = cut(TILES * D // 2).bitcast(BF16).rearrange("p (t c) -> p t c", c=D)
            q2T = cut(PAIR * INNER // 2).bitcast(BF16).rearrange("p (u k r) -> p u k r", u=PAIR, r=P)
            res = cut(PAIR * D).rearrange("p (u c) -> p u c", u=PAIR)
            amax, step1, inv1 = cut(TILES), cut(TILES), cut(TILES)
            sc1 = cut(TILES * 3).rearrange("p (t g) -> p t g", g=3)
            amax2, inv2, sc2 = cut(TILES), cut(TILES), cut(TILES)
            round_c = cut(1)
            silu = work[:, 0, 0:INNER].rearrange("p (b c) -> p b c", b=2)
            q2 = work[:, 0, INNER:2 * INNER].bitcast(BF16).rearrange("p (u c) -> p u c", u=PAIR)
            prod = work[:, 1, :].rearrange("p (u c) -> p u c", u=PAIR)
            BATCH = TILES // 3
            batches = TILES // BATCH
            LAG = 3
            PEELED = 3

            with nc.Block() as block:
                @block.gpsimd
                def _(pool):
                    pool.memset(round_c, ROUND).then_inc(s_round, 1)

                @block.sync
                def _(sp):
                    def body(i):
                        for u in range(PAIR):
                            t = PAIR * i + u
                            sp.wait_ge(s["out"], t + 1)
                            sp.dma_start(out[bass.ds(P * t, P), :], res[:, u, :]).then_inc(s_st[u], 16)
                    body(0)
                    with sp.Fori(1, PASSES - 1) as i:
                        body(i)
                    for t in range(TILES - PAIR, TILES):
                        rows = min(P, ROWS - P * t)
                        sp.wait_ge(s["out"], t + 1)
                        sp.dma_start(out[P * t:P * t + rows, :], res[0:rows, t % PAIR, :]).then_inc(s_st[t % PAIR], 16)
                    for u in range(PAIR):
                        sp.wait_ge(s_st[u], 16 * PASSES)

                @block.scalar
                def _(act):
                    act.wait_ge(s_round, 1)

                    def turned(c):
                        for j in range(BATCH):
                            t = BATCH * c + j
                            act.wait_ge(s["t1"], t + 1)
                            nc.scalar.activation(col(t)(q1T), bank[4 + j % 2][:, :].bitcast(BF16)[:, 0:D], ACT.Copy).then_inc(s["q1T"], 1)

                    def batch(c):
                        act.wait_ge(s_sc, c + 1)
                        for j in range(BATCH):
                            t = BATCH * c + j
                            nc.scalar.activation(col(t)(x_all), col(t)(x_all), ACT.Identity, bias=round_c,
                                                 scale=inv1[:, bass.ds(t, 1)]).then_inc(s["r1"], 1)
                        if not is_first(c):
                            turned(c - 1)
                    for_each(act, batches, batch)
                    turned(batches - 1)

                    def step(tau, u):
                        if exists(tau):
                            for b in range(2):
                                act.wait_ge(s[f"g{b}"], tau + 1)
                                if reuses(tau, 1):
                                    act.wait_ge(s[f"p{b}"], tau)
                                nc.scalar.activation(silu[:, b, :], bank[2 * b][:, :], ACT.Silu,
                                                     scale=sc1[:, bass.ds(tau, 1), 2 * b]).then_inc(s[f"sl{b}"], 1)
                        t = tau - 1
                        if exists(t):
                            act.wait_ge(s["sc2"], t + 1)
                            x = prod[:, 1 - u, :]
                            nc.scalar.activation(x, x, ACT.Identity, bias=round_c, scale=inv2[:, bass.ds(t, 1)]).then_inc(s["r2"], 1)
                        t = tau - 2
                        if exists(t):
                            act.wait_ge(s["t2"], t + 1)
                            if reuses(t):
                                act.wait_ge(s["dn"], t - 1)
                            src = bank[5][:, :].bitcast(BF16).rearrange("p (k r) -> p k r", r=P)
                            nc.scalar.activation(q2T[:, u], src, ACT.Copy).then_inc(s["q2T"], 1)
                    steps(act, step, PEELED, LAG)

                @block.tensor
                def _(pe):
                    def turn(c):
                        for j in range(BATCH):
                            t = BATCH * c + j
                            pe.wait_ge(s["q1"], t + 1)
                            if not (is_first(c) and j < 2):
                                pe.wait_ge(s["q1T"], t - 1)
                            for k in range(KT):
                                mm = nc.tensor.transpose(bank[4 + j % 2][:, :].bitcast(BF16)[:, P * k:P * (k + 1)],
                                                         q1[:, bass.ds(t, 1), P * k:P * (k + 1)].rearrange("p a c -> p (a c)"), ident_bf[:, :])
                            mm.then_inc(s["t1"], 1)
                    for_each(pe, batches, turn)

                    def step(tau, u):
                        if exists(tau):
                            pe.wait_ge(s["q1T"], tau + 1)
                            for b in range(2):
                                for half in range(2):
                                    if reuses(tau, 1):
                                        pe.wait_ge(s[f"sl{b}" if half == 0 else f"p{b}"], tau)
                                    w0 = INNER * half + BANK * b
                                    for k in range(KT):
                                        mm = nc.tensor.matmul(bank[2 * b + half][:, :],
                                                              q1T[:, bass.ds(tau, 1), P * k:P * (k + 1)].rearrange("p a c -> p (a c)"),
                                                              ffn_up_q[:, k, w0:w0 + BANK], start=(k == 0), stop=(k == KT - 1))
                                    mm.then_inc(s[f"{'gu'[half]}{b}"], 1)
                        t = tau - 2
                        if exists(t):
                            pe.wait_ge(s["q2"], t + 1)
                            if reuses(t, 1):
                                pe.wait_ge(s["q2T"], t)
                            for k in range(IB):
                                mm = nc.tensor.transpose(bank[5][:, :].bitcast(BF16)[:, P * k:P * (k + 1)], q2[:, u, P * k:P * (k + 1)], ident_bf[:, :])
                            mm.then_inc(s["t2"], 1)
                        t = tau - 3
                        if exists(t):
                            pe.wait_ge(s["q2T"], t + 1)
                            if reuses(t):
                                pe.wait_ge(s["out"], t - 1)
                            for k in range(IB):
                                mm = nc.tensor.matmul(bank[7 - u][:, 0:D], q2T[:, 1 - u, k, :], ffn_down_q[:, k, :],
                                                      start=(k == 0), stop=(k == IB - 1))
                            mm.then_inc(s["dn"], 1)
                    steps(pe, step, PEELED, LAG)

                @block.vector
                def _(dve):
                    chain = Chain(dve, s_chain)
                    V = nc.vector
                    base = chain.n
                    links = [0]

                    def scales(c):
                        chain.n, chain.base = 0, base + c * links[0]
                        for j in range(BATCH):
                            t = BATCH * c + j
                            V.tensor_scalar(col(t)(x_all), col(t)(h), rstd[:, bass.ds(t, 1)], shift[:, bass.ds(t, 1)],
                                            ALU.mult, ALU.add).then_inc(s["xn"], 1)
                        dve.wait_ge(s["xn"], BATCH * c + BATCH)
                        a, d, inv = (x[:, bass.ds(BATCH * c, BATCH)] for x in (amax, step1, inv1))
                        chain.link(V.tensor_reduce(a, x_all[:, bass.ds(BATCH * c, BATCH), :], AX.X, ALU.max, apply_absolute_value=True))
                        chain.link(V.tensor_scalar(a, a, 1e-5, None, ALU.max))
                        V.tensor_scalar(d, a, 1.0 / 127.0, None, ALU.mult)
                        chain.link(V.reciprocal(inv, a))
                        V.tensor_scalar(sc1[:, bass.ds(BATCH * c, BATCH), 0], d, w_scale[:, 0:1], None, ALU.mult)
                        V.tensor_scalar(sc1[:, bass.ds(BATCH * c, BATCH), 1], d, w_scale[:, 1:2], None, ALU.mult)
                        V.tensor_scalar(sc1[:, bass.ds(BATCH * c, BATCH), 2], d, w_scale[:, 0:1], None, ALU.mult)
                        V.tensor_scalar(inv, inv, 127.0, None, ALU.mult).then_inc(s_sc, 1)
                        links[0] = links[0] or chain.n

                    def quantised(c):
                        for j in range(BATCH):
                            t = BATCH * c + j
                            dve.wait_ge(s["r1"], t + 1)
                            V.tensor_scalar(col(t)(q1), col(t)(x_all), ROUND, 127.0, ALU.subtract, ALU.min).then_inc(s["q1"], 1)

                    scales(0)

                    def batch(c, last=False):
                        if not last:
                            scales(c + 1)
                        quantised(c)
                    batch(0)
                    with dve.Fori(1, batches - 1) as c:
                        batch(c)
                    batch(batches - 1, last=True)
                    before = base + batches * links[0]
                    PER_TILE = 3

                    def step(tau, u):
                        chain.n, chain.base = 0, before + PER_TILE * tau
                        if exists(tau):
                            for b in range(2):
                                dve.wait_ge(s[f"sl{b}"], tau + 1)
                                dve.wait_ge(s[f"u{b}"], tau + 1)
                                V.scalar_tensor_tensor(prod[:, u, BANK * b:BANK * (b + 1)], bank[2 * b + 1][:, :], sc1[:, bass.ds(tau, 1), 1],
                                                       silu[:, b, :], ALU.mult, ALU.mult).then_inc(s[f"p{b}"], 1)
                            dve.wait_ge(s["p1"], tau + 1)
                            a, inv, sc = (x[:, bass.ds(tau, 1)] for x in (amax2, inv2, sc2))
                            chain.link(V.tensor_reduce(a, prod[:, u, :], AX.X, ALU.max, apply_absolute_value=True))
                        t = tau - 1
                        if exists(t):
                            dve.wait_ge(s["r2"], t + 1)
                            if reuses(t):
                                dve.wait_ge(s["t2"], t - 1)
                            V.tensor_scalar(q2[:, 1 - u, :], prod[:, 1 - u, :], ROUND, 127.0, ALU.subtract, ALU.min).then_inc(s["q2"], 1)
                        if exists(tau):
                            chain.link(V.tensor_scalar(a, a, 1e-5, None, ALU.max))
                            chain.link(V.reciprocal(inv, a))
                            V.tensor_scalar(inv, inv, 127.0, None, ALU.mult).then_inc(s["sc2"], 1)
                            V.tensor_scalar(sc, a, 1.0 / 127.0, w_scale[:, 2:3], ALU.mult, ALU.mult)
                        t = tau - 3
                        if exists(t):
                            dve.wait_ge(s["dn"], t + 1)
                            dve.wait_ge(s["sc2"], t + 1)
                            if reuses(t):
                                dve.wait_ge(s_st[1 - u], (16 // PAIR) * (t - (1 - u)))
                            V.scalar_tensor_tensor(res[:, 1 - u, :], bank[7 - u][:, 0:D], sc2[:, bass.ds(t, 1)], col(t)(h), ALU.mult,
                                                   ALU.add).then_inc(s["out"], 1)
                    steps(dve, step, PEELED, LAG)

        phases = [embed_phase, stats_phase, lambda: project_phase(0), lambda: attention_phase(0), lambda: output_phase(0),
                  route_phase, expert_phase, lambda: project_phase(1), lambda: attention_phase(1),
                  lambda: output_phase(1), ffn_phase]
        for phase in phases:
            with nc.cleanup_on_exit():
                phase()


def _tables():
    angle_of = 1.0 / 10000.0 ** (np.arange(0, DH, 2, dtype=np.float32) / np.float32(DH))
    pos = np.arange(PADDED) % SEQ
    freqs = pos.astype(np.float32)[:, None] * angle_of.astype(np.float32)[None, :]
    ang = np.concatenate((freqs, freqs), axis=-1)[:, ::2]
    c, s = np.cos(ang), np.sin(ang)
    cos = np.repeat(c, 2, axis=1)
    sin = np.stack((-s, s), axis=-1).reshape(PADDED, DH)
    quarter = np.float32(1.0 / DH ** 0.5)
    cos = np.concatenate((cos * quarter, cos), axis=1).astype(np.float32)
    sin = np.concatenate((sin * quarter, sin), axis=1).astype(np.float32)
    mask = (np.arange(P)[:, None] // DH == np.arange(HH)[None, :]).astype(np.float32)
    rem = (np.arange(HR)[:, None] // REM == np.arange(HH)[None, :]).astype(np.float32)
    iota = np.tile(np.arange(EXPERTS, dtype=np.float32), (P, 1))
    return {"rope_cos": cos, "rope_sin": sin, "head_mask": mask, "rem_mask": rem, "ident_in": np.eye(P, dtype=np.float32), "iota_in": iota}


def _layout(i):
    i = {k: np.asarray(v) for k, v in i.items()}
    x = i["x"].reshape(IMAGES, 3, 8, 16, 8, 16)
    gu = np.concatenate([
        np.concatenate((i["L0_ffn_gate_proj"], i["L0_ffn_shared_gate_w"][None]), axis=0),
        np.concatenate((i["L0_ffn_up_proj"], i["L0_ffn_shared_up_w"][None]), axis=0)], axis=1)
    down = np.concatenate((i["L0_ffn_down_proj"], i["L0_ffn_shared_down_w"][None]), axis=0)
    arrays = {
        "patches_t": x.transpose(3, 5, 1, 0, 2, 4).reshape(768, IMAGES * PATCHES),
        "txt": i["txt"],
        "w_emb_t": i["L0_tok_W"].T,
        "b_emb": i["L0_tok_b"],
        "w_qkv": np.concatenate((i["L0_attn_Wq"], i["L0_attn_Wk"], i["L0_attn_Wv"]), axis=1),
        "b_qkv": np.concatenate((i["L0_attn_bq"], i["L0_attn_bk"], i["L0_attn_bv"])),
        "w_o0": i["L0_attn_Wo"],
        "b_o0": i["L0_attn_bo"],
        "w_gate_t": i["L0_ffn_gate_w"].T,
        "e_bias": i["L0_ffn_e_bias"],
        "w_gu_t": gu.transpose(2, 0, 1),
        "w_down_t": down.transpose(2, 0, 1),
        "w_v1_t": i["L1_attn_Wv"].T,
        "b_v1": i["L1_attn_bv"],
        "w_o1_t": i["L1_attn_Wo"].T,
        "b_o1": i["L1_attn_bo"],
        "ffn_up_t": np.concatenate((i["L1_ffn_w_gate"], i["L1_ffn_w_up"]), axis=0).T,
        "ffn_down_t": i["L1_ffn_w_down"].T,
    }
    arrays.update(_tables())
    return {k: np.ascontiguousarray(v) for k, v in arrays.items()}


def build(nc, arrays):
    args = [nc.dram_tensor(f"in_{k}_dram", v.shape, mybir.dt.from_np(v.dtype), kind="ExternalInput").ap() for k, v in arrays.items()]
    out = nc.dram_tensor("out_0_dram", (ROWS, D), F32, kind="ExternalOutput").ap()
    fusion_kernel(nc, *args, out)


def kernel(**inputs):
    import concourse.bacc as _bacc
    from concourse.bass_utils import run_bass_kernel_spmd as _run

    nc = _bacc.Bacc("TRN2", target_bir_lowering=False, num_devices=1)
    arrays = _layout(inputs)
    build(nc, arrays)
    r = _run(nc, [{f"in_{k}_dram": v for k, v in arrays.items()}], core_ids=[0])
    return r.results[0]["out_0_dram"].reshape(IMAGES, SEQ, D)
```

```python
from contextlib import ExitStack

import numpy as np

import concourse.bass as bass
from concourse import mybir

ALU = mybir.AluOpType
ACT = mybir.ActivationFunctionType
AX = mybir.AxisListType
F32 = mybir.dt.float32
BF16 = mybir.dt.bfloat16
F16 = mybir.dt.float16
U32 = mybir.dt.uint32
F32R = mybir.dt.float32r

P = 128
D = 256
KT = D // P
IMAGES = 16
PATCHES = 64
TEXT = 77
SEQ = PATCHES + TEXT
ROWS = IMAGES * SEQ
TILES = -(-ROWS // P)
PADDED = TILES * P
EMB_K = 768 // P
EMB_TILES = IMAGES * PATCHES // P
PAIR = 2
PASSES = TILES // PAIR
HEADS = 16
DH = D // HEADS
HH = HEADS // KT
REM = SEQ - P
HR = HH * REM
VC = 3 * DH + 1
SLOTS = HEADS + KT
SGROUPS = SLOTS // 3
TGROUPS = 6
EXPERTS = 16
BRANCHES = EXPERTS + 1
INTER = 128
GROUPS = 4
TOPK = 4
CHUNK = 3 * P
CHUNKS = PADDED // CHUNK
INNER = 1024
IB = INNER // P
BANK = 512
ROUND = 12582912.0
LN_EPS = 1e-5
LOWEST = -3.0e38


def for_each(eng, count, body):
    body(0)
    with eng.Fori(1, count) as i:
        body(i)


def steps(eng, step, peeled, lag):
    for tau in range(PAIR * peeled):
        step(tau, tau % PAIR)
    if peeled < PASSES:
        with eng.Fori(peeled, PASSES) as i:
            for u in range(PAIR):
                step(PAIR * i + u, u)
    for tau in range(TILES, TILES + lag):
        step(tau, tau % PAIR)


def exists(t):
    return not isinstance(t, int) or 0 <= t < TILES


def reuses(t, slots=PAIR):
    return not isinstance(t, int) or t >= slots


def is_first(i):
    return isinstance(i, int) and i == 0


class Chain:

    def __init__(self, eng, semaphore):
        self.eng, self.semaphore, self.base, self.n = eng, semaphore, 0, 0

    def link(self, instruction):
        instruction.then_inc(self.semaphore, 1)
        self.n += 1
        self.eng.wait_ge(self.semaphore, self.base + self.n)


def fusion_kernel(nc, patches_t, txt, w_emb_t, b_emb, w_qkv, b_qkv, w_o0, b_o0, w_gate_t, e_bias,
                  w_gu_t, w_down_t, w_v1_t, b_v1, w_o1_t, b_o1, ffn_up_t, ffn_down_t,
                  rope_cos, rope_sin, head_mask, rem_mask, ident_in, iota_in, out):
    ctx = ExitStack()
    with ctx:
        offset_of = {}

        def sb(name, shape, dt=F32):
            tensor = ctx.enter_context(nc.sbuf_tensor(name, shape, dt))
            offset_of[name] = nc.sbuf_base - int(np.prod(shape[1:])) * mybir.dt.size(dt)
            return tensor

        def rounded(name, place, words, n):
            return nc.alloc_sbuf_tensor_at(name, [P, n], F32R, offset=offset_of[place] + 4 * words)[:, :]

        def sem(name):
            return nc.alloc_semaphore(name=name)

        def dram(name, shape, dt=F32):
            return nc.dram_tensor(name, shape, dt, kind="Internal").ap()

        h0_dram = dram("h0_dram", [PADDED, D])
        v_dram = dram("v_dram", [PADDED, HEADS * VC], BF16)
        o_dram = dram("o_dram", [PADDED, D])

        h = sb("h", [P, TILES, D])
        qT = sb("qT", [P, KT, PADDED])
        kT = sb("kT", [P, KT, PADDED])
        stats = sb("stats", [P, TILES, 6])
        mean_var = sb("mean_var", [P, TILES, 2])
        rstd = sb("rstd", [P, TILES])
        shift = sb("shift", [P, TILES])
        expo = sb("expo", [P, TILES])
        ident = sb("ident", [P, P])
        ident_bf = sb("ident_bf", [P, P], BF16)
        iota = sb("iota", [P, EXPERTS])
        ones = sb("ones", [P, P])
        carrier = sb("carrier", [P, 4])

        wqkv_sb = sb("wqkv_sb", [P, KT, 3 * D])
        wo_sb = [sb(f"wo{n}_sb", [P, KT, D]) for n in range(2)]
        wv1_sb = sb("wv1_sb", [P, KT, D])
        wgate_sb = sb("wgate_sb", [P, KT, EXPERTS])
        bo_sb = [sb(f"bo{n}_sb", [P, D]) for n in range(2)]
        bv1_sb = sb("bv1_sb", [P, D])
        ebias_sb = sb("ebias_sb", [P, EXPERTS])
        ffn_up_q = sb("ffn_up_q", [P, KT, 2 * INNER], BF16)
        ffn_down_q = sb("ffn_down_q", [P, IB, D], BF16)
        w_scale = sb("w_scale", [P, 3])
        tables = sb("tables", [P, 2, TILES, 2 * DH])
        cos_sb, sin_sb = tables[:, 0], tables[:, 1]
        mask_sb = sb("mask_sb", [P, HH])
        rmask_sb = sb("rmask_sb", [HR, HH])
        rmask_bf = sb("rmask_bf", [HR, HH], BF16)

        s_moe = [nc.alloc_semaphore(name=f"moe{n}") for n in range(3)]

        xn = sb("xn", [P, PAIR, D])
        xT = sb("xT", [P, PAIR, D])
        work = sb("work", [P, 12 * D])

        moe_up = BRANCHES * 2 * INTER
        experts_words = KT * moe_up + BRANCHES * D
        region_words = 2 * experts_words
        region = sb("region", [P, region_words])
        bqkv_sb = region[:, region_words - 4 * D:region_words - D]
        bemb_sb = region[:, region_words - D:]
        used = [0]

        def piece(n, dt=F32):
            words = n if dt == F32 else n // 2
            a = used[0]
            used[0] += words
            v = region[:, a:a + words]
            return v if dt == F32 else v.bitcast(dt)

        q_masked = piece(PAIR * KT * HH * P).rearrange("p (s t h q) -> p s t h q", s=PAIR, t=KT, h=HH)
        q_rem = piece(PAIR * KT * P).rearrange("p (s t q) -> p s t q", s=PAIR, t=KT)
        prob = piece(PAIR * SLOTS * SEQ).rearrange("p (s n k) -> p s n k", s=PAIR, n=SLOTS)
        pT = piece(2 * HEADS * P, F16).rearrange("p (a h q) -> p a h q", a=2, h=HEADS)
        pT_rem = piece(2 * 2 * KT * P, F16).rearrange("p (a n q) -> p a n q", a=2, n=2 * KT)
        pT_corner = piece(KT * P, F16).rearrange("p (t q) -> p t q", t=KT)
        v_main = piece(PAIR * HEADS * VC, BF16).rearrange("p (s c) -> p s c", s=PAIR)
        v_rem = piece(PAIR * HEADS * VC, BF16).rearrange("p (s c) -> p s c", s=PAIR)
        v_rep = piece(PAIR * HEADS * VC, BF16).rearrange("p (s c) -> p s c", s=PAIR)
        v_diag = piece(PAIR * HEADS * VC, BF16).rearrange("p (s c) -> p s c", s=PAIR)
        prob_last = piece(PAIR * HEADS * REM).rearrange("p (s c) -> p s c", s=PAIR)
        neg_max = piece(PAIR * SLOTS).rearrange("p (s n) -> p s n", s=PAIR)
        o_sum = piece(D)
        o_den = piece(HEADS)
        o_out = piece(PAIR * D).rearrange("p (s c) -> p s c", s=PAIR)
        r_raw = piece(HEADS * VC)
        r_sum = piece(D)
        r_den = piece(HEADS)
        r_out = piece(PAIR * D).rearrange("p (s c) -> p s c", s=PAIR)
        assert used[0] <= region_words
        raw = region[:, 0:experts_words]

        def gate_up(x):
            return x[:, 0:KT * moe_up].rearrange("p (t e c) -> p t e c", t=KT, e=BRANCHES)

        def downs(x):
            return x[:, KT * moe_up:].rearrange("p (e c) -> p e c", e=BRANCHES)
        low_r = rounded("low_r", "region", 0, experts_words)
        high_r = rounded("high_r", "region", experts_words, experts_words)
        gu_lo, gu_hi, down_lo, down_hi = (f(x) for f in (gate_up, downs) for x in (low_r, high_r))
        x_hi, x_lo = (rounded(n, place, 0, KT * PADDED).rearrange("p (k r) -> p k r", k=KT) for n, place in (("x_hi", "qT"), ("x_lo", "kT")))
        PIECES = 3
        piece_words = experts_words // PIECES
        assert piece_words == moe_up == BRANCHES * D
        raw_pieces, low_pieces, high_pieces = ([x[:, piece_words * n:piece_words * (n + 1)] for n in range(PIECES)]
                                               for x in (raw, low_r, high_r))

        bank = [ctx.enter_context(nc.psum_tensor(f"bank{n}", [P, BANK], F32)) for n in range(8)]

        def col(t, n=1):
            return lambda x: x[:, bass.ds(t, 1), :].rearrange("p a c -> p (a c)")

        def tile_cols(x, t):
            return x[:, :, bass.ds(P * t, P)]

        v_all = region[:, 0:TILES * HEADS * VC // 2].bitcast(BF16).rearrange("p (t c) -> p t c", t=TILES)

        def carry(k=0):
            return nc.vector.tensor_copy(carrier[:, k:k + 1], ones[:, 0:1])

        def means(dve, slot, n, ready, count, done):
            dve.wait_ge(ready, count)
            carry(3)
            for j in range(slot, slot + n):
                last = nc.vector.bn_aggr(mean_var[:, j, :], stats[:, j, :])
            last.then_inc(done, 1)

        def variances(dve, t, slot, n, ready, count, done):
            dve.wait_ge(ready, count)
            nc.vector.tensor_scalar(rstd[:, bass.ds(t, n)], mean_var[:, slot:slot + n, 1], LN_EPS, None, ALU.add).then_inc(done, 1)

        def raise_power(pool, t, n, ready, count, done):
            pool.wait_ge(ready, count)
            r = rstd[:, bass.ds(t, n)]
            nc.gpsimd.tensor_tensor(r, r, expo[:, 0:n], ALU.pow).then_inc(done, 1)

        def shifts(dve, t, slot, n, ready, count, done):
            dve.wait_ge(ready, count)
            nc.vector.scalar_tensor_tensor(shift[:, bass.ds(t, n)], mean_var[:, slot:slot + n, 0], -1.0, rstd[:, bass.ds(t, n)],
                                           ALU.mult, ALU.mult).then_inc(done, 1)

        s_project = nc.alloc_semaphore(name="project_weights")
        s_late = nc.alloc_semaphore(name="late_weights")
        PROJECT_LOADS, LATE_LOADS = 4, 7

        def load_late_weights(sp):
            def late(dst, src):
                sp.dma_start(dst, src).then_inc(s_late, 16)
            for n, (w, b) in enumerate(((w_o0, b_o0), (w_o1_t, b_o1))):
                late(wo_sb[n][:, :, :], w.rearrange("(k p) c -> p k c", p=P))
                late(bo_sb[n][:, :], b.rearrange("(a c) -> a c", a=1).broadcast_to([P, D]))
            late(wv1_sb[:, :, :], w_v1_t.rearrange("(k p) c -> p k c", p=P))
            late(bv1_sb[:, :], b_v1.rearrange("(a c) -> a c", a=1).broadcast_to([P, D]))
            late(wgate_sb[:, :, :], w_gate_t.rearrange("(k p) c -> p k c", p=P))

        def embed_phase():
            s_w, s_mask = sem("e_w"), sem("e_mask")
            s_raw = [sem(f"e_raw{g}") for g in range(3)]
            s_patch = [sem(f"e_patch{t}") for t in range(EMB_TILES)]
            s_mm, s_add = sem("e_mm"), sem("e_add")
            s_set = sem("e_set")
            s_pad, s_id = sem("e_pad"), sem("e_id")
            s_chain = sem("e_chain")
            s_sum, s_tot = sem("e_sum"), sem("e_tot")
            s_inv, s_scaled = sem("e_inv"), sem("e_scaled")
            s_stats, s_mv, s_var, s_rstd, s_shift = (sem("e_" + x) for x in ("stats", "mv", "var", "rstd", "shift"))
            BATCH = TILES // 3
            batches = TILES // BATCH
            s_h = [sem(f"e_h{c}") for c in range(batches)]
            images_of = [min(IMAGES, -(-BATCH * P * (c + 1) // SEQ)) for c in range(batches)]
            last_of = [(n - 1) // 2 for n in images_of]
            s_st = [sem(f"e_st{c}") for c in range(batches)]

            def batch_of(t):
                return next(c for c in range(batches) if t <= last_of[c])
            at = [0]

            def cut(n):
                at[0] += n
                return region[:, at[0] - n:at[0]]
            patch = cut(EMB_TILES * EMB_K * P).rearrange("p (t k r) -> p t k r", t=EMB_TILES, k=EMB_K)
            raw_up = cut(KT * 2 * INNER).rearrange("p (g k c) -> p g k c", g=2, k=KT)
            raw_down = cut(IB * D).rearrange("p (k c) -> p k c", k=IB)
            raws = [raw_up[:, 0], raw_up[:, 1], raw_down]
            embedded = cut(EMB_TILES * D).rearrange("p (t c) -> p t c", t=EMB_TILES)
            w_emb = cut(EMB_K * D).rearrange("p (k c) -> p k c", k=EMB_K)
            zero, abs_sum, inverse, round_c = cut(D), cut(3), cut(3), cut(1)
            assert at[0] <= region_words - 4 * D
            with nc.Block() as block:
                @block.sync
                def _(sp):
                    sp.dma_start(w_emb, w_emb_t.rearrange("(k p) c -> p k c", p=P)).then_inc(s_w, 16)
                    src = patches_t.rearrange("(k p) r -> p k r", p=P)
                    for t in range(EMB_TILES):
                        sp.dma_start(patch[:, t], src[:, :, P * t:P * (t + 1)]).then_inc(s_patch[t], 16)
                        if t == 0:
                            sp.dma_start(bemb_sb, b_emb.rearrange("(a c) -> a c", a=1).broadcast_to([P, D])).then_inc(s_w, 16)
                    for t in range(EMB_TILES):
                        sp.wait_ge(s_add, t + 1)
                        for j in range(2):
                            dst = h0_dram[SEQ * (2 * t + j):SEQ * (2 * t + j) + PATCHES, :]
                            sp.dma_start(dst, embedded[PATCHES * j:PATCHES * (j + 1), t, :]).then_inc(s_st[batch_of(t)], 16)
                        for c in range(batches):
                            if t != min(last_of[c] + 1, EMB_TILES - 1):
                                continue
                            stores = 2 * (last_of[c] - (last_of[c - 1] if c else -1))
                            sp.wait_ge(s_st[c], 16 * stores)
                            if c == 0:
                                sp.wait_ge(s_pad, 16 * 3)
                            rows = h0_dram[BATCH * P * c:BATCH * P * (c + 1), :].rearrange("(t p) c -> p t c", p=P)
                            sp.dma_start(h[:, BATCH * c:BATCH * (c + 1), :], rows).then_inc(s_h[c], 16)

                @block.gpsimd
                def _(pool):
                    pool.memset(zero, 0.0).then_inc(s_set, 1)
                    pool.memset(round_c, ROUND).then_inc(s_set, 1)
                    pool.memset(ones[:, :], 1.0).then_inc(s_set, 1)
                    pool.memset(expo[:, :], -0.5).then_inc(s_set, 1)
                    pool.wait_ge(s_set, 4)
                    pad = PADDED - ROWS
                    pool.dma_start(h0_dram[ROWS:PADDED, :], zero[0:pad, :]).then_inc(s_pad, 16)
                    pool.dma_start(o_dram[ROWS:PADDED, :], zero[0:pad, :]).then_inc(s_pad, 16)
                    rows = h0_dram[0:ROWS, :].rearrange("(b s) c -> b s c", s=SEQ)
                    pool.dma_start(rows[:, PATCHES:SEQ, :], txt).then_inc(s_pad, 16)
                    pool.wait_ge(s_pad, 16 * 3)
                    for c in range(batches):
                        raise_power(pool, BATCH * c, BATCH, s_var, c + 1, s_rstd)

                @block.scalar
                def _(act):
                    for g in range(2):
                        act.wait_ge(s_patch[2 * g + 1], 16)
                        src = ffn_up_t.rearrange("(k p) c -> p k c", p=P)[:, :, INNER * g:INNER * (g + 1)]
                        act.dma_start(raw_up[:, g], src).then_inc(s_raw[g], 16)
                    act.dma_start(raw_down, ffn_down_t.rearrange("(k p) c -> p k c", p=P)).then_inc(s_raw[2], 16)
                    for dst, src in ((ident[:, :], ident_in), (iota[:, :], iota_in), (mask_sb[:, :], head_mask),
                                     (rmask_sb[:, :], rem_mask),
                                     (ebias_sb[:, :], e_bias.rearrange("(a c) -> a c", a=1).broadcast_to([P, EXPERTS]))):
                        act.dma_start(dst, src).then_inc(s_mask, 16)

                    def project(dst, src):
                        act.dma_start(dst, src).then_inc(s_project, 16)
                    act.wait_ge(s_add, EMB_TILES)
                    project(wqkv_sb[:, :, :], w_qkv.rearrange("(k p) c -> p k c", p=P))
                    project(bqkv_sb, b_qkv.rearrange("(a c) -> a c", a=1).broadcast_to([P, 3 * D]))
                    project(cos_sb, rope_cos.rearrange("(t p) c -> p t c", p=P))
                    project(sin_sb, rope_sin.rearrange("(t p) c -> p t c", p=P))
                    act.wait_ge(s_mask, 16 * 5)
                    act.activation(ident_bf[:, :], ident[:, :], ACT.Copy).then_inc(s_id, 1)
                    act.activation(rmask_bf[:, :], rmask_sb[:, :], ACT.Copy).then_inc(s_id, 1)
                    act.wait_ge(s_set, 4)
                    act.wait_ge(s_inv, 1)
                    for g in range(3):
                        act.activation(raws[g], raws[g], ACT.Identity, bias=round_c, scale=inverse[:, g:g + 1]).then_inc(s_scaled, 1)
                    act.wait_ge(s_id, 2)

                @block.tensor
                def _(pe):
                    pe.wait_ge(s_w, 32)
                    for t in range(EMB_TILES):
                        pe.wait_ge(s_patch[t], 16)
                        if t >= 2:
                            pe.wait_ge(s_add, t - 1)
                        for k in range(EMB_K):
                            mm = nc.tensor.matmul(bank[t % 2][:, 0:D], patch[:, t, k, :], w_emb[:, k, :],
                                                  start=(k == 0), stop=(k == EMB_K - 1))
                        mm.then_inc(s_mm, 1)
                    pe.wait_ge(s_set, 4)
                    pe.wait_ge(s_sum, 3)
                    nc.tensor.matmul(bank[2][:, 0:3], ones[:, :], abs_sum, start=True, stop=True).then_inc(s_tot, 1)

                @block.vector
                def _(dve):
                    dve.wait_ge(s_w, 32)
                    for t in range(EMB_TILES):
                        dve.wait_ge(s_mm, t + 1)
                        nc.vector.tensor_tensor(embedded[:, t, :], bank[t % 2][:, 0:D], bemb_sb, ALU.add).then_inc(s_add, 1)
                        g = t - (EMB_TILES - 3)
                        if g >= 0:
                            dve.wait_ge(s_raw[g], 16)
                            nc.vector.tensor_reduce(abs_sum[:, g:g + 1], raws[g], AX.XY, ALU.add, apply_absolute_value=True).then_inc(s_sum, 1)

                    chain = Chain(dve, s_chain)
                    dve.wait_ge(s_tot, 1)
                    chain.link(nc.vector.tensor_scalar(w_scale[:, :], bank[2][:, 0:3], 1.0 / (D * INNER), 1e-5, ALU.mult, ALU.max))
                    nc.vector.reciprocal(inverse, w_scale[:, :]).then_inc(s_inv, 1)
                    quant = [ffn_up_q[:, :, 0:INNER], ffn_up_q[:, :, INNER:], ffn_down_q[:, :, :]]

                    def ternary(g):
                        dve.wait_ge(s_scaled, g + 1)
                        chain.link(nc.vector.tensor_scalar(raws[g], raws[g], ROUND, 1.0, ALU.subtract, ALU.min))
                        chain.link(nc.vector.tensor_scalar(quant[g], raws[g], -1.0, None, ALU.max))

                    def batch_stats(c):
                        dve.wait_ge(s_h[c], 16)
                        for t in range(BATCH * c, BATCH * (c + 1)):
                            nc.vector.bn_stats(stats[:, t, :], h[:, t, :]).then_inc(s_stats, 1)
                        means(dve, BATCH * c, BATCH, s_stats, BATCH * (c + 1), s_mv)
                        variances(dve, BATCH * c, BATCH * c, BATCH, s_mv, c + 1, s_var)
                    for c in range(batches):
                        ternary(c)
                        batch_stats(c)
                    for c in range(batches):
                        shifts(dve, BATCH * c, BATCH * c, BATCH, s_rstd, c + 1, s_shift)
                    dve.wait_ge(s_shift, batches)

        def project_phase(layer):
            n = f"p{layer}_"
            s_xn, s_tx, s_xT = sem(n + "xn"), sem(n + "tx"), sem(n + "xT")
            s_qk, s_v = sem(n + "qk"), sem(n + "v")
            s_qkb, s_vb = sem(n + "qkb"), sem(n + "vb")
            s_cos, s_sin, s_rot = sem(n + "cos"), sem(n + "sin"), sem(n + "rot")
            s_tq, s_qT = sem(n + "tq"), sem(n + "qT")
            s_v0, s_r1, s_v1, s_v2 = sem(n + "v0"), sem(n + "r1"), sem(n + "v1"), sem(n + "v2")
            s_one, s_st = sem(n + "one"), sem(n + "st")
            qk_cols = 2 * D if layer == 0 else 0
            at = [TILES * HEADS * VC // 2]

            def cut(n):
                at[0] += PAIR * n
                return region[:, at[0] - PAIR * n:at[0]].rearrange("p (u c) -> p u c", u=PAIR)
            qk, qk_cos, qk_rot, v, v_res = cut(2 * D), cut(2 * D), cut(2 * D), cut(D), cut(D)
            assert at[0] <= region_words - 4 * D
            w = wqkv_sb if layer == 0 else wv1_sb
            bias = bqkv_sb if layer == 0 else bv1_sb
            turned = qk_rot if layer == 0 else v
            turns = 4 if layer == 0 else 2
            s_turned = s_rot if layer == 0 else s_vb

            def v_parts(t):
                return col(t)(v_all).rearrange("p (h c) -> p h c", c=VC)
            PRODUCT, ROTATE, TURN = 2, 3, 4
            PEELED = 3

            def heads(x):
                return x.rearrange("p (h c) -> p h c", c=DH)

            with nc.Block() as block:
                @block.gpsimd
                def _(pool):
                    columns = v_all.rearrange("p t (h c) -> p (t h) c", c=VC)
                    pool.memset(columns[:, :, VC - 1:VC], 1.0).then_inc(s_one, 1)
                    if layer == 0:
                        pool.wait_ge(s_project, 16 * PROJECT_LOADS)

                    def step(tau, u):
                        t = tau - ROTATE
                        if exists(t):
                            if layer == 0:
                                pool.wait_ge(s_qkb, t + 1)
                                if reuses(t):
                                    pool.wait_ge(s_rot, t - 1)
                                x = qk[:, 1 - u, :].rearrange("p (a h c) -> p a h c", a=2, c=DH)
                                o = qk_cos[:, 1 - u, :].rearrange("p (a h c) -> p a h c", a=2, c=DH)
                                c = cos_sb[:, bass.ds(t, 1), :].rearrange("p x (a c) -> p (x a) c", a=2)
                                c = c.unsqueeze(2).broadcast_to([P, 2, HEADS, DH])
                                nc.gpsimd.tensor_tensor(o, x, c, ALU.mult).then_inc(s_cos, 1)
                            pool.wait_ge(s_v0, t + 1)
                            if reuses(t):
                                pool.wait_ge(s_v2, t - 1)
                            nc.gpsimd.tensor_tensor(heads(v_res[:, 1 - u, :]), heads(v[:, 1 - u, :]), v_parts(t)[:, :, 0:DH],
                                                    ALU.subtract).then_inc(s_r1, 1)
                        t = tau - TURN
                        if exists(t):
                            pool.wait_ge(s_v1, t + 1)
                            nc.gpsimd.tensor_tensor(v_parts(t)[:, :, 2 * DH:3 * DH], heads(v_res[:, u, :]),
                                                    v_parts(t)[:, :, DH:2 * DH], ALU.subtract).then_inc(s_v2, 1)
                    steps(pool, step, PEELED, TURN)

                @block.scalar
                def _(act):
                    def step(tau, u):
                        t = tau
                        if exists(t):
                            if reuses(t):
                                act.wait_ge(s_tx, t - 1)
                            nc.scalar.activation(xn[:, u, :], col(t)(h), ACT.Identity, bias=shift[:, bass.ds(t, 1)],
                                                 scale=rstd[:, bass.ds(t, 1)]).then_inc(s_xn, 1)
                        t = tau - 1
                        if exists(t):
                            act.wait_ge(s_tx, t + 1)
                            if reuses(t):
                                act.wait_ge(s_v, t - 1)
                            nc.scalar.activation(xT[:, 1 - u, :], bank[1 - u][:, 0:D], ACT.Copy).then_inc(s_xT, 1)
                        t = tau - ROTATE
                        if exists(t):
                            act.wait_ge(s_vb, t + 1)
                            nc.scalar.activation(v_parts(t)[:, :, 0:DH], heads(v[:, 1 - u, :]), ACT.Copy).then_inc(s_v0, 1)
                        t = tau - TURN
                        if exists(t):
                            act.wait_ge(s_r1, t + 1)
                            nc.scalar.activation(v_parts(t)[:, :, DH:2 * DH], heads(v_res[:, u, :]), ACT.Copy).then_inc(s_v1, 1)
                            act.wait_ge(s_tq, t + 1)
                            src = bank[6 + u][:, 0:turns * P].rearrange("p (k q) -> p k q", q=P)
                            if layer == 0:
                                nc.scalar.activation(tile_cols(qT, t), src[:, 0:KT], ACT.Copy)
                                nc.scalar.activation(tile_cols(kT, t), src[:, KT:2 * KT], ACT.Copy).then_inc(s_qT, 1)
                            else:
                                nc.scalar.activation(tile_cols(qT, t), src, ACT.Copy, scale=0.5).then_inc(s_qT, 1)
                    steps(act, step, PEELED, TURN)

                @block.tensor
                def _(pe):
                    if layer == 0:
                        pe.wait_ge(s_project, 16 * PROJECT_LOADS)

                    def step(tau, u):
                        t = tau - 1
                        if exists(t):
                            pe.wait_ge(s_xn, t + 1)
                            if reuses(t):
                                pe.wait_ge(s_xT, t - 1)
                            for k in range(KT):
                                mm = nc.tensor.transpose(bank[1 - u][:, P * k:P * (k + 1)], xn[:, 1 - u, P * k:P * (k + 1)], ident[:, :])
                            mm.then_inc(s_tx, 1)
                        t = tau - PRODUCT
                        if exists(t):
                            pe.wait_ge(s_xT, t + 1)
                            if layer == 0:
                                if reuses(t):
                                    pe.wait_ge(s_qkb, t - 1)
                                for k in range(KT):
                                    mm = nc.tensor.matmul(bank[4 + u][:, :], xT[:, u, P * k:P * (k + 1)], w[:, k, 0:2 * D],
                                                          start=(k == 0), stop=(k == KT - 1))
                                mm.then_inc(s_qk, 1)
                            if reuses(t):
                                pe.wait_ge(s_vb, t - 1)
                            for k in range(KT):
                                mm = nc.tensor.matmul(bank[2 + u][:, 0:D], xT[:, u, P * k:P * (k + 1)], w[:, k, qk_cols:qk_cols + D],
                                                      start=(k == 0), stop=(k == KT - 1))
                            mm.then_inc(s_v, 1)
                        t = tau - TURN
                        if exists(t):
                            pe.wait_ge(s_turned, t + 1)
                            if reuses(t):
                                pe.wait_ge(s_qT, t - 1)
                            for k in range(turns):
                                mm = nc.tensor.transpose(bank[6 + u][:, P * k:P * (k + 1)], turned[:, u, P * k:P * (k + 1)], ident[:, :])
                            mm.then_inc(s_tq, 1)
                    steps(pe, step, PEELED, TURN)

                @block.vector
                def _(dve):
                    if layer == 0:
                        dve.wait_ge(s_project, 16 * PROJECT_LOADS)

                    def step(tau, u):
                        t = tau - ROTATE
                        if exists(t) and layer == 0:
                            dve.wait_ge(s_qkb, t + 1)
                            if reuses(t):
                                dve.wait_ge(s_tq, t - 1)
                            x = qk[:, 1 - u, :].rearrange("p (a h j w) -> p a h j w", a=2, h=HEADS, w=2)
                            o = qk_rot[:, 1 - u, :].rearrange("p (a h j w) -> p a h j w", a=2, h=HEADS, w=2)
                            s = sin_sb[:, bass.ds(t, 1), :].rearrange("p x (a j w) -> p (x a) j w", a=2, w=2)
                            for a in range(2):
                                for w2 in range(2):
                                    sw = s[:, a, :, w2].unsqueeze(1).broadcast_to([P, HEADS, DH // 2])
                                    last = nc.vector.tensor_tensor(o[:, a, :, :, w2], x[:, a, :, :, 1 - w2], sw, ALU.mult)
                            last.then_inc(s_sin, 1)
                            dve.wait_ge(s_sin, t + 1)
                            dve.wait_ge(s_cos, t + 1)
                            nc.vector.tensor_tensor(qk_rot[:, 1 - u, :], qk_rot[:, 1 - u, :], qk_cos[:, 1 - u, :], ALU.add).then_inc(s_rot, 1)
                        t = tau - PRODUCT
                        if exists(t):
                            if layer == 0:
                                dve.wait_ge(s_qk, t + 1)
                                if reuses(t):
                                    dve.wait_ge(s_cos, t - 1)
                                nc.vector.tensor_tensor(qk[:, u, :], bank[4 + u][:, :], bias[:, 0:2 * D], ALU.add).then_inc(s_qkb, 1)
                            dve.wait_ge(s_v, t + 1)
                            if reuses(t):
                                dve.wait_ge(s_r1, t - 1)
                                if layer == 1:
                                    dve.wait_ge(s_tq, t - 1)
                            nc.vector.tensor_tensor(v[:, u, :], bank[2 + u][:, 0:D], bias[:, qk_cols:qk_cols + D], ALU.add).then_inc(s_vb, 1)
                    steps(dve, step, PEELED, TURN)

                @block.sync
                def _(sp):
                    if layer == 0:
                        load_late_weights(sp)
                    sp.wait_ge(s_one, 1)

                    def body(i):
                        sp.wait_ge(s_v2, PAIR * i + PAIR)
                        dst = v_dram[bass.ds(PAIR * P * i, PAIR * P), :].rearrange("(u p) c -> p u c", p=P)
                        sp.dma_start(dst, v_all[:, bass.ds(PAIR * i, PAIR), :]).then_inc(s_st, 16)
                    for_each(sp, PASSES, body)
                    sp.wait_ge(s_st, 16 * PASSES)

        select = wqkv_sb[:, :, :].rearrange("p k c -> p (k c)")[:, 0:EXPERTS * P // 2].bitcast(BF16).rearrange("p (e q) -> p e q", e=EXPERTS)

        def build_select(pool, s_sel):
            pool.memset(select[:, :, :], 0.0).then_inc(s_sel, 1)
            for a in range(3):
                pool.wait_ge(s_sel, a + 1)
                pool.affine_select(out=select[:, :, :], in_=select[:, :, :], compare_op=ALU.not_equal, fill=1.0, base=-EXPERTS * a,
                                   pattern=[[-1, EXPERTS], [0, P]], channel_multiplier=1).then_inc(s_sel, 1)

        def attention_phase(layer):
            n = f"a{layer}_"
            keys = kT if layer == 0 else qT
            s_zero, s_qzero = sem(n + "zero"), sem(n + "qzero")
            s_ld = [sem(n + f"ld{u}") for u in range(PAIR)]
            s_qm = sem(n + "qm")
            s_s = sem(n + "s")
            s_max = sem(n + "max")
            s_exp = sem(n + "exp")
            s_t = sem(n + "t")
            s_hi, s_lo = sem(n + "hi"), sem(n + "lo")
            s_pl = sem(n + "pl")
            s_vd = sem(n + "vd")
            s_o, s_oe = sem(n + "o"), sem(n + "oe")
            s_r, s_rc = sem(n + "r"), sem(n + "rc")
            s_rd, s_ro = sem(n + "rd"), sem(n + "ro")
            s_oo = sem(n + "oo")
            s_pchain = sem(n + "pchain")
            s_st = [sem(n + f"st{u}") for u in range(PAIR)]
            s_sel = sem(n + "sel")
            passes = IMAGES // PAIR
            LOADS = 4
            hc = HH * VC
            LAG = 2
            turn_needs = [2, 3, 4, 6, 6, 6]

            def o_rows(b, lo, count):
                if layer == 0:
                    return o_dram[bass.ds(SEQ * b + lo, count), :]
                flat = o_dram[bass.ds(SEQ * b, SEQ), :].rearrange("s c -> (s c)")
                return flat.rearrange("(h s d) -> s h d", h=HEADS, d=DH)[lo:lo + count]

            with nc.Block() as block:
                @block.sync
                def _(sp):
                    def load(b, u):
                        rows, rem = v_dram[bass.ds(SEQ * b, P), :], v_dram[bass.ds(SEQ * b + P, REM), :]
                        sp.dma_start(v_main[:, u, :], rows).then_inc(s_ld[u], 16)
                        sp.dma_start(v_rem[0:REM, u, :], rem).then_inc(s_ld[u], 16)
                        sp.dma_start(v_rem[32:32 + REM, u, :], rem).then_inc(s_ld[u], 16)
                        sp.dma_start(v_rep[0:HR, u, :], rem.unsqueeze(0).broadcast_to([HH, REM, HEADS * VC])).then_inc(s_ld[u], 16)

                    def store(b, u):
                        sp.wait_ge(s_oo, b + 1)
                        src, rsrc = o_out[:, u, :], r_out[0:REM, u, :]
                        if layer == 1:
                            src, rsrc = (x.rearrange("p (h d) -> p h d", d=DH) for x in (src, rsrc))
                        sp.dma_start(o_rows(b, 0, P), src).then_inc(s_st[u], 16)
                        sp.wait_ge(s_ro, b + 1)
                        sp.dma_start(o_rows(b, P, REM), rsrc).then_inc(s_st[u], 16)

                    sp.wait_ge(s_zero, 2)
                    for u in range(PAIR):
                        load(u, u)

                    def body(i, last=False):
                        for u in range(PAIR):
                            b = PAIR * i + u
                            sp.wait_ge(s_r, b + 1)
                            if not last:
                                load(b + PAIR, u)
                            store(b, u)
                    body(0)
                    with sp.Fori(1, passes - 1) as i:
                        body(i)
                    body(passes - 1, last=True)
                    for u in range(PAIR):
                        sp.wait_ge(s_st[u], 32 * passes)

                @block.gpsimd
                def _(pool):
                    pool.memset(q_rem[:, :, :, :], 0.0).then_inc(s_qzero, 1)
                    pool.wait_ge(s_qzero, 1)

                    def masks(b, u, first):
                        if not first:
                            pool.wait_ge(s_s, SGROUPS * b - SGROUPS * (PAIR - 1))
                        m = mask_sb[:, :]
                        for k in range(KT):
                            q = qT[:, k, bass.ds(SEQ * b, P)].unsqueeze(1).broadcast_to([P, HH, P])
                            nc.gpsimd.tensor_tensor(q_masked[:, u, k], q, m.unsqueeze(2).broadcast_to([P, HH, P]), ALU.mult).then_inc(s_qm, 1)
                        for k in range(KT):
                            q = qT[:, k, bass.ds(SEQ * b + P, REM)].unsqueeze(1).broadcast_to([P, HH, REM])
                            o = q_rem[:, u, k, 0:HR].rearrange("p (h q) -> p h q", h=HH)
                            nc.gpsimd.tensor_tensor(o, q, m.unsqueeze(2).broadcast_to([P, HH, REM]), ALU.mult).then_inc(s_qm, 1)

                    def last_keys(b, u, first):
                        pool.wait_ge(s_exp, SGROUPS * b + SGROUPS)
                        if not first:
                            pool.wait_ge(s_t, TGROUPS * b - TGROUPS * (PAIR - 1))
                        one = ones[:, 0:1].unsqueeze(2).broadcast_to([P, HEADS, REM])
                        nc.gpsimd.tensor_tensor(prob_last[:, u, :].rearrange("p (h k) -> p h k", k=REM), prob[:, u, 0:HEADS, P:SEQ], one,
                                                ALU.mult).then_inc(s_pl, 1)

                    def diagonal(b, u):
                        pool.wait_ge(s_ld[u], (16 * LOADS // PAIR) * (b - u) + 16 * LOADS)
                        m = rmask_bf[:, :].unsqueeze(2).broadcast_to([HR, HH, VC])
                        for k in range(KT):
                            o = v_diag[0:HR, u, hc * k:hc * (k + 1)].rearrange("p (h c) -> p h c", c=VC)
                            x = v_rep[0:HR, u, hc * k:hc * (k + 1)].rearrange("p (h c) -> p h c", c=VC)
                            c = nc.gpsimd.tensor_tensor(o, x, m, ALU.mult)
                        c.then_inc(s_vd, 1)

                    def first_rows(b, u):
                        pool.wait_ge(s_oe, KT * b + KT)
                        if not (isinstance(b, int) and b < PAIR):
                            pool.wait_ge(s_st[u], 16 * b - 16 * u)
                        den = o_den[:, :].unsqueeze(2).broadcast_to([P, HEADS, DH])
                        nc.gpsimd.tensor_tensor(o_out[:, u, :].rearrange("p (h d) -> p h d", d=DH),
                                                o_sum[:, :].rearrange("p (h d) -> p h d", d=DH), den, ALU.mult).then_inc(s_oo, 1)

                    def last_rows(b, u):
                        pool.wait_ge(s_rc, b + 1)
                        parts = r_raw[0:REM, :].rearrange("p (h c) -> p h c", c=VC)
                        total = r_sum[0:REM, :].rearrange("p (h c) -> p h c", c=DH)
                        nc.gpsimd.tensor_tensor(total, parts[:, :, 0:DH], parts[:, :, DH:2 * DH], ALU.add).then_inc(s_pchain, 1)
                        pool.wait_ge(s_pchain, 2 * b + 1)
                        nc.gpsimd.tensor_tensor(total, total, parts[:, :, 2 * DH:3 * DH], ALU.add).then_inc(s_pchain, 1)
                        pool.wait_ge(s_pchain, 2 * b + 2)
                        pool.wait_ge(s_rd, b + 1)
                        if not (isinstance(b, int) and b < PAIR):
                            pool.wait_ge(s_st[u], 16 * b - 16 * u)
                        o = r_out[0:REM, u, :].rearrange("p (h c) -> p h c", c=DH)
                        den = r_den[0:REM, :].unsqueeze(2).broadcast_to([REM, HEADS, DH])
                        nc.gpsimd.tensor_tensor(o, total, den, ALU.mult).then_inc(s_ro, 1)

                    for u in range(PAIR):
                        masks(u, u, True)
                    if layer == 0:
                        build_select(pool, s_sel)

                    def body(i, last=False):
                        for u in range(PAIR):
                            last_keys(PAIR * i + u, u, is_first(i))
                            diagonal(PAIR * i + u, u)
                            if not last:
                                masks(PAIR * i + PAIR + u, u, False)
                            if not (is_first(i) and u == 0):
                                first_rows(PAIR * i + u - 1, 1 - u)
                                last_rows(PAIR * i + u - 1, 1 - u)
                    body(0)
                    body(1)
                    with pool.Fori(2, passes - 1) as i:
                        body(i)
                    body(passes - 1, last=True)
                    first_rows(IMAGES - 1, 1)
                    last_rows(IMAGES - 1, 1)

                @block.tensor
                def _(pe):
                    def scores(b, u, g, first):
                        n = SGROUPS * b + g
                        if not (first and u == 0 and g < 2):
                            pe.wait_ge(s_exp, n - 1)
                        for j in range(3):
                            s = 3 * g + j
                            k = s // HH if s < HEADS else s - HEADS
                            q = q_masked[:, u, k, s % HH, :] if s < HEADS else q_rem[:, u, k, :]
                            mm = nc.tensor.matmul(bank[g % 2][:, SEQ * j:SEQ * (j + 1)], q, keys[:, k, bass.ds(SEQ * b, SEQ)],
                                                  start=True, stop=True)
                        mm.then_inc(s_s, 1)

                    def turn(b, u, g, first):
                        n = TGROUPS * b + g
                        pe.wait_ge(s_exp, SGROUPS * b + turn_needs[g])
                        if not (first and u == 0 and g < 2):
                            pe.wait_ge(s_lo, n - 1)
                        ps = bank[2 + g % 2]
                        if g < 4:
                            for j in range(4):
                                mm = nc.tensor.transpose(ps[:, P * j:P * (j + 1)], prob[:, u, 4 * g + j, 0:P], ident[:, :])
                        elif g == 4:
                            for k in range(KT):
                                nc.tensor.transpose(ps[:, P * k:P * (k + 1)], prob[:, u, HEADS + k, 0:P], ident[:, :])
                            pe.wait_ge(s_pl, b + 1)
                            for k in range(KT):
                                mm = nc.tensor.transpose(ps[0:HR, P * (KT + k):P * (KT + k + 1)],
                                                         prob_last[:, u, HR * k:HR * (k + 1)], ident[:, :])
                        else:
                            for k in range(KT):
                                mm = nc.tensor.transpose(ps[0:REM, P * k:P * (k + 1)], prob[:, u, HEADS + k, P:SEQ], ident[:, :])
                        mm.then_inc(s_t, 1)

                    def values(b, u, g):
                        first = isinstance(b, int) and b == 0
                        n = TGROUPS * b + g
                        pe.wait_ge(s_lo, n + 1)
                        for hd in range(4 * g, 4 * g + 4) if g < 4 else ():
                            k, j = hd // HH, hd % HH
                            if j == 0 and not first:
                                pe.wait_ge(s_oe, KT * b + k - 1)
                            for a in range(2):
                                nc.tensor.matmul(bank[4 + k][:, VC * j:VC * (j + 1)], pT[:, a, hd, :], v_main[:, u, VC * hd:VC * (hd + 1)],
                                                 start=(j == 0 and a == 0), stop=False, skip_group_check=True)
                        if g == 4:
                            pe.wait_ge(s_vd, b + 1)
                            for k in range(KT):
                                for a in range(2):
                                    mm = nc.tensor.matmul(bank[4 + k][:, 0:hc], pT_rem[0:HR, a, KT + k, :], v_diag[0:HR, u, hc * k:hc * (k + 1)],
                                                          start=False, stop=(a == 1), skip_group_check=True)
                            mm.then_inc(s_o, 1)
                            if not first:
                                pe.wait_ge(s_rc, b)
                            for hd in range(HEADS):
                                k, j = hd // HH, hd % HH
                                for a in range(2):
                                    nc.tensor.matmul(bank[6 + k][0:REM, VC * j:VC * (j + 1)], pT_rem[:, a, k, REM * j:REM * (j + 1)],
                                                     v_main[:, u, VC * hd:VC * (hd + 1)], start=(j == 0 and a == 0), stop=False,
                                                     skip_group_check=True)
                        if g == 5:
                            for hd in range(HEADS):
                                k, j = hd // HH, hd % HH
                                mm = nc.tensor.matmul(bank[6 + k][0:REM, VC * j:VC * (j + 1)], pT_corner[:, k, REM * j:REM * (j + 1)],
                                                      v_rem[:, u, VC * hd:VC * (hd + 1)], start=False, stop=(j == HH - 1),
                                                      skip_group_check=True)
                            mm.then_inc(s_r, 1)

                    pe.wait_ge(s_zero, 2)

                    for g, masked in enumerate((1, 1, 2, 2, 2, 4)):
                        pe.wait_ge(s_qm, masked)
                        scores(0, 0, g, True)

                    def body(i, last=False):
                        first = is_first(i)
                        for u in range(PAIR):
                            b = PAIR * i + u
                            ahead = not (last and u == PAIR - 1)
                            if ahead:
                                pe.wait_ge(s_qm, 4 * b + 8)
                            for g in range(TGROUPS):
                                turn(b, u, g, first)
                                if ahead:
                                    scores(b + 1, 1 - u, g, False)
                                if g < LAG:
                                    if not (first and u == 0):
                                        values(b - 1, 1 - u, TGROUPS - LAG + g)
                                    continue
                                if g == LAG:
                                    pe.wait_ge(s_ld[u], 16 * LOADS * i + 16 * LOADS)
                                values(b, u, g - LAG)
                    body(0)
                    with pe.Fori(1, passes - 1) as i:
                        body(i)
                    body(passes - 1, last=True)
                    for g in range(TGROUPS - LAG, TGROUPS):
                        values(IMAGES - 1, 1, g)

                @block.scalar
                def _(act):
                    def exps(b, u, g, first):
                        if g == 0 and not first:
                            act.wait_ge(s_t, TGROUPS * b - TGROUPS * (PAIR - 1))
                        act.wait_ge(s_max, SGROUPS * b + g + 1)
                        for j in range(3):
                            s = 3 * g + j
                            e = nc.scalar.activation(prob[:, u, s, :], bank[g % 2][:, SEQ * j:SEQ * (j + 1)], ACT.Exp,
                                                     bias=neg_max[:, u, s:s + 1])
                        e.then_inc(s_exp, 1)

                    def high(b, u, g):
                        act.wait_ge(s_t, TGROUPS * b + g + 1)
                        ps = bank[2 + g % 2]
                        if g < 4:
                            c = nc.scalar.activation(pT[:, 0, 4 * g:4 * g + 4, :], ps[:, :].rearrange("p (h q) -> p h q", q=P), ACT.Copy)
                        elif g == 4:
                            both = ps[:, :].rearrange("p (n q) -> p n q", q=P)
                            nc.scalar.activation(pT_rem[:, 0, 0:KT, :], both[:, 0:KT], ACT.Copy)
                            c = nc.scalar.activation(pT_rem[0:HR, 0, KT:2 * KT, :], both[0:HR, KT:2 * KT], ACT.Copy)
                        else:
                            if not (isinstance(b, int) and b == 0):
                                act.wait_ge(s_r, b)
                            c = nc.scalar.activation(pT_corner[0:REM, :, :], ps[0:REM, 0:KT * P].rearrange("p (n q) -> p n q", q=P), ACT.Copy)
                        c.then_inc(s_hi, 1)

                    def last_rows(b, k):
                        if k == 0:
                            act.wait_ge(s_r, b + 1)
                            if not (isinstance(b, int) and b == 0):
                                act.wait_ge(s_ro, b)
                        c = nc.scalar.activation(r_raw[0:REM, hc * k:hc * (k + 1)], bank[6 + k][0:REM, 0:hc], ACT.Copy)
                        if k == KT - 1:
                            c.then_inc(s_rc, 1)

                    for g in range(SGROUPS):
                        exps(0, 0, g, True)

                    def body(i, last=False):
                        first = is_first(i)
                        for u in range(PAIR):
                            b = PAIR * i + u
                            for g in range(TGROUPS):
                                high(b, u, g)
                                if not (last and u == PAIR - 1):
                                    exps(b + 1, 1 - u, g, first and u == 0)
                                if g == 2 and not (first and u == 0):
                                    for k in range(KT):
                                        last_rows(b - 1, k)
                    body(0)
                    with act.Fori(1, passes - 1) as i:
                        body(i)
                    body(passes - 1, last=True)
                    for k in range(KT):
                        last_rows(IMAGES - 1, k)

                @block.vector
                def _(dve):
                    nc.vector.memset(v_rem, 0.0).then_inc(s_zero, 1)
                    nc.vector.memset(pT_corner, 0.0).then_inc(s_zero, 1)
                    dve.wait_ge(s_zero, 2)

                    def maxima(b, u, g):
                        dve.wait_ge(s_s, SGROUPS * b + g + 1)
                        nc.vector.tensor_reduce(neg_max[:, u, 3 * g:3 * g + 3], bank[g % 2][:, 0:3 * SEQ].rearrange("p (n k) -> p n k", n=3),
                                                AX.X, ALU.max, negate=True).then_inc(s_max, 1)

                    def low(b, u, g):
                        dve.wait_ge(s_hi, TGROUPS * b + g + 1)
                        ps = bank[2 + g % 2][:, :].rearrange("p (n q) -> p n q", q=P)
                        if g < 4:
                            c = nc.vector.tensor_tensor(pT[:, 1, 4 * g:4 * g + 4, :], ps, pT[:, 0, 4 * g:4 * g + 4, :], ALU.subtract)
                        elif g == 4:
                            nc.vector.tensor_tensor(pT_rem[:, 1, 0:KT, :], ps[:, 0:KT], pT_rem[:, 0, 0:KT, :], ALU.subtract)
                            c = nc.vector.tensor_tensor(pT_rem[0:HR, 1, KT:2 * KT, :], ps[0:HR, KT:2 * KT], pT_rem[0:HR, 0, KT:2 * KT, :], ALU.subtract)
                        else:
                            c = nc.vector.tensor_tensor(pT_corner[32:32 + REM, :, :], ps[0:REM, 0:KT], pT_corner[0:REM, :, :], ALU.subtract)
                        c.then_inc(s_lo, 1)

                    def rows(b, k):
                        if k == 0:
                            dve.wait_ge(s_o, b + 1)
                            if not (isinstance(b, int) and b == 0):
                                dve.wait_ge(s_oo, b)
                        parts = bank[4 + k][:, 0:hc].rearrange("p (h c) -> p h c", c=VC)
                        nc.vector.reciprocal(o_den[:, HH * k:HH * (k + 1)], parts[:, :, VC - 1])
                        three = parts[:, :, 0:3 * DH].rearrange("p h (a d) -> p h d a", a=3)
                        nc.vector.tensor_reduce(o_sum[:, P * k:P * (k + 1)].rearrange("p (h d) -> p h d", d=DH),
                                                three, AX.X, ALU.add).then_inc(s_oe, 1)

                    def last_sums(b):
                        dve.wait_ge(s_rc, b + 1)
                        nc.vector.reciprocal(r_den[0:REM, :], r_raw[0:REM, :].rearrange("p (h c) -> p h c", c=VC)[:, :, VC - 1]).then_inc(s_rd, 1)

                    for g in range(SGROUPS):
                        maxima(0, 0, g)

                    def body(i, last=False):
                        first = is_first(i)
                        for u in range(PAIR):
                            b = PAIR * i + u
                            for g in range(TGROUPS):
                                if not (last and u == PAIR - 1):
                                    maxima(b + 1, 1 - u, g)
                                low(b, u, g)
                                if g in (0, 2) and not (first and u == 0):
                                    rows(b - 1, g // 2)
                                if g == 4 and not (first and u == 0):
                                    last_sums(b - 1)
                    body(0)
                    body(1)
                    with dve.Fori(2, passes - 1) as i:
                        body(i)
                    body(passes - 1, last=True)
                    for k in range(KT):
                        rows(IMAGES - 1, k)
                    last_sums(IMAGES - 1)

        def output_phase(layer):
            n = f"o{layer}_"
            s_ld = [sem(n + f"ld{c}") for c in range(3)]
            s_t, s_T, s_mm, s_bias, s_add = (sem(n + x) for x in ("t", "T", "mm", "bias", "add"))
            s_st, s_mv, s_var, s_rstd, s_shift = (sem(n + x) for x in ("stats", "mv", "var", "rstd", "shift"))
            o_in = region[:, experts_words:experts_words + TILES * D].rearrange("p (t c) -> p t c", t=TILES)
            BATCH = TILES // 3
            batches = TILES // BATCH
            LAG = 4
            AHEAD = 7
            with nc.Block() as block:
                @block.sync
                def _(sp):
                    for c in range(batches):
                        rows = o_dram[BATCH * P * c:BATCH * P * (c + 1), :].rearrange("(t p) c -> p t c", p=P)
                        sp.dma_start(o_in[:, BATCH * c:BATCH * (c + 1), :], rows).then_inc(s_ld[c], 16)
                    if layer == 0:
                        for k in range(KT):
                            sp.dma_start(gate_up(raw)[:, k], w_gu_t[P * k:P * (k + 1)]).then_inc(s_moe[k], 16)
                        sp.dma_start(downs(raw), w_down_t).then_inc(s_moe[KT], 16)

                @block.gpsimd
                def _(pool):
                    pool.wait_ge(s_late, 16 * LATE_LOADS)

                    def step(tau, u):
                        t = tau
                        if exists(t):
                            nc.gpsimd.tensor_tensor(col(t)(h), col(t)(h), bo_sb[layer][:, :], ALU.add).then_inc(s_bias, 1)
                        t = tau - AHEAD
                        if exists(t):
                            raise_power(pool, t, 1, s_var, t + 1, s_rstd)
                    steps(pool, step, 4, AHEAD)

                @block.tensor
                def _(pe):
                    pe.wait_ge(s_late, 16 * LATE_LOADS)

                    def turn(t, u):
                        if reuses(t):
                            pe.wait_ge(s_T, t - 1)
                        for k in range(KT):
                            mm = nc.tensor.transpose(bank[u][:, P * k:P * (k + 1)], o_in[:, t, P * k:P * (k + 1)], ident[:, :])
                        mm.then_inc(s_t, 1)

                    def product(t, u):
                        pe.wait_ge(s_T, t + 1)
                        if reuses(t):
                            pe.wait_ge(s_add, t - 1)
                        for k in range(KT):
                            mm = nc.tensor.matmul(bank[2 + u][:, 0:D], xT[:, u, P * k:P * (k + 1)], wo_sb[layer][:, k, :],
                                                  start=(k == 0), stop=(k == KT - 1))
                        mm.then_inc(s_mm, 1)

                    for t in range(TILES):
                        pe.wait_ge(s_ld[t // BATCH], 16)
                        turn(t, t % PAIR)
                        if t >= 1:
                            product(t - 1, (t - 1) % PAIR)
                    product(TILES - 1, (TILES - 1) % PAIR)

                @block.scalar
                def _(act):
                    def body(i):
                        for u in range(PAIR):
                            t = PAIR * i + u
                            act.wait_ge(s_t, t + 1)
                            if not is_first(i):
                                act.wait_ge(s_mm, t - 1)
                            nc.scalar.activation(xT[:, u, :], bank[u][:, 0:D], ACT.Copy).then_inc(s_T, 1)
                    for_each(act, PASSES, body)

                @block.vector
                def _(dve):
                    def step(tau, u):
                        t = tau
                        if exists(t):
                            dve.wait_ge(s_mm, t + 1)
                            dve.wait_ge(s_bias, t + 1)
                            nc.vector.tensor_tensor(col(t)(h), bank[2 + u][:, 0:D], col(t)(h), ALU.add).then_inc(s_add, 1)
                        t = tau - 4
                        if exists(t):
                            shifts(dve, t, u, 1, s_rstd, t + 1, s_shift)
                        t = tau - 3
                        if exists(t):
                            variances(dve, t, 1 - u, 1, s_mv, t + 1, s_var)
                        t = tau - 2
                        if exists(t):
                            if reuses(t):
                                dve.wait_ge(s_shift, t - 1)
                            means(dve, u, 1, s_st, t + 1, s_mv)
                        t = tau - 1
                        if exists(t):
                            dve.wait_ge(s_add, t + 1)
                            carry()
                            nc.vector.bn_stats(stats[:, 1 - u, :], col(t)(h)).then_inc(s_st, 1)
                    steps(dve, step, 3, LAG)
                    dve.wait_ge(s_shift, TILES)

        w_rows = tables[:, :, :, :].rearrange("p a t c -> p (a t c)").bitcast(BF16)


        def route_phase():
            s_chain = sem("r_chain")
            s_zero, s_xlo, s_whi, s_wlo = (sem("r_" + x) for x in ("zero", "xlo", "whi", "wlo"))
            s_xn, s_tx, s_xT, s_res = sem("r_xn"), sem("r_tx"), sem("r_xT"), sem("r_res")
            s_mm, s_sig, s_w, s_tw, s_wT = (sem("r_" + x) for x in ("mm", "sig", "w", "tw", "wT"))
            at = [0]

            def cut(n):
                at[0] += n
                return work[:, at[0] - n:at[0]]
            BATCH = TILES // 3
            batches = TILES // BATCH
            PEELED, LAG = 2, 2
            scores_all = cut(TILES * EXPERTS)
            w3 = cut(TILES * P // 2).bitcast(BF16).rearrange("p (t c) -> p t c", t=TILES)
            choice = cut(BATCH * EXPERTS)
            hi2 = cut(BATCH * GROUPS * 2)
            lo2 = cut(BATCH * GROUPS * 2)
            top1, mid, low = cut(BATCH * GROUPS), cut(BATCH * GROUPS), cut(BATCH * GROUPS)
            group_pad = cut(BATCH * 8).rearrange("p (t k) -> p t k", t=BATCH)
            gval = cut(BATCH * 8).rearrange("p (t k) -> p t k", t=BATCH)
            gidx = cut(BATCH * 8).bitcast(U32).rearrange("p (t k) -> p t k", t=BATCH)
            ghot = cut(BATCH * GROUPS * 2).rearrange("p (t g k) -> p t g k", t=BATCH, k=2)
            gmask = cut(BATCH * GROUPS)
            kept = cut(BATCH * EXPERTS)
            kval = cut(BATCH * 8).rearrange("p (t k) -> p t k", t=BATCH)
            kidx = cut(BATCH * 8).bitcast(U32).rearrange("p (t k) -> p t k", t=BATCH)
            khot = cut(BATCH * EXPERTS * TOPK).rearrange("p (t e k) -> p t e k", t=BATCH, k=TOPK)
            chosen = cut(BATCH * EXPERTS)
            weight = cut(BATCH * EXPERTS)
            den = cut(BATCH)
            rest = cut(BATCH * EXPERTS)
            assert at[0] <= 12 * D

            def by_tile(x):
                return x.rearrange("p (t e) -> p t e", t=BATCH)

            def low_weights(eng, ops, n):
                eng.wait_ge(s_whi, n + 1)
                ops.tensor_tensor(low_pieces[n], raw_pieces[n], high_pieces[n].bitcast(F32), ALU.subtract).then_inc(s_wlo, 1)

            with nc.Block() as block:
                @block.gpsimd
                def _(pool):
                    pool.memset(w3[:, :, :], 0.0).then_inc(s_zero, 1)
                    pool.memset(group_pad[:, :, :], LOWEST).then_inc(s_zero, 1)

                    def low_rows(i):
                        for u in range(PAIR):
                            t = PAIR * i + u
                            pool.wait_ge(s_res, t + 1)
                            x = xT[:, u, :].rearrange("p (k q) -> p k q", q=P)
                            nc.gpsimd.tensor_tensor(tile_cols(x_lo, t), x, tile_cols(x_hi, t).bitcast(F32), ALU.subtract).then_inc(s_xlo, 1)
                    for_each(pool, PASSES, low_rows)
                    low_weights(pool, nc.gpsimd, 1)

                @block.scalar
                def _(act):
                    def step(tau, u):
                        t = tau
                        if exists(t):
                            if reuses(t):
                                act.wait_ge(s_tx, t - 1)
                            nc.scalar.activation(xn[:, u, :], col(t)(h), ACT.Identity, bias=shift[:, bass.ds(t, 1)],
                                                 scale=rstd[:, bass.ds(t, 1)]).then_inc(s_xn, 1)
                        t = tau - 1
                        if exists(t):
                            act.wait_ge(s_tx, t + 1)
                            if reuses(t):
                                act.wait_ge(s_mm, t - 1)
                                act.wait_ge(s_xlo, t - 1)
                            nc.scalar.activation(xT[:, 1 - u, :], bank[1 - u][:, 0:D], ACT.Copy).then_inc(s_xT, 1)
                            nc.scalar.activation(tile_cols(x_hi, t), bank[1 - u][:, 0:D].rearrange("p (k q) -> p k q", q=P),
                                                 ACT.Copy).then_inc(s_res, 1)
                        t = tau - 2
                        if exists(t):
                            act.wait_ge(s_mm, t + 1)
                            nc.scalar.activation(scores_all[:, bass.ds(EXPERTS * t, EXPERTS)], bank[2 + u][:, 0:EXPERTS],
                                                 ACT.Sigmoid).then_inc(s_sig, 1)
                    def high_weights(n):
                        act.wait_ge(s_moe[n], 16)
                        nc.scalar.activation(high_pieces[n], raw_pieces[n], ACT.Copy).then_inc(s_whi, 1)

                    high_weights(0)
                    steps(act, step, PEELED, LAG)
                    for n in range(1, PIECES):
                        high_weights(n)

                    def copy_out(c):
                        for j in range(BATCH):
                            t = BATCH * c + j
                            act.wait_ge(s_tw, t + 1)
                            src = bank[4 + j % 2][:, :].bitcast(BF16)[:, 0:P]
                            nc.scalar.activation(w_rows[:, bass.ds(P * t, P)], src, ACT.Copy).then_inc(s_wT, 1)
                    for_each(act, batches, copy_out)

                @block.tensor
                def _(pe):
                    def step(tau, u):
                        t = tau
                        if exists(t):
                            pe.wait_ge(s_xn, t + 1)
                            if reuses(t):
                                pe.wait_ge(s_res, t - 1)
                            for k in range(KT):
                                mm = nc.tensor.transpose(bank[u][:, P * k:P * (k + 1)], xn[:, u, P * k:P * (k + 1)], ident[:, :])
                            mm.then_inc(s_tx, 1)
                        t = tau - 1
                        if exists(t):
                            pe.wait_ge(s_xT, t + 1)
                            if reuses(t):
                                pe.wait_ge(s_sig, t - 1)
                            for k in range(KT):
                                mm = nc.tensor.matmul(bank[3 - u][:, 0:EXPERTS], xT[:, 1 - u, P * k:P * (k + 1)], wgate_sb[:, k, :],
                                                      start=(k == 0), stop=(k == KT - 1))
                            mm.then_inc(s_mm, 1)
                    steps(pe, step, PEELED, LAG)

                    def turn(c):
                        for j in range(BATCH):
                            t = BATCH * c + j
                            pe.wait_ge(s_w, c + 1)
                            if not (is_first(c) and j < 2):
                                pe.wait_ge(s_wT, t - 1)
                            nc.tensor.transpose(bank[4 + j % 2][:, :].bitcast(BF16)[:, 0:P],
                                                w3[:, bass.ds(t, 1), :].rearrange("p a c -> p (a c)"), ident_bf[:, :]).then_inc(s_tw, 1)
                    for_each(pe, batches, turn)

                @block.vector
                def _(dve):
                    chain = Chain(dve, s_chain)
                    dve.wait_ge(s_zero, 2)
                    links = [0]

                    def body(c):
                        chain.n, chain.base = 0, c * links[0]
                        V = nc.vector
                        tt = V.tensor_tensor
                        scores = scores_all[:, bass.ds(BATCH * EXPERTS * c, BATCH * EXPERTS)]
                        w_part = w3[:, bass.ds(BATCH * c, BATCH), 0:3 * EXPERTS].rearrange("p t (a e) -> p t a e", a=3)
                        dve.wait_ge(s_sig, BATCH * c + BATCH)
                        eb = ebias_sb[:, :].unsqueeze(1).broadcast_to([P, BATCH, EXPERTS])
                        chain.link(tt(by_tile(choice), by_tile(scores), eb, ALU.add))
                        four = choice.rearrange("p (g x) -> p g x", x=4)
                        a2, b2 = (x.rearrange("p (g x) -> p g x", x=2) for x in (hi2, lo2))
                        tt(a2, four[:, :, 0:2], four[:, :, 2:4], ALU.max)
                        chain.link(tt(b2, four[:, :, 0:2], four[:, :, 2:4], ALU.min))
                        tt(top1, a2[:, :, 0], a2[:, :, 1], ALU.max)
                        tt(mid, a2[:, :, 0], a2[:, :, 1], ALU.min)
                        chain.link(tt(low, b2[:, :, 0], b2[:, :, 1], ALU.max))
                        chain.link(tt(mid, mid, low, ALU.max))
                        g4 = group_pad[:, :, 0:GROUPS]
                        chain.link(tt(g4, top1.rearrange("p (t g) -> p t g", t=BATCH), mid.rearrange("p (t g) -> p t g", t=BATCH), ALU.add))
                        carry()
                        for u in range(BATCH):
                            last = V.max(gval[:, u, :], group_pad[:, u, :])
                        chain.link(last)
                        carry()
                        for u in range(BATCH):
                            last = V.max_index(gidx[:, u, :], gval[:, u, :], group_pad[:, u, :])
                        chain.link(last)
                        io = iota[:, 0:GROUPS].unsqueeze(1).unsqueeze(3).broadcast_to([P, BATCH, GROUPS, 2])
                        ix = gidx[:, :, 0:2].unsqueeze(2).broadcast_to([P, BATCH, GROUPS, 2])
                        chain.link(tt(ghot, io, ix, ALU.is_equal))
                        chain.link(V.tensor_reduce(gmask, ghot.rearrange("p t g k -> p (t g) k"), AX.X, ALU.add))
                        gm = gmask.unsqueeze(2).broadcast_to([P, BATCH * GROUPS, 4])
                        chain.link(tt(kept.rearrange("p (g x) -> p g x", x=4), four, gm, ALU.mult))
                        carry()
                        for u in range(BATCH):
                            last = V.max(kval[:, u, :], kept[:, EXPERTS * u:EXPERTS * (u + 1)])
                        chain.link(last)
                        carry()
                        for u in range(BATCH):
                            last = V.max_index(kidx[:, u, :], kval[:, u, :], kept[:, EXPERTS * u:EXPERTS * (u + 1)])
                        chain.link(last)
                        io = iota[:, :].unsqueeze(1).unsqueeze(3).broadcast_to([P, BATCH, EXPERTS, TOPK])
                        ix = kidx[:, :, 0:TOPK].unsqueeze(2).broadcast_to([P, BATCH, EXPERTS, TOPK])
                        chain.link(tt(khot, io, ix, ALU.is_equal))
                        chain.link(V.tensor_reduce(chosen, khot.rearrange("p t e k -> p (t e) k"), AX.X, ALU.add))
                        chain.link(tt(weight, scores, chosen, ALU.mult))
                        chain.link(V.tensor_reduce(den, by_tile(weight), AX.X, ALU.add))
                        chain.link(V.tensor_scalar(den, den, 1e-20, None, ALU.add))
                        chain.link(V.reciprocal(den, den))
                        chain.link(V.tensor_scalar(den, den, 2.5, None, ALU.mult))
                        chain.link(tt(by_tile(weight), by_tile(weight), den.unsqueeze(2).broadcast_to([P, BATCH, EXPERTS]), ALU.mult))
                        chain.link(V.tensor_copy(w_part[:, :, 0, :], by_tile(weight)))
                        chain.link(tt(by_tile(rest), by_tile(weight), w_part[:, :, 0, :], ALU.subtract))
                        chain.link(V.tensor_copy(w_part[:, :, 1, :], by_tile(rest)))
                        tt(w_part[:, :, 2, :], by_tile(rest), w_part[:, :, 1, :], ALU.subtract).then_inc(s_w, 1)
                        links[0] = links[0] or chain.n
                    low_weights(dve, nc.vector, 0)
                    for_each(dve, batches, body)
                    low_weights(dve, nc.vector, 2)


        def expert_phase():
            s_g, s_u, s_wb = sem("m_g"), sem("m_u"), sem("m_wb")
            s_silu, s_prod, s_in, s_hi, s_lo, s_dn, s_y = (sem("m_" + x) for x in ("silu", "prod", "in", "hi", "lo", "dn", "y"))
            s_st, s_mv, s_var, s_rstd, s_shift = (sem("m_" + x) for x in ("stats", "mv", "var", "rstd", "shift"))
            order = [EXPERTS] + list(range(EXPERTS))
            at = [0]

            def cut(slots):
                at[0] += slots * CHUNK
                return work[:, at[0] - slots * CHUNK:at[0]].rearrange("p (s c) -> p s c", s=slots)
            silu = [x[:, :, :].rearrange("p u c -> p (u c)")[:, 0:CHUNK] for x in (xn, xT)]
            prod, inter = cut(1), cut(1)
            inter_r = rounded("inter_r", "work", at[0], 6 * CHUNK).rearrange("p (a s c) -> p a s c", a=2, s=3)
            inter_hi, inter_lo = inter_r[:, 0], inter_r[:, 1]
            cut(6)
            assert at[0] <= 12 * D

            def part_slot(s):
                return 2 if s == 0 else s % 2

            with nc.Block() as block:
                @block.gpsimd
                def _(pool):
                    def powers(c):
                        raise_power(pool, 3 * c, 3, s_var, c + 1, s_rstd)
                    for_each(pool, CHUNKS, powers)

                @block.tensor
                def _(pe):
                    def body(c):
                        xc_hi, xc_lo = ([x[:, k, bass.ds(CHUNK * c, CHUNK)] for k in range(KT)] for x in (x_hi, x_lo))

                        def weight_rows(s):
                            if not (is_first(c) and s == 1):
                                pe.wait_ge(s_in, BRANCHES * c + s - (s == 1))
                            nc.tensor.matmul(bank[4][:, 0:CHUNK], select[:, order[s], :], w_rows[:, bass.ds(CHUNK * c, CHUNK)],
                                             start=True, stop=True).then_inc(s_wb, 1)

                        def up(s, half, used, done):
                            e, n = order[s], BRANCHES * c + s
                            if s == 0 and not is_first(c):
                                pe.wait_ge(used, n)
                            elif not (is_first(c) and s < 2):
                                pe.wait_ge(used, n - 1)
                            ps = bank[2 * half + s % 2][:, 0:CHUNK]
                            cols = slice(INTER * half, INTER * (half + 1))
                            parts = [(k, w[:, k, e, cols], x[k]) for k in range(KT)
                                     for w, x in ((gu_hi, xc_hi), (gu_lo, xc_hi), (gu_hi, xc_lo))]
                            for i, (k, w, x) in enumerate(parts):
                                mm = nc.tensor.matmul(ps, w, x, start=(i == 0), stop=(i == len(parts) - 1))
                            mm.then_inc(done, 1)

                        for s in range(BRANCHES):
                            up(s, 0, s_silu, s_g)
                            if s >= 1:
                                weight_rows(s)
                            up(s, 1, s_prod, s_u)
                            if s >= 1:
                                down(c, s - 1)
                            elif not is_first(c):
                                down(c - 1, BRANCHES - 1)

                    def down(c, s):
                        e, n = order[s], BRANCHES * c + s
                        pe.wait_ge(s_lo, n + 1)
                        for j in range(3):
                            if s == 0 and not is_first(c):
                                pe.wait_ge(s_y, 3 * c - 2 + j)
                            hi, lo = (x[:, part_slot(s), P * j:P * (j + 1)] for x in (inter_hi, inter_lo))
                            parts = [(hi, down_hi[:, e, :]), (lo, down_hi[:, e, :]), (hi, down_lo[:, e, :])]
                            for i, (x, w) in enumerate(parts):
                                mm = nc.tensor.matmul(bank[5 + j][:, 0:D], x, w, start=(s == 0 and i == 0),
                                                      stop=(s == BRANCHES - 1 and i == 2))
                        mm.then_inc(s_dn, 1)

                    for_each(pe, CHUNKS, body)
                    down(CHUNKS - 1, BRANCHES - 1)

                @block.scalar
                def _(act):
                    def body(c):
                        for s in range(BRANCHES):
                            n = BRANCHES * c + s
                            if not (is_first(c) and s == 0):
                                high(n - 1, (s - 1) % BRANCHES, is_first(c) and s <= 3)
                            act.wait_ge(s_g, n + 1)
                            if s == 0 and not is_first(c):
                                act.wait_ge(s_prod, n)
                            elif not (is_first(c) and s < 2):
                                act.wait_ge(s_prod, n - 1)
                            nc.scalar.activation(silu[s % 2], bank[s % 2][:, 0:CHUNK], ACT.Silu).then_inc(s_silu, 1)

                    def high(n, s, first):
                        act.wait_ge(s_in, n + 1)
                        if not first:
                            act.wait_ge(s_dn, n - 1)
                        nc.scalar.activation(inter_hi[:, part_slot(s), :], inter[:, 0, :], ACT.Copy).then_inc(s_hi, 1)
                    for_each(act, CHUNKS, body)
                    high(BRANCHES * CHUNKS - 1, BRANCHES - 1, False)

                @block.vector
                def _(dve):
                    def body(c):
                        for s in range(BRANCHES):
                            n = BRANCHES * c + s
                            dve.wait_ge(s_silu, n + 1)
                            dve.wait_ge(s_u, n + 1)
                            if s == 0:
                                nc.vector.tensor_tensor(inter[:, 0, :], silu[0], bank[2][:, 0:CHUNK], ALU.mult).then_inc(s_prod, 1)
                                dve.wait_ge(s_prod, n + 1)
                                carry().then_inc(s_in, 1)
                            else:
                                nc.vector.tensor_tensor(prod[:, 0, :], silu[s % 2], bank[2 + s % 2][:, 0:CHUNK], ALU.mult).then_inc(s_prod, 1)
                                dve.wait_ge(s_prod, n + 1)
                                dve.wait_ge(s_wb, EXPERTS * c + s)
                                nc.vector.tensor_tensor(inter[:, 0, :], prod[:, 0, :], bank[4][:, 0:CHUNK], ALU.mult).then_inc(s_in, 1)
                            dve.wait_ge(s_hi, n + 1)
                            nc.vector.tensor_tensor(inter_lo[:, part_slot(s), :], inter[:, 0, :], inter_hi[:, part_slot(s), :].bitcast(F32),
                                                    ALU.subtract).then_inc(s_lo, 1)
                            dve.wait_ge(s_lo, n + 1)
                            if s < FINISH and not is_first(c):
                                finish(c - 1, s)

                    FINISH = 6

                    def finish(c, stage):
                        if stage == 0:
                            dve.wait_ge(s_dn, BRANCHES * c + BRANCHES)
                            for j in range(3):
                                t = 3 * c + j
                                nc.vector.tensor_tensor(col(t)(h), bank[5 + j][:, 0:D], col(t)(h), ALU.add).then_inc(s_y, 1)
                        if stage == 1:
                            for j in range(3):
                                t = 3 * c + j
                                dve.wait_ge(s_y, t + 1)
                                carry(j)
                                nc.vector.bn_stats(stats[:, j, :], col(t)(h)).then_inc(s_st, 1)
                        if stage == 2:
                            if not (isinstance(c, int) and c == 0):
                                dve.wait_ge(s_shift, c)
                            means(dve, 0, 3, s_st, 3 * c + 3, s_mv)
                        if stage == 3:
                            variances(dve, 3 * c, 0, 3, s_mv, c + 1, s_var)
                        if stage == 5:
                            shifts(dve, 3 * c, 0, 3, s_rstd, c + 1, s_shift)
                    body(0)
                    body(1)
                    with dve.Fori(2, CHUNKS) as c:
                        body(c)
                    for stage in range(FINISH):
                        finish(CHUNKS - 1, stage)
                    dve.wait_ge(s_shift, CHUNKS)

        def ffn_phase():
            names = ("xn", "r1", "q1", "t1", "q1T", "g0", "u0", "sl0", "p0", "g1", "u1", "sl1", "p1", "sc2", "step2", "inv", "r2", "q2", "t2",
                     "q2T", "dn", "dns", "out")
            s = {x: sem("f_" + x) for x in names}
            s_chain, s_sc, s_round = (sem("f_" + x) for x in ("chain", "sc", "round"))
            s_st = [sem(f"f_st{u}") for u in range(PAIR)]
            BATCH = TILES // 3
            at = [0]

            def cut(n):
                at[0] += n
                return region[:, at[0] - n:at[0]]
            x_all = cut(TILES * D).rearrange("p (t c) -> p t c", c=D)
            q1 = cut(TILES * D // 2).bitcast(BF16).rearrange("p (t c) -> p t c", c=D)
            q1T = cut(TILES * D // 2).bitcast(BF16).rearrange("p (t c) -> p t c", c=D)
            q2T = cut(PAIR * INNER // 2).bitcast(BF16).rearrange("p (u k r) -> p u k r", u=PAIR, r=P)
            res = cut(PAIR * D).rearrange("p (u c) -> p u c", u=PAIR)
            amax, step1, inv1 = cut(TILES), cut(TILES), cut(TILES)
            sc1 = cut(TILES * 3).rearrange("p (t g) -> p t g", g=3)
            amax2, inv2, sc2 = cut(TILES), cut(TILES), cut(TILES)
            scaled = cut(PAIR * D).rearrange("p (u c) -> p u c", u=PAIR)
            round_c = cut(1)
            down_step = cut(1)
            silu = cut(INNER).rearrange("p (b c) -> p b c", b=2)
            q2 = cut(INNER).bitcast(BF16).rearrange("p (u c) -> p u c", u=PAIR)
            prod_limit = cut(2 * (INNER + 2)).rearrange("p (u c) -> p u c", u=PAIR)
            prod, limit = prod_limit[:, :, 0:INNER], prod_limit[:, :, INNER:]
            batches = TILES // BATCH
            LAG = 3
            PEELED = 3

            with nc.Block() as block:
                @block.gpsimd
                def _(pool):
                    pool.memset(round_c, ROUND).then_inc(s_round, 1)
                    pool.memset(limit, 1e-5).then_inc(s_round, 1)

                    def step(tau, u):
                        t = tau - 3
                        if exists(t):
                            pool.wait_ge(s["dns"], t + 1)
                            if reuses(t):
                                pool.wait_ge(s_st[1 - u], (16 // PAIR) * (t - (1 - u)))
                            nc.gpsimd.tensor_tensor(res[:, 1 - u, :], scaled[:, 1 - u, :], col(t)(h), ALU.add).then_inc(s["out"], 1)
                    steps(pool, step, PEELED, LAG)

                @block.sync
                def _(sp):
                    def body(i):
                        for u in range(PAIR):
                            t = PAIR * i + u
                            sp.wait_ge(s["out"], t + 1)
                            sp.dma_start(out[bass.ds(P * t, P), :], res[:, u, :]).then_inc(s_st[u], 16)
                    body(0)
                    with sp.Fori(1, PASSES - 1) as i:
                        body(i)
                    for t in range(TILES - PAIR, TILES):
                        rows = min(P, ROWS - P * t)
                        sp.wait_ge(s["out"], t + 1)
                        sp.dma_start(out[P * t:P * t + rows, :], res[0:rows, t % PAIR, :]).then_inc(s_st[t % PAIR], 16)
                    for u in range(PAIR):
                        sp.wait_ge(s_st[u], 16 * PASSES)

                @block.scalar
                def _(act):
                    act.wait_ge(s_round, 2)

                    def turned(c):
                        for j in range(BATCH):
                            t = BATCH * c + j
                            act.wait_ge(s["t1"], t + 1)
                            nc.scalar.activation(col(t)(q1T), bank[4 + j % 2][:, :].bitcast(BF16)[:, 0:D], ACT.Copy).then_inc(s["q1T"], 1)

                    def batch(c):
                        act.wait_ge(s_sc, c + 1)
                        for j in range(BATCH):
                            t = BATCH * c + j
                            nc.scalar.activation(col(t)(x_all), col(t)(x_all), ACT.Identity, bias=round_c,
                                                 scale=inv1[:, bass.ds(t, 1)]).then_inc(s["r1"], 1)
                        if not is_first(c):
                            turned(c - 1)
                    for_each(act, batches, batch)
                    turned(batches - 1)

                    def step(tau, u):
                        if exists(tau):
                            for b in range(2):
                                act.wait_ge(s[f"g{b}"], tau + 1)
                                if reuses(tau, 1):
                                    act.wait_ge(s[f"p{b}"], tau)
                                nc.scalar.activation(silu[:, b, :], bank[2 * b][:, :], ACT.Silu,
                                                     scale=sc1[:, bass.ds(tau, 1), 2 * b]).then_inc(s[f"sl{b}"], 1)
                        t = tau - 1
                        if exists(t):
                            act.wait_ge(s["sc2"], t + 1)
                            x = prod[:, 1 - u, :]
                            nc.scalar.activation(x, x, ACT.Identity, bias=round_c, scale=inv2[:, bass.ds(t, 1)]).then_inc(s["r2"], 1)
                        t = tau - 2
                        if exists(t):
                            act.wait_ge(s["t2"], t + 1)
                            if reuses(t):
                                act.wait_ge(s["dn"], t - 1)
                            src = bank[5][:, :].bitcast(BF16).rearrange("p (k r) -> p k r", r=P)
                            nc.scalar.activation(q2T[:, u], src, ACT.Copy).then_inc(s["q2T"], 1)
                        t = tau - 3
                        if exists(t):
                            act.wait_ge(s["step2"], t + 1)
                            if reuses(t):
                                act.wait_ge(s["out"], t - 1)
                            act.wait_ge(s["dn"], t + 1)
                            nc.scalar.activation(scaled[:, 1 - u, :], bank[7 - u][:, 0:D], ACT.Copy,
                                                 scale=sc2[:, bass.ds(t, 1)]).then_inc(s["dns"], 1)
                    steps(act, step, PEELED, LAG)

                @block.tensor
                def _(pe):
                    def turn(c):
                        for j in range(BATCH):
                            t = BATCH * c + j
                            pe.wait_ge(s["q1"], t + 1)
                            if not (is_first(c) and j < 2):
                                pe.wait_ge(s["q1T"], t - 1)
                            for k in range(KT):
                                mm = nc.tensor.transpose(bank[4 + j % 2][:, :].bitcast(BF16)[:, P * k:P * (k + 1)],
                                                         q1[:, bass.ds(t, 1), P * k:P * (k + 1)].rearrange("p a c -> p (a c)"), ident_bf[:, :])
                            mm.then_inc(s["t1"], 1)
                    for_each(pe, batches, turn)

                    def step(tau, u):
                        if exists(tau):
                            pe.wait_ge(s["q1T"], tau + 1)
                            for b in range(2):
                                for half in range(2):
                                    if reuses(tau, 1):
                                        pe.wait_ge(s[f"sl{b}" if half == 0 else f"p{b}"], tau)
                                    w0 = INNER * half + BANK * b
                                    for k in range(KT):
                                        mm = nc.tensor.matmul(bank[2 * b + half][:, :],
                                                              q1T[:, bass.ds(tau, 1), P * k:P * (k + 1)].rearrange("p a c -> p (a c)"),
                                                              ffn_up_q[:, k, w0:w0 + BANK], start=(k == 0), stop=(k == KT - 1))
                                    mm.then_inc(s[f"{'gu'[half]}{b}"], 1)
                        t = tau - 2
                        if exists(t):
                            pe.wait_ge(s["q2"], t + 1)
                            if reuses(t, 1):
                                pe.wait_ge(s["q2T"], t)
                            for k in range(IB):
                                mm = nc.tensor.transpose(bank[5][:, :].bitcast(BF16)[:, P * k:P * (k + 1)], q2[:, u, P * k:P * (k + 1)], ident_bf[:, :])
                            mm.then_inc(s["t2"], 1)
                        t = tau - 3
                        if exists(t):
                            pe.wait_ge(s["q2T"], t + 1)
                            if reuses(t):
                                pe.wait_ge(s["dns"], t - 1)
                            for k in range(IB):
                                mm = nc.tensor.matmul(bank[7 - u][:, 0:D], q2T[:, 1 - u, k, :], ffn_down_q[:, k, :],
                                                      start=(k == 0), stop=(k == IB - 1))
                            mm.then_inc(s["dn"], 1)
                    steps(pe, step, PEELED, LAG)

                @block.vector
                def _(dve):
                    chain = Chain(dve, s_chain)
                    V = nc.vector
                    dve.wait_ge(s_round, 2)
                    chain.link(V.tensor_scalar(down_step, w_scale[:, 2:3], 1.0 / 127.0, None, ALU.mult))
                    base = chain.n
                    links = [0]

                    def scales(c):
                        chain.n, chain.base = 0, base + c * links[0]
                        for j in range(BATCH):
                            t = BATCH * c + j
                            V.tensor_scalar(col(t)(x_all), col(t)(h), rstd[:, bass.ds(t, 1)], shift[:, bass.ds(t, 1)],
                                            ALU.mult, ALU.add).then_inc(s["xn"], 1)
                        dve.wait_ge(s["xn"], BATCH * c + BATCH)
                        a, d, inv = (x[:, bass.ds(BATCH * c, BATCH)] for x in (amax, step1, inv1))
                        chain.link(V.tensor_reduce(a, x_all[:, bass.ds(BATCH * c, BATCH), :], AX.X, ALU.max, apply_absolute_value=True))
                        chain.link(V.tensor_scalar(d, a, 1e-5, 1.0 / 127.0, ALU.max, ALU.mult))
                        V.tensor_scalar(sc1[:, bass.ds(BATCH * c, BATCH), 0], d, w_scale[:, 0:1], None, ALU.mult)
                        V.tensor_scalar(sc1[:, bass.ds(BATCH * c, BATCH), 1], d, w_scale[:, 1:2], None, ALU.mult)
                        V.tensor_scalar(sc1[:, bass.ds(BATCH * c, BATCH), 2], d, w_scale[:, 0:1], None, ALU.mult)
                        chain.link(V.tensor_scalar(a, a, 1e-5, None, ALU.max))
                        chain.link(V.reciprocal(inv, a))
                        V.tensor_scalar(inv, inv, 127.0, None, ALU.mult).then_inc(s_sc, 1)
                        links[0] = links[0] or chain.n

                    def quantised(c):
                        for j in range(BATCH):
                            t = BATCH * c + j
                            dve.wait_ge(s["r1"], t + 1)
                            V.tensor_scalar(col(t)(q1), col(t)(x_all), ROUND, 127.0, ALU.subtract, ALU.min).then_inc(s["q1"], 1)

                    scales(0)

                    def batch(c, last=False):
                        if not last:
                            scales(c + 1)
                        quantised(c)
                    batch(0)
                    with dve.Fori(1, batches - 1) as c:
                        batch(c)
                    batch(batches - 1, last=True)
                    before = base + batches * links[0]
                    PER_TILE = 1

                    def step(tau, u):
                        chain.n, chain.base = 0, before + PER_TILE * tau
                        if exists(tau):
                            for b in range(2):
                                dve.wait_ge(s[f"sl{b}"], tau + 1)
                                dve.wait_ge(s[f"u{b}"], tau + 1)
                                V.scalar_tensor_tensor(prod[:, u, BANK * b:BANK * (b + 1)], bank[2 * b + 1][:, :], sc1[:, bass.ds(tau, 1), 1],
                                                       silu[:, b, :], ALU.mult, ALU.mult).then_inc(s[f"p{b}"], 1)
                        t = tau - 1
                        if exists(t):
                            dve.wait_ge(s["r2"], t + 1)
                            if reuses(t):
                                dve.wait_ge(s["t2"], t - 1)
                            V.tensor_scalar(q2[:, 1 - u, :], prod[:, 1 - u, :], ROUND, 127.0, ALU.subtract, ALU.min).then_inc(s["q2"], 1)
                        if exists(tau):
                            dve.wait_ge(s["p1"], tau + 1)
                            a, inv, sc = (x[:, bass.ds(tau, 1)] for x in (amax2, inv2, sc2))
                            chain.link(V.tensor_reduce(a, prod_limit[:, u, :], AX.X, ALU.max, apply_absolute_value=True))
                            V.reciprocal(inv, a).then_inc(s["inv"], 1)
                            V.tensor_scalar(sc, a, down_step, None, ALU.mult).then_inc(s["step2"], 1)
                            dve.wait_ge(s["inv"], tau + 1)
                            V.tensor_scalar(inv, inv, 127.0, None, ALU.mult).then_inc(s["sc2"], 1)
                    steps(dve, step, PEELED, LAG)

        phases = [embed_phase, lambda: project_phase(0), lambda: attention_phase(0), lambda: output_phase(0),
                  route_phase, expert_phase, lambda: project_phase(1), lambda: attention_phase(1),
                  lambda: output_phase(1), ffn_phase]
        for phase in phases:
            with nc.cleanup_on_exit():
                phase()


def _tables():
    angle_of = 1.0 / 10000.0 ** (np.arange(0, DH, 2, dtype=np.float32) / np.float32(DH))
    pos = np.arange(PADDED) % SEQ
    freqs = pos.astype(np.float32)[:, None] * angle_of.astype(np.float32)[None, :]
    ang = np.concatenate((freqs, freqs), axis=-1)[:, ::2]
    c, s = np.cos(ang), np.sin(ang)
    cos = np.repeat(c, 2, axis=1)
    sin = np.stack((-s, s), axis=-1).reshape(PADDED, DH)
    quarter = np.float32(1.0 / DH ** 0.5)
    cos = np.concatenate((cos * quarter, cos), axis=1).astype(np.float32)
    sin = np.concatenate((sin * quarter, sin), axis=1).astype(np.float32)
    mask = (np.arange(P)[:, None] // DH == np.arange(HH)[None, :]).astype(np.float32)
    rem = (np.arange(HR)[:, None] // REM == np.arange(HH)[None, :]).astype(np.float32)
    iota = np.tile(np.arange(EXPERTS, dtype=np.float32), (P, 1))
    return {"rope_cos": cos, "rope_sin": sin, "head_mask": mask, "rem_mask": rem, "ident_in": np.eye(P, dtype=np.float32), "iota_in": iota}


def _layout(i):
    i = {k: np.asarray(v) for k, v in i.items()}
    x = i["x"].reshape(IMAGES, 3, 8, 16, 8, 16)
    gu = np.concatenate([
        np.concatenate((i["L0_ffn_gate_proj"], i["L0_ffn_shared_gate_w"][None]), axis=0),
        np.concatenate((i["L0_ffn_up_proj"], i["L0_ffn_shared_up_w"][None]), axis=0)], axis=1)
    down = np.concatenate((i["L0_ffn_down_proj"], i["L0_ffn_shared_down_w"][None]), axis=0)
    arrays = {
        "patches_t": x.transpose(3, 5, 1, 0, 2, 4).reshape(768, IMAGES * PATCHES),
        "txt": i["txt"],
        "w_emb_t": i["L0_tok_W"].T,
        "b_emb": i["L0_tok_b"],
        "w_qkv": np.concatenate((i["L0_attn_Wq"], i["L0_attn_Wk"], i["L0_attn_Wv"]), axis=1),
        "b_qkv": np.concatenate((i["L0_attn_bq"], i["L0_attn_bk"], i["L0_attn_bv"])),
        "w_o0": i["L0_attn_Wo"],
        "b_o0": i["L0_attn_bo"],
        "w_gate_t": i["L0_ffn_gate_w"].T,
        "e_bias": i["L0_ffn_e_bias"],
        "w_gu_t": gu.transpose(2, 0, 1),
        "w_down_t": down.transpose(2, 0, 1),
        "w_v1_t": i["L1_attn_Wv"].T,
        "b_v1": i["L1_attn_bv"],
        "w_o1_t": i["L1_attn_Wo"].T,
        "b_o1": i["L1_attn_bo"],
        "ffn_up_t": np.concatenate((i["L1_ffn_w_gate"], i["L1_ffn_w_up"]), axis=0).T,
        "ffn_down_t": i["L1_ffn_w_down"].T,
    }
    arrays.update(_tables())
    return {k: np.ascontiguousarray(v) for k, v in arrays.items()}


def build(nc, arrays):
    args = [nc.dram_tensor(f"in_{k}_dram", v.shape, mybir.dt.from_np(v.dtype), kind="ExternalInput").ap() for k, v in arrays.items()]
    out = nc.dram_tensor("out_0_dram", (ROWS, D), F32, kind="ExternalOutput").ap()
    fusion_kernel(nc, *args, out)


def kernel(**inputs):
    import concourse.bacc as _bacc
    from concourse.bass_utils import run_bass_kernel_spmd as _run

    nc = _bacc.Bacc("TRN2", target_bir_lowering=False, num_devices=1)
    arrays = _layout(inputs)
    build(nc, arrays)
    r = _run(nc, [{f"in_{k}_dram": v for k, v in arrays.items()}], core_ids=[0])
    return r.results[0]["out_0_dram"].reshape(IMAGES, SEQ, D)
```
